# Optimizing a Trainium2 kernel written in Bass

```python
import numpy as np
import jax
import jax.numpy as jnp

def _softmax(x, axis=-1):
    return jax.nn.softmax(x, axis=axis)

def _gelu(x):
    return jax.nn.gelu(x, approximate=True)

def _silu(x):
    return jax.nn.silu(x)

def _sigmoid(x):
    return jax.nn.sigmoid(x)

def _layernorm(x, axis=-1, eps=1e-05):
    m = jnp.mean(x, axis=axis, keepdims=True)
    v = jnp.var(x, axis=axis, keepdims=True)
    return (x - m) / jnp.sqrt(v + eps)

def _scatter_add(tgt, idx, src, axis=0):
    return tgt.at[idx].add(src)

def _segment_sum(src, seg, n):
    return jax.ops.segment_sum(src, seg, n)
kernel_name = 'mk_gnn_preln_d4_gnn_r32_c6fd5d'

def setup_inputs(seed: int=0):
    np.random.seed(seed)
    _w = jnp.asarray

    def _rec_inputs():
        import jax
        import jax.numpy as jnp
        _gk = jax.random.key(seed)
        x = -0.000202 + 1 * jax.random.normal(jax.random.fold_in(_gk, 1), (3125, 64), jnp.float32)
        _s = jax.random.randint(jax.random.fold_in(_gk, 2), (50000,), 0, 3125, jnp.int32)
        _d = jax.random.randint(jax.random.fold_in(_gk, 3), (50000,), 0, 3125, jnp.int32)
        _loop = jnp.arange(3125, dtype=jnp.int32)
        src = jnp.concatenate([_s, _d, _loop])
        dst = jnp.concatenate([_d, _s, _loop])
        _o = jnp.argsort(dst, stable=True)
        src = src[_o]
        dst = dst[_o]
        edge_attr_64 = -1.00939e-05 + 0.999822 * jax.random.normal(jax.random.fold_in(_gk, 12), (103125, 64), jnp.float32)
        edge_attr_64_n2 = -1.00939e-05 + 0.999822 * jax.random.normal(jax.random.fold_in(_gk, 13), (103125, 64), jnp.float32)
        edge_type_8 = jax.random.randint(jax.random.fold_in(_gk, 15), (103125,), 0, 8, jnp.int32)
        edge_weight = jax.random.uniform(jax.random.fold_in(_gk, 16), (103125,), jnp.float32, 0.0, 1)
        return (x, src, dst, edge_attr_64, edge_attr_64_n2, edge_type_8, edge_weight)
    x, src, dst, edge_attr_64, edge_attr_64_n2, edge_type_8, edge_weight = _rec_inputs()

    def _L0_gnn_setup():
        import jax, jax.numpy as jnp
        import numpy as np
        N_NODES = 3125
        N_EDGES = 50000
        DIM = 64
        N_LAYERS = 2
        key = jax.random.key(seed)
        ks = jax.random.split(key, 7)
        scale = 1.0 / np.sqrt(DIM)
        return {'inputs': jax.random.normal(ks[0], (N_NODES, DIM), dtype=jnp.float32), 'edge_weight': jax.random.uniform(ks[1], (N_EDGES,), dtype=jnp.float32), 'W_self': jax.random.normal(ks[2], (N_LAYERS, DIM, DIM), dtype=jnp.float32) * scale, 'W_neigh': jax.random.normal(ks[3], (N_LAYERS, DIM, DIM), dtype=jnp.float32) * scale, 'b_neigh': jnp.zeros((N_LAYERS, DIM), dtype=jnp.float32), 'src': jax.random.randint(ks[4], (N_EDGES,), 0, N_NODES, dtype=jnp.int32), 'dst': jax.random.randint(ks[5], (N_EDGES,), 0, N_NODES, dtype=jnp.int32)}
    _L0_gnn_all = _L0_gnn_setup()
    _L0_gnn_in = {k: v for k, v in _L0_gnn_all.items() if k in ('W_self', 'W_neigh', 'b_neigh')}
    del _L0_gnn_all

    def _L1_gnn_setup():
        import jax, jax.numpy as jnp
        import numpy as np
        N_NODES = 3125
        N_EDGES = 50000
        IN_F = 64
        HID_F = 64

        def _norms(src, dst, n_nodes, dtype):
            ones = jnp.ones(src.shape[0], dtype=dtype)
            deg_out = jax.ops.segment_sum(ones, src, num_segments=n_nodes)
            deg_in = jax.ops.segment_sum(ones, dst, num_segments=n_nodes)
            norm_out = jnp.where(deg_out > 0, jax.lax.rsqrt(jnp.maximum(deg_out, 1.0)), 0.0)[:, None]
            norm_in = jnp.where(deg_in > 0, jax.lax.rsqrt(jnp.maximum(deg_in, 1.0)), 0.0)[:, None]
            return (norm_out, norm_in)

        def _stag_conv(h, a, W, b, src, dst, norm_out, norm_in, n_nodes):
            h = h * norm_out
            m = h[src] * a
            agg = jax.ops.segment_sum(m, dst, num_segments=n_nodes)
            return agg * norm_in @ W + b
        key = jax.random.key(seed)
        ks = jax.random.split(key, 16)
        x = jax.random.normal(ks[0], (N_NODES, IN_F), dtype=jnp.float32)
        src = jax.random.randint(ks[1], (N_EDGES,), 0, N_NODES, dtype=jnp.int32)
        dst = jax.random.randint(ks[2], (N_EDGES,), 0, N_NODES, dtype=jnp.int32)
        a_mu0 = 1.0 + jax.random.normal(ks[3], (IN_F,), dtype=jnp.float32)
        a_ls0 = jnp.ones((IN_F,), dtype=jnp.float32)
        a_mu1 = 1.0 + jax.random.normal(ks[4], (HID_F,), dtype=jnp.float32)
        a_ls1 = jnp.ones((HID_F,), dtype=jnp.float32)
        W0 = jax.random.normal(ks[5], (IN_F, HID_F), dtype=jnp.float32) / np.sqrt(IN_F)
        b0 = jnp.zeros((HID_F,), dtype=jnp.float32)
        W1 = jax.random.normal(ks[6], (HID_F, HID_F), dtype=jnp.float32) / np.sqrt(HID_F)
        b1 = jnp.zeros((HID_F,), dtype=jnp.float32)
        eps0 = jax.random.normal(ks[7], (N_EDGES, IN_F), dtype=jnp.float32)
        eps1 = jax.random.normal(ks[8], (N_EDGES, HID_F), dtype=jnp.float32)
        return {'x': x, 'src': src, 'dst': dst, 'a_mu0': a_mu0, 'a_ls0': a_ls0, 'a_mu1': a_mu1, 'a_ls1': a_ls1, 'W0': W0, 'b0': b0, 'W1': W1, 'b1': b1, 'eps0': eps0, 'eps1': eps1}
    _L1_gnn_all = _L1_gnn_setup()
    _L1_gnn_in = {k: v for k, v in _L1_gnn_all.items() if k in ('a_mu0', 'a_ls0', 'a_mu1', 'a_ls1', 'W0', 'b0', 'W1', 'b1')}
    del _L1_gnn_all

    def _L2_gnn_setup():
        import jax, jax.numpy as jnp
        import numpy as np
        H = 5
        NEG_SLOPE = 0.2
        N_NODES = 50000
        N_EDGES = 12500
        IN_CH = 64
        OUT_CH = 64

        def gatv2_layer(x, src, dst, Wl, bl, Wr, br, att, bias, n_nodes):
            C = att.shape[1]
            xl = (x @ Wl + bl).reshape(n_nodes, H, C)
            xr = (x @ Wr + br).reshape(n_nodes, H, C)
            e = jax.nn.leaky_relu(xl[src] + xr[dst], NEG_SLOPE)
            alpha = jnp.einsum('ehc,hc->eh', e, att)
            m = jax.ops.segment_max(alpha, dst, num_segments=n_nodes)
            m = jnp.where(jnp.isfinite(m), m, 0.0)
            a = jnp.exp(alpha - m[dst])
            denom = jax.ops.segment_sum(a, dst, num_segments=n_nodes)
            a = a / (denom[dst] + 1e-16)
            out = jax.ops.segment_sum(a[:, :, None] * xl[src], dst, num_segments=n_nodes)
            return out.mean(axis=1) + bias
        key = jax.random.key(seed)
        ks = jax.random.split(key, 17)
        s = 0.05
        inp = {'x': jax.random.normal(ks[0], (N_NODES, IN_CH), jnp.float32), 'edge_index': jax.random.randint(ks[1], (2, N_EDGES), 0, N_NODES, jnp.int64), 'W1l': jax.random.normal(ks[2], (IN_CH, H * IN_CH), jnp.float32) * s, 'b1l': jnp.zeros((H * IN_CH,), jnp.float32), 'W1r': jax.random.normal(ks[3], (IN_CH, H * IN_CH), jnp.float32) * s, 'b1r': jnp.zeros((H * IN_CH,), jnp.float32), 'att1': jax.random.normal(ks[4], (H, IN_CH), jnp.float32) * s, 'bias1': jnp.zeros((IN_CH,), jnp.float32), 'W2l': jax.random.normal(ks[5], (IN_CH, H * OUT_CH), jnp.float32) * s, 'b2l': jnp.zeros((H * OUT_CH,), jnp.float32), 'W2r': jax.random.normal(ks[6], (IN_CH, H * OUT_CH), jnp.float32) * s, 'b2r': jnp.zeros((H * OUT_CH,), jnp.float32), 'att2': jax.random.normal(ks[7], (H, OUT_CH), jnp.float32) * s, 'bias2': jnp.zeros((OUT_CH,), jnp.float32), 'Wfc': jax.random.normal(ks[8], (OUT_CH, OUT_CH), jnp.float32) * s, 'bfc': jnp.zeros((OUT_CH,), jnp.float32)}
        return inp
    _L2_gnn_all = _L2_gnn_setup()
    _L2_gnn_in = {k: v for k, v in _L2_gnn_all.items() if k in ('W1l', 'b1l', 'W1r', 'b1r', 'att1', 'bias1', 'W2l', 'b2l', 'W2r', 'b2r', 'att2', 'bias2', 'Wfc', 'bfc')}
    del _L2_gnn_all

    def _L3_gnn_setup():
        import jax, jax.numpy as jnp
        import numpy as np
        N, E, R, H = (50000, 25000, 8, 4)
        F_IN, HID, OUT = (64, 64, 64)
        NEG_SLOPE = 0.2

        def _glorot(key, shape):
            fan_in, fan_out = (shape[-2], shape[-1])
            std = np.sqrt(2.0 / (fan_in + fan_out)).astype(np.float32)
            return jax.random.normal(key, shape, dtype=jnp.float32) * std

        def _rgat_conv(x, src, dst, etype, W, Q, K, b):
            n = x.shape[0]
            hc = W.shape[-1]
            xw = jnp.einsum('ni,rio->rno', x, W)
            qn = jnp.einsum('rno,roh->rnh', xw, Q)
            kn = jnp.einsum('rno,roh->rnh', xw, K)
            alpha = jax.nn.leaky_relu(qn[etype, dst] + kn[etype, src], NEG_SLOPE)
            amax = jax.ops.segment_max(alpha, dst, num_segments=n)
            amax = jnp.where(jnp.isfinite(amax), amax, 0.0)
            ex = jnp.exp(alpha - amax[dst])
            denom = jax.ops.segment_sum(ex, dst, num_segments=n)
            attn = ex / (denom[dst] + 1e-16)
            out_j = xw[etype, src].reshape(-1, H, hc // H)
            agg = jax.ops.segment_sum(attn[:, :, None] * out_j, dst, num_segments=n)
            return agg.reshape(n, hc) + b
        key = jax.random.key(seed)
        ks = jax.random.split(key, 12)
        x = jax.random.normal(ks[0], (N, F_IN), dtype=jnp.float32)
        adj_t = jax.random.randint(ks[1], (2, E), 0, N, dtype=jnp.int32)
        edge_types = jax.random.randint(ks[2], (E,), 0, R, dtype=jnp.int32)
        W1 = _glorot(ks[3], (R, F_IN, HID))
        Q1 = _glorot(ks[4], (R, HID, H))
        K1 = _glorot(ks[5], (R, HID, H))
        b1 = jnp.zeros((HID,), jnp.float32)
        W2 = _glorot(ks[6], (R, HID, OUT))
        Q2 = _glorot(ks[7], (R, OUT, H))
        K2 = _glorot(ks[8], (R, OUT, H))
        b2 = jnp.zeros((OUT,), jnp.float32)
        return dict(x=x, adj_t=adj_t, edge_types=edge_types, W1=W1, Q1=Q1, K1=K1, b1=b1, W2=W2, Q2=Q2, K2=K2, b2=b2)
    _L3_gnn_all = _L3_gnn_setup()
    _L3_gnn_in = {k: v for k, v in _L3_gnn_all.items() if k in ('W1', 'Q1', 'K1', 'b1', 'W2', 'Q2', 'K2', 'b2')}
    del _L3_gnn_all
    return {'x': x, 'src': src, 'dst': dst, 'edge_attr_64': edge_attr_64, 'edge_attr_64_n2': edge_attr_64_n2, 'edge_type_8': edge_type_8, 'edge_weight': edge_weight, 'L0_gnn_W_self': _L0_gnn_in['W_self'], 'L0_gnn_W_neigh': _L0_gnn_in['W_neigh'], 'L0_gnn_b_neigh': _L0_gnn_in['b_neigh'], 'L1_gnn_a_mu0': _L1_gnn_in['a_mu0'], 'L1_gnn_a_ls0': _L1_gnn_in['a_ls0'], 'L1_gnn_a_mu1': _L1_gnn_in['a_mu1'], 'L1_gnn_a_ls1': _L1_gnn_in['a_ls1'], 'L1_gnn_W0': _L1_gnn_in['W0'], 'L1_gnn_b0': _L1_gnn_in['b0'], 'L1_gnn_W1': _L1_gnn_in['W1'], 'L1_gnn_b1': _L1_gnn_in['b1'], 'L2_gnn_W1l': _L2_gnn_in['W1l'], 'L2_gnn_b1l': _L2_gnn_in['b1l'], 'L2_gnn_W1r': _L2_gnn_in['W1r'], 'L2_gnn_b1r': _L2_gnn_in['b1r'], 'L2_gnn_att1': _L2_gnn_in['att1'], 'L2_gnn_bias1': _L2_gnn_in['bias1'], 'L2_gnn_W2l': _L2_gnn_in['W2l'], 'L2_gnn_b2l': _L2_gnn_in['b2l'], 'L2_gnn_W2r': _L2_gnn_in['W2r'], 'L2_gnn_b2r': _L2_gnn_in['b2r'], 'L2_gnn_att2': _L2_gnn_in['att2'], 'L2_gnn_bias2': _L2_gnn_in['bias2'], 'L2_gnn_Wfc': _L2_gnn_in['Wfc'], 'L2_gnn_bfc': _L2_gnn_in['bfc'], 'L3_gnn_W1': _L3_gnn_in['W1'], 'L3_gnn_Q1': _L3_gnn_in['Q1'], 'L3_gnn_K1': _L3_gnn_in['K1'], 'L3_gnn_b1': _L3_gnn_in['b1'], 'L3_gnn_W2': _L3_gnn_in['W2'], 'L3_gnn_Q2': _L3_gnn_in['Q2'], 'L3_gnn_K2': _L3_gnn_in['K2'], 'L3_gnn_b2': _L3_gnn_in['b2']}

def reference(x, src, dst, edge_attr_64, edge_attr_64_n2, edge_type_8, edge_weight, L0_gnn_W_self, L0_gnn_W_neigh, L0_gnn_b_neigh, L1_gnn_a_mu0, L1_gnn_a_ls0, L1_gnn_a_mu1, L1_gnn_a_ls1, L1_gnn_W0, L1_gnn_b0, L1_gnn_W1, L1_gnn_b1, L2_gnn_W1l, L2_gnn_b1l, L2_gnn_W1r, L2_gnn_b1r, L2_gnn_att1, L2_gnn_bias1, L2_gnn_W2l, L2_gnn_b2l, L2_gnn_W2r, L2_gnn_b2r, L2_gnn_att2, L2_gnn_bias2, L2_gnn_Wfc, L2_gnn_bfc, L3_gnn_W1, L3_gnn_Q1, L3_gnn_K1, L3_gnn_b1, L3_gnn_W2, L3_gnn_Q2, L3_gnn_K2, L3_gnn_b2):
    import jax
    import jax.numpy as jnp

    def _L0_gnn_ref(inputs, edge_weight, W_self, W_neigh, b_neigh, src, dst):
        import jax, jax.numpy as jnp
        import numpy as np
        N_NODES = 3125
        N_EDGES = 50000
        DIM = 64
        N_LAYERS = 2
        n = inputs.shape[0]
        deg = jax.ops.segment_sum(jnp.ones_like(edge_weight), dst, num_segments=n)
        inv_deg = jnp.where(deg > 0, 1.0 / jnp.maximum(deg, 1.0), 0.0)[:, None]
        h = inputs
        for l in range(W_self.shape[0]):
            msg = h[src] * edge_weight[:, None]
            h_neigh = jax.ops.segment_sum(msg, dst, num_segments=n) * inv_deg
            h = h @ W_self[l].T + h_neigh @ W_neigh[l].T + b_neigh[l]
            if l < W_self.shape[0] - 1:
                h = jax.nn.relu(h)
        return h

    def _L1_gnn_ref(x, src, dst, a_mu0, a_ls0, a_mu1, a_ls1, W0, b0, W1, b1, eps0, eps1):
        import jax, jax.numpy as jnp
        import numpy as np
        N_NODES = 3125
        N_EDGES = 50000
        IN_F = 64
        HID_F = 64

        def _norms(src, dst, n_nodes, dtype):
            ones = jnp.ones(src.shape[0], dtype=dtype)
            deg_out = jax.ops.segment_sum(ones, src, num_segments=n_nodes)
            deg_in = jax.ops.segment_sum(ones, dst, num_segments=n_nodes)
            norm_out = jnp.where(deg_out > 0, jax.lax.rsqrt(jnp.maximum(deg_out, 1.0)), 0.0)[:, None]
            norm_in = jnp.where(deg_in > 0, jax.lax.rsqrt(jnp.maximum(deg_in, 1.0)), 0.0)[:, None]
            return (norm_out, norm_in)

        def _stag_conv(h, a, W, b, src, dst, norm_out, norm_in, n_nodes):
            h = h * norm_out
            m = h[src] * a
            agg = jax.ops.segment_sum(m, dst, num_segments=n_nodes)
            return agg * norm_in @ W + b
        n_nodes = x.shape[0]
        norm_out, norm_in = _norms(src, dst, n_nodes, x.dtype)
        a0 = a_mu0 + jnp.exp(a_ls0) * eps0
        a1 = a_mu1 + jnp.exp(a_ls1) * eps1
        h = _stag_conv(x, a0, W0, b0, src, dst, norm_out, norm_in, n_nodes)
        h = jax.nn.relu(h)
        h = _stag_conv(h, a1, W1, b1, src, dst, norm_out, norm_in, n_nodes)
        return jax.nn.softmax(h, axis=-1)

    def _L2_gnn_ref(x, edge_index, W1l, b1l, W1r, b1r, att1, bias1, W2l, b2l, W2r, b2r, att2, bias2, Wfc, bfc):
        import jax, jax.numpy as jnp
        import numpy as np
        H = 5
        NEG_SLOPE = 0.2
        N_NODES = 50000
        N_EDGES = 12500
        IN_CH = 64
        OUT_CH = 64

        def gatv2_layer(x, src, dst, Wl, bl, Wr, br, att, bias, n_nodes):
            C = att.shape[1]
            xl = (x @ Wl + bl).reshape(n_nodes, H, C)
            xr = (x @ Wr + br).reshape(n_nodes, H, C)
            e = jax.nn.leaky_relu(xl[src] + xr[dst], NEG_SLOPE)
            alpha = jnp.einsum('ehc,hc->eh', e, att)
            m = jax.ops.segment_max(alpha, dst, num_segments=n_nodes)
            m = jnp.where(jnp.isfinite(m), m, 0.0)
            a = jnp.exp(alpha - m[dst])
            denom = jax.ops.segment_sum(a, dst, num_segments=n_nodes)
            a = a / (denom[dst] + 1e-16)
            out = jax.ops.segment_sum(a[:, :, None] * xl[src], dst, num_segments=n_nodes)
            return out.mean(axis=1) + bias
        n = x.shape[0]
        loop = jnp.arange(n, dtype=edge_index.dtype)
        src = jnp.concatenate([edge_index[0], loop])
        dst = jnp.concatenate([edge_index[1], loop])
        h = jax.nn.relu(gatv2_layer(x, src, dst, W1l, b1l, W1r, b1r, att1, bias1, n))
        h = jax.nn.relu(gatv2_layer(h, src, dst, W2l, b2l, W2r, b2r, att2, bias2, n))
        return h @ Wfc + bfc

    def _L3_gnn_ref(x, adj_t, edge_types, W1, Q1, K1, b1, W2, Q2, K2, b2):
        import jax, jax.numpy as jnp
        import numpy as np
        N, E, R, H = (50000, 25000, 8, 4)
        F_IN, HID, OUT = (64, 64, 64)
        NEG_SLOPE = 0.2

        def _glorot(key, shape):
            fan_in, fan_out = (shape[-2], shape[-1])
            std = np.sqrt(2.0 / (fan_in + fan_out)).astype(np.float32)
            return jax.random.normal(key, shape, dtype=jnp.float32) * std

        def _rgat_conv(x, src, dst, etype, W, Q, K, b):
            n = x.shape[0]
            hc = W.shape[-1]
            xw = jnp.einsum('ni,rio->rno', x, W)
            qn = jnp.einsum('rno,roh->rnh', xw, Q)
            kn = jnp.einsum('rno,roh->rnh', xw, K)
            alpha = jax.nn.leaky_relu(qn[etype, dst] + kn[etype, src], NEG_SLOPE)
            amax = jax.ops.segment_max(alpha, dst, num_segments=n)
            amax = jnp.where(jnp.isfinite(amax), amax, 0.0)
            ex = jnp.exp(alpha - amax[dst])
            denom = jax.ops.segment_sum(ex, dst, num_segments=n)
            attn = ex / (denom[dst] + 1e-16)
            out_j = xw[etype, src].reshape(-1, H, hc // H)
            agg = jax.ops.segment_sum(attn[:, :, None] * out_j, dst, num_segments=n)
            return agg.reshape(n, hc) + b
        src, dst = (adj_t[0], adj_t[1])
        h = _rgat_conv(x, src, dst, edge_types, W1, Q1, K1, b1)
        h = jax.nn.relu(h)
        return _rgat_conv(h, src, dst, edge_types, W2, Q2, K2, b2)
    edge_index = jnp.stack([src, dst])
    h = jnp.maximum(_layernorm(x, axis=-1), 0.0)
    x = x + _L0_gnn_ref(h, edge_weight, L0_gnn_W_self, L0_gnn_W_neigh, L0_gnn_b_neigh, src, dst)
    h = jnp.maximum(_layernorm(x, axis=-1), 0.0)
    x = x + _L1_gnn_ref(h, src, dst, L1_gnn_a_mu0, L1_gnn_a_ls0, L1_gnn_a_mu1, L1_gnn_a_ls1, L1_gnn_W0, L1_gnn_b0, L1_gnn_W1, L1_gnn_b1, edge_attr_64, edge_attr_64_n2)
    h = jnp.maximum(_layernorm(x, axis=-1), 0.0)
    x = x + _L2_gnn_ref(h, edge_index, L2_gnn_W1l, L2_gnn_b1l, L2_gnn_W1r, L2_gnn_b1r, L2_gnn_att1, L2_gnn_bias1, L2_gnn_W2l, L2_gnn_b2l, L2_gnn_W2r, L2_gnn_b2r, L2_gnn_att2, L2_gnn_bias2, L2_gnn_Wfc, L2_gnn_bfc)
    h = jnp.maximum(_layernorm(x, axis=-1), 0.0)
    x = x + _L3_gnn_ref(h, edge_index, edge_type_8, L3_gnn_W1, L3_gnn_Q1, L3_gnn_K1, L3_gnn_b1, L3_gnn_W2, L3_gnn_Q2, L3_gnn_K2, L3_gnn_b2)
    return x

_drawn_inputs = setup_inputs


def setup_inputs(seed=0):
    import zlib

    import numpy as np

    out = dict(_drawn_inputs(seed))
    spreads = {'L0_gnn_b_neigh': (0.0, 0.1),
     'L1_gnn_a_ls0': (1.0, 0.6),
     'L1_gnn_a_ls1': (1.0, 0.6),
     'L1_gnn_b0': (0.0, 2.0),
     'L1_gnn_b1': (0.0, 2.0),
     'L2_gnn_b1l': (0.0, 0.8),
     'L2_gnn_b1r': (0.0, 0.8),
     'L2_gnn_bias1': (0.0, 0.8),
     'L2_gnn_b2l': (0.0, 0.8),
     'L2_gnn_b2r': (0.0, 0.8),
     'L2_gnn_bias2': (0.0, 0.427),
     'L2_gnn_bfc': (0.0, 0.1),
     'L3_gnn_b1': (0.0, 0.375),
     'L3_gnn_b2': (0.0, 0.1)}
    factors = {'edge_attr_64': 8.0,
     'edge_attr_64_n2': 8.0,
     'L1_gnn_a_mu0': 7.339,
     'L1_gnn_a_mu1': 8.0,
     'L1_gnn_W0': 6.913,
     'L1_gnn_W1': 6.161,
     'L2_gnn_W1l': 8.0,
     'L2_gnn_W1r': 8.0,
     'L2_gnn_att1': 8.0,
     'L2_gnn_W2l': 8.0,
     'L2_gnn_W2r': 8.0,
     'L2_gnn_att2': 8.0,
     'L2_gnn_Wfc': 2.866,
     'L3_gnn_Q1': 2.673,
     'L3_gnn_K1': 2.998,
     'L3_gnn_Q2': 4.209,
     'L3_gnn_K2': 5.529}
    for name, (base, spread) in spreads.items():
        noise = np.random.default_rng([zlib.crc32(name.encode()), seed]).standard_normal(out[name].shape)
        drawn = base * np.exp(spread * noise) if base else spread * noise
        out[name] = jnp.asarray(drawn.astype(out[name].dtype))
    for name, factor in factors.items():
        out[name] = (out[name] * factor).astype(out[name].dtype)
    return out
```

```python
import concourse.bass as bass
from concourse import mybir
from concourse.alu_op_type import AluOpType as ALU
from contextlib import ExitStack

F32 = mybir.dt.float32
I32 = mybir.dt.int32
ACT = mybir.ActivationFunctionType
AX = mybir.AxisListType.X

P = 128
N = 3125
E = 103125
D = 64
BN = 125
NB = N // BN
C = 128
NCH = 832
NT = 7
NS = NT * P
EP = 125
HALF = 8
U = 2 * HALF
TURNS = NCH // U
NG = NS // HALF
MROWS = E // C + 2
BANK = 512
R = 8
HA = 5
HR = 4
DR = D // HR
EPS = 1e-5
TINY = 1e-16
SLOPE = 0.2
FAR = -1e30
SRC, SRC_TYPE, BLOCK, DLOC, WEIGHT, SRC_LO, SRC_HI, TYPE = range(8)
assert NCH * C >= E + NB * C and NCH % U == 0 and NS >= NCH


def build(nc, io, out):
    ctx = ExitStack()
    with ctx:
        phase = [0]

        def sb(name, shape, dt=F32, stack=ctx):
            return stack.enter_context(nc.sbuf_tensor(f"{name}_{phase[0]}", shape, dt))

        def pb(name, shape, dt=F32, stack=ctx):
            return stack.enter_context(nc.psum_tensor(f"{name}_{phase[0]}", shape, dt))

        def sem(name):
            return ctx.enter_context(nc.semaphore(name))

        meta = nc.dram_tensor("meta", [MROWS, 4, C], I32, kind="Internal").ap()
        chunk_row_dram = nc.dram_tensor("chunk_rows", [2, NS], I32, kind="Internal").ap()
        hist_dram = nc.dram_tensor("hist", [NB * C], F32, kind="Internal").ap()
        slots = nc.dram_tensor("slots", [NG, P, R * HALF], I32, kind="Internal").ap()
        node_table = nc.dram_tensor("node_table", [N, D], F32, kind="Internal").ap()
        xl_table = nc.dram_tensor("xl_table", [N, HA * D + HA], F32, kind="Internal").ap()
        rel_table = nc.dram_tensor("rel_table", [N * R, D + HR], F32, kind="Internal").ap()
        stash_a = nc.dram_tensor("stash_a", [NG, P, HALF * (HA * D + HA)], F32, kind="Internal").ap()
        stash_r = nc.dram_tensor("stash_r", [NG, P, HALF * (D + HR)], F32, kind="Internal").ap()

        X = sb("X", [BN, NB, D])
        H = sb("H", [BN, NB, D])
        ident = sb("ident", [P, P])
        ones = sb("ones", [P, P])
        pos = sb("pos", [P, P])
        part = sb("part", [P, 1])
        key = sb("key", [P, NT, C])
        rows = sb("rows", [1, 2, NS], I32)
        bc_n = sb("bc_n", [BN, 9, D])
        bc_big = sb("bc_big", [BN, 4, HA * D])
        att_bc = sb("att_bc", [P, 2, HA * D])
        e_ls = sb("e_ls", [BN, 4, D])
        w0 = sb("w0", [P, 2, D])
        w1 = sb("w1", [D, 2, D])
        w2 = sb("w2", [D, 4, HA * D])
        wfc = sb("wfc", [D, D])
        w3 = sb("w3", [D, 2, R, D])
        w3t = sb("w3t", [D, 2, R, D])
        kq = sb("kq", [D, 2, R, 2, HR])
        wkq = sb("wkq", [D, 2, 2, R, HR])
        deg_in = sb("deg_in", [BN, NB])
        deg_out = sb("deg_out", [BN, NB])

        dve_step = sem("dve_step")
        steps = [0]

        def link(ins):
            steps[0] += 1
            ins.then_inc(dve_step, 1)
            nc.vector.wait_ge(dve_step, steps[0])

        s_const = sem("constants_made")
        s_dst = sem("dst_loaded")
        s_meta = sem("meta_packed")
        s_zero = sem("zeros_made")
        s_tail = sem("meta_tail_zeroed")
        s_cnt = sem("counts_made")
        s_sum = sem("counts_summed")
        s_idx = sem("row_indices_made")
        s_rowsT = sem("chunk_rows_turned")
        s_rowsC = sem("chunk_rows_copied")
        s_rowsD = sem("chunk_rows_in_dram")
        s_rowsS = sem("chunk_rows_loaded")
        s_got = sem("meta_gathered")
        s_slotT = sem("slots_turned")
        s_slotA = sem("slots_arranged")
        s_slotC = sem("slots_copied")
        s_slotD = sem("slots_in_dram")
        s_x = sem("x_loaded")

        st = ExitStack()
        with st:
            NREC = 8
            dst_l = sb("dst_l", [EP, E // EP], I32, st)
            dst_f = sb("dst_f", [EP, E // EP], F32, st)
            cmp_l = sb("cmp_l", [EP, E // EP], F32, st)
            zrow = sb("zrow", [2, 4, C], I32, st)
            cnt = sb("cnt", [EP, NB + 1], F32, st)
            first = sb("first", [P, NB + 1], F32, st)
            nb = sb("nb", [P, NB], F32, st)
            t_f = sb("t_f", [P, NB], F32, st)
            t_i = sb("t_i", [P, NB], I32, st)
            t_j = sb("t_j", [P, NB], I32, st)
            nch = sb("nch", [P, NB], F32, st)
            cs = sb("cs", [P, NB], F32, st)
            pad = sb("pad", [P, NB], F32, st)
            dpad = sb("dpad", [P, NB], F32, st)
            cid = sb("cid", [P, NT], F32, st)
            cmp = sb("cmp", [P, NT, NB], F32, st)
            prod = sb("prod", [P, NT, NB], F32, st)
            be = sb("be", [P, 2, NT], F32, st)
            padc = sb("padc", [P, NT], F32, st)
            endc = sb("endc", [P, NT], F32, st)
            nv = sb("nv", [P, NT], F32, st)
            e0c = sb("e0c", [P, NT], F32, st)
            e0i = sb("e0i", [P, NT], I32, st)
            ridx = sb("ridx", [P, 2, NT], I32, st)
            off = sb("off", [P, NT], I32, st)
            bit_i = sb("bit_i", [P, NT], I32, st)
            bit = sb("bit", [P, 7, NT], F32, st)
            nbit = sb("nbit", [P, 7, NT], F32, st)
            base = sb("base", [P, NT], F32, st)
            rows7 = sb("rows7", [NT, 2, C], I32, st)
            got = sb("got", [P, NT, 2, 4, C], I32, st)
            wa = sb("wa", [P, NT, 4, 2 * C], F32, st)
            wb = sb("wb", [P, NT, 4, 2 * C], F32, st)
            fin = wa[:, :, :, :].rearrange("p t a k -> p (t a k)").rearrange("p (r t c) -> p r t c", r=NREC, t=NT)
            rec = got[:, :, :, :, :].rearrange("p t h a k -> p (t h a k)").rearrange("p (g r e) -> p g r e", g=NG, r=NREC)
            valid = sb("valid", [P, NT, C], F32, st)
            src_c = sb("src_c", [P, NT, C], I32, st)
            lo_i = sb("lo_i", [P, NT, C], I32, st)
            ps_cnt = pb("ps_cnt", [P, BANK], F32, st)
            ps_row = pb("ps_row", [P, BANK], F32, st)
            ps_turn = pb("ps_turn", [P, 2, 2 * BANK], F32, st)

            with nc.Block() as block:
                @block.sync
                def _(sp):
                    sp.dma_start(dst_l[:, :], io["dst"].rearrange("(p k) -> p k", p=EP)).then_inc(s_dst, 16)
                    full = (MROWS - 2) * C
                    for a, name in enumerate(("src", "dst", "edge_type_8", "edge_weight")):
                        v = io[name]
                        if name == "edge_weight":
                            v = v.bitcast(I32)
                        sp.dma_start(meta[0:MROWS - 2, a, :], v[0:full].rearrange("(r k) -> r k", k=C)).then_inc(s_meta, 16)
                        sp.dma_start(meta[MROWS - 2:MROWS - 1, a, 0:E - full],
                                     v[full:E].rearrange("(r k) -> r k", r=1)).then_inc(s_meta, 16)
                    for n, name in enumerate(("L0_gnn_b_neigh", "L1_gnn_b0", "L1_gnn_b1", "L2_gnn_bias1", "L2_gnn_bias2", "L2_gnn_bfc", "L3_gnn_b1", "L3_gnn_b2")):
                        for k in range(2 if n == 0 else 1):
                            v = io[name][k] if n == 0 else io[name]
                            sp.dma_start(bc_n[:, n + (k if n == 0 else 1), :], v.partition_broadcast(BN)).then_inc(s_x, 16)
                    for n, name in enumerate(("L1_gnn_a_mu0", "L1_gnn_a_ls0", "L1_gnn_a_mu1", "L1_gnn_a_ls1")):
                        sp.dma_start(e_ls[:, n, :], io[name].partition_broadcast(BN)).then_inc(s_x, 16)
                    for n, name in enumerate(("L2_gnn_b1l", "L2_gnn_b1r", "L2_gnn_b2l", "L2_gnn_b2r")):
                        sp.dma_start(bc_big[:, n, :], io[name].partition_broadcast(BN)).then_inc(s_x, 16)
                    for n, name in enumerate(("L2_gnn_W1l", "L2_gnn_W1r", "L2_gnn_W2l", "L2_gnn_W2r")):
                        sp.dma_start(w2[:, n, :], io[name]).then_inc(s_x, 16)
                    for n in range(2):
                        sp.dma_start(att_bc[:, n, :], io[f"L2_gnn_att{n + 1}"].rearrange("h f -> (h f)").partition_broadcast(P)).then_inc(s_x, 16)
                        sp.dma_start(w0[0:D, n, :], io["L0_gnn_W_self_T"][n]).then_inc(s_x, 16)
                        sp.dma_start(w0[D:P, n, :], io["L0_gnn_W_neigh_T"][n]).then_inc(s_x, 16)
                        sp.dma_start(w1[:, n, :], io[f"L1_gnn_W{n}"]).then_inc(s_x, 16)
                        sp.dma_start(w3[:, n, :, :], io[f"L3_gnn_W{n + 1}"].rearrange("r i o -> i r o")).then_inc(s_x, 16)
                        sp.dma_start(w3t[:, n, :, :], io[f"L3_gnn_W{n + 1}_T"].rearrange("r i o -> i r o")).then_inc(s_x, 16)
                        sp.dma_start(kq[:, n, :, 0, :], io[f"L3_gnn_K{n + 1}"].rearrange("r i o -> i r o")).then_inc(s_x, 16)
                        sp.dma_start(kq[:, n, :, 1, :], io[f"L3_gnn_Q{n + 1}"].rearrange("r i o -> i r o")).then_inc(s_x, 16)
                    sp.dma_start(wfc[:, :], io["L2_gnn_Wfc"]).then_inc(s_x, 16)
                    sp.dma_start(X[:, :, :], io["x"].rearrange("(b p) f -> p b f", p=BN)).then_inc(s_x, 16)
                    sp.wait_ge(s_zero, 1)
                    sp.dma_start(meta[MROWS - 2:MROWS - 1, :, E - full:C],
                                 zrow[0:1, :, E - full:C]).then_inc(s_tail, 16)
                    sp.dma_start(meta[MROWS - 1:MROWS, :, :], zrow[1:2, :, :]).then_inc(s_tail, 16)
                    sp.wait_ge(s_rowsC, 1)
                    for k in range(2):
                        sp.dma_start(chunk_row_dram[k, :].rearrange("(t c) -> t c", t=NT),
                                     rows7[:, k, :]).then_inc(s_rowsD, 16)
                    sp.wait_ge(s_rowsD, 32)
                    sp.dma_start(rows[0:1, :, :], chunk_row_dram.rearrange("k n -> (k n)").rearrange("(a k n) -> a k n", a=1, k=2)).then_inc(s_rowsS, 16)
                    sp.wait_ge(s_rowsS, 16)
                    sp.wait_ge(s_x, 16 * 39)
                    sp.wait_ge(s_slotC, NREC + 1)
                    sp.dma_start(slots.rearrange("g p r -> p g r"), rec[:, :, :, :].rearrange("p g a e -> p g (a e)")).then_inc(s_slotD, 16)
                    sp.wait_ge(s_slotD, 16)

                @block.gpsimd
                def _(pool):
                    nc.gpsimd.iota(pos[:, :], [[1, P]], base=0, channel_multiplier=0,
                                   allow_small_or_imprecise_dtypes=True).then_inc(s_const, 1)
                    nc.gpsimd.iota(part[:, :], [[1, 1]], base=0, channel_multiplier=1,
                                   allow_small_or_imprecise_dtypes=True).then_inc(s_const, 1)
                    nc.gpsimd.iota(cid[:, :], [[P, NT]], base=0, channel_multiplier=1,
                                   allow_small_or_imprecise_dtypes=True).then_inc(s_const, 1)
                    nc.gpsimd.memset(ones[:, :], 1.0).then_inc(s_const, 1)
                    nc.gpsimd.memset(zrow[:, :, :], 0).then_inc(s_zero, 1)
                    pool.wait_ge(s_meta, 16 * 8)
                    pool.wait_ge(s_tail, 32)
                    pool.wait_ge(s_idx, 1)
                    for t in range(NT):
                        for h in range(2):
                            pool.indirect_dma_start(
                                got[:, t, h, :, :].rearrange("p a k -> p (a k)"), None,
                                meta.rearrange("r a k -> r (a k)"),
                                bass.IndirectOffsetOnAxis(ridx[:, h, t:t + 1], 0)).then_inc(s_got, 16)

                @block.tensor
                def _(pe):
                    pe.wait_ge(s_const, 4)
                    pe.wait_ge(s_cnt, 1)
                    nc.tensor.matmul(ps_cnt[:, 0:NB + 1], ones[0:EP, :], cnt[:, :], start=True, stop=True).then_inc(s_sum, 1)
                    pe.wait_ge(s_idx, 1)
                    for k in range(2):
                        last = nc.tensor.transpose(ps_row[0:NT, k * P:(k + 1) * P], be[:, k, :], ident[:, :])
                    last.then_inc(s_rowsT, 1)
                    pe.wait_ge(s_slotA, 1)
                    for a in range(NREC):
                        if a >= 2:
                            pe.wait_ge(s_slotC, a - 1)
                        for t in range(NT):
                            last = nc.tensor.transpose(ps_turn[:, a % 2, t * P:(t + 1) * P], fin[:, a, t, :], ident[:, :])
                        last.then_inc(s_slotT, 1)

                @block.scalar
                def _(act):
                    act.wait_ge(s_rowsT, 1)
                    nc.scalar.activation(rows7[:, :, :], ps_row[0:NT, 0:2 * P].rearrange("t (k c) -> t k c", k=2),
                                         ACT.Copy).then_inc(s_rowsC, 1)
                    for a in range(NREC):
                        act.wait_ge(s_slotT, a + 1)
                        dest = rec[:, :, a, :] if a in (SRC, SRC_TYPE, BLOCK) else rec[:, :, a, :].bitcast(F32)
                        nc.scalar.activation(dest, ps_turn[:, a % 2, 0:NS].rearrange("p (g e) -> p g e", e=HALF), ACT.Copy).then_inc(s_slotC, 1)
                    act.wait_ge(s_x, 16 * 39)
                    for k in (1, 3):
                        last = nc.scalar.activation(e_ls[:, k, :], e_ls[:, k, :], ACT.Exp)
                    last.then_inc(s_slotC, 1)

                @block.vector
                def _(dve):
                    v = nc.vector
                    dve.wait_ge(s_const, 4)
                    link(v.tensor_scalar(ident[:, :], pos[:, :], part[:, 0:1], None, ALU.is_equal))
                    dve.wait_ge(s_dst, 16)
                    v.memset(cnt[:, 0:1], 0.0)
                    v.memset(cnt[:, NB:NB + 1], float(E // EP))
                    link(v.tensor_copy(dst_f[:, :], dst_l[:, :]))
                    for b in range(1, NB):
                        link(v.tensor_scalar(cmp_l[:, :], dst_f[:, :], float(BN * b), None, ALU.is_lt, ALU.add,
                                             accum_out=cnt[:, b:b + 1]))
                    v.tensor_copy(t_f[:, 0:1], part[:, 0:1]).then_inc(s_cnt, 1)
                    dve.wait_ge(s_sum, 1)
                    link(v.tensor_copy(first[:, :], ps_cnt[:, 0:NB + 1]))
                    link(v.tensor_tensor(nb[:, :], first[:, 1:NB + 1], first[:, 0:NB], ALU.subtract))
                    link(v.tensor_scalar(t_i[:, :], nb[:, :], float(C - 1), None, ALU.add))
                    link(v.tensor_scalar(t_j[:, :], t_i[:, :], 7, None, ALU.arith_shift_right))
                    link(v.tensor_scalar(nch[:, :], t_j[:, :], 1.0, None, ALU.max))
                    link(v.tensor_tensor_scan(cs[:, :], ones[:, 0:NB], nch[:, :], 0.0, ALU.mult, ALU.add))
                    link(v.tensor_tensor(cs[:, :], cs[:, :], nch[:, :], ALU.subtract))
                    link(v.scalar_tensor_tensor(pad[:, :], cs[:, :], float(C), first[:, 0:NB], ALU.mult, ALU.subtract))
                    v.memset(dpad[:, 0:1], 0.0)
                    link(v.tensor_tensor(dpad[:, 1:NB], pad[:, 1:NB], pad[:, 0:NB - 1], ALU.subtract))
                    link(v.tensor_tensor(cmp[:, :, :], cid[:, :].unsqueeze(2).to_broadcast([P, NT, NB]),
                                         cs[:, :].unsqueeze(1).to_broadcast([P, NT, NB]), ALU.is_ge))
                    link(v.tensor_reduce(be[:, 0, :], cmp[:, :, :], AX, ALU.add))
                    link(v.tensor_scalar(be[:, 0, :], be[:, 0, :], -1.0, None, ALU.add))
                    link(v.tensor_tensor(prod[:, :, :], cmp[:, :, :], dpad[:, :].unsqueeze(1).to_broadcast([P, NT, NB]), ALU.mult))
                    link(v.tensor_reduce(padc[:, :], prod[:, :, :], AX, ALU.add))
                    link(v.tensor_tensor(prod[:, :, :], cmp[:, :, :], nb[:, :].unsqueeze(1).to_broadcast([P, NT, NB]), ALU.mult))
                    link(v.tensor_reduce(endc[:, :], prod[:, :, :], AX, ALU.add))
                    link(v.scalar_tensor_tensor(e0c[:, :], cid[:, :], float(C), padc[:, :], ALU.mult, ALU.subtract))
                    link(v.tensor_tensor(nv[:, :], endc[:, :], e0c[:, :], ALU.subtract))
                    link(v.tensor_scalar(be[:, 1, :], e0c[:, :], float(E - 1), None, ALU.min))
                    link(v.tensor_scalar(e0c[:, :], e0c[:, :], float((MROWS - 1) * C - 1), None, ALU.min))
                    link(v.tensor_copy(e0i[:, :], e0c[:, :]))
                    link(v.tensor_scalar(ridx[:, 0, :], e0i[:, :], 7, None, ALU.arith_shift_right))
                    link(v.tensor_scalar(ridx[:, 1, :], ridx[:, 0, :], 1.0, None, ALU.add))
                    v.tensor_scalar(off[:, :], e0i[:, :], C - 1, None, ALU.bitwise_and).then_inc(s_idx, 1)
                    dve.wait_ge(s_idx, 1)
                    for k in range(7):
                        link(v.tensor_scalar(bit_i[:, :], off[:, :], k, 1, ALU.arith_shift_right, ALU.bitwise_and))
                        link(v.tensor_copy(bit[:, k, :], bit_i[:, :]))
                    link(v.tensor_scalar(nbit[:, :, :], bit[:, :, :], -1.0, 1.0, ALU.mult, ALU.add))
                    dve.wait_ge(s_got, 16 * 2 * NT)
                    for h in range(2):
                        link(v.tensor_copy(wa[:, :, 0:3, h * C:(h + 1) * C], got[:, :, h, 0:3, :]))
                        link(v.tensor_copy(wa[:, :, 3, h * C:(h + 1) * C], got[:, :, h, 3, :].bitcast(F32)))
                    now, nxt, width = wa, wb, 2 * C
                    for k in range(6, -1, -1):
                        s = 1 << k
                        width = max(width - s, C)
                        for t in range(NT):
                            link(v.tensor_scalar(nxt[:, t, :, 0:width], now[:, t, :, 0:width], nbit[:, k, t:t + 1], None, ALU.mult))
                            link(v.scalar_tensor_tensor(nxt[:, t, :, 0:width], now[:, t, :, s:s + width], bit[:, k, t:t + 1],
                                                        nxt[:, t, :, 0:width], ALU.mult, ALU.add))
                        now, nxt = nxt, now
                    for t in range(NT):
                        v.tensor_scalar(valid[:, t, :], pos[:, :], nv[:, t:t + 1], None, ALU.is_lt)
                    link(v.tensor_scalar(base[:, :], be[:, 0, :], float(BN), -1.0, ALU.mult, ALU.add))
                    a_src, a_dst = now[:, :, 0, 0:C], now[:, :, 1, 0:C]
                    link(v.scalar_tensor_tensor(key[:, :, :], a_dst, 1.0, valid[:, :, :], ALU.add, ALU.mult))
                    link(v.tensor_scalar(key[:, :, :], key[:, :, :], -1.0, None, ALU.add))
                    for t in range(NT):
                        link(v.scalar_tensor_tensor(fin[:, DLOC, t, :], now[:, t, 1, 0:C], base[:, t:t + 1], valid[:, t, :],
                                                    ALU.subtract, ALU.mult))
                    link(v.tensor_scalar(fin[:, DLOC, :, :], fin[:, DLOC, :, :], -1.0, None, ALU.add))
                    link(v.tensor_copy(fin[:, SRC, :, :], a_src))
                    link(v.tensor_copy(fin[:, TYPE, :, :], now[:, :, 2, 0:C]))
                    link(v.tensor_copy(fin[:, WEIGHT, :, :], now[:, :, 3, 0:C]))
                    link(v.tensor_copy(src_c[:, :, :], a_src))
                    link(v.tensor_scalar(lo_i[:, :, :], src_c[:, :, :], C - 1, None, ALU.bitwise_and))
                    link(v.scalar_tensor_tensor(fin[:, SRC_LO, :, :], lo_i[:, :, :], 1.0, valid[:, :, :], ALU.add, ALU.mult))
                    link(v.tensor_scalar(fin[:, SRC_LO, :, :], fin[:, SRC_LO, :, :], -1.0, None, ALU.add))
                    link(v.tensor_scalar(lo_i[:, :, :], src_c[:, :, :], 7, None, ALU.arith_shift_right))
                    link(v.tensor_copy(fin[:, SRC_HI, :, :], lo_i[:, :, :]))
                    link(v.tensor_copy(fin[:, BLOCK, :, :], be[:, 0, :].unsqueeze(2).to_broadcast([P, NT, C])))
                    v.scalar_tensor_tensor(fin[:, SRC_TYPE, :, :], fin[:, SRC, :, :], float(R), fin[:, TYPE, :, :],
                                           ALU.mult, ALU.add).then_inc(s_slotA, 1)

        s_sq = sem("variances_made")
        s_rt = sem("roots_made")
        n_norm = [0]

        def norm(act, dve, part_of, st_tiles):
            mean, cen, sq, var = st_tiles
            n = n_norm[0]
            if part_of == "scalar":
                act.wait_ge(s_sq, n + 1)
                nc.scalar.activation(var[:, :], var[:, :], ACT.Sqrt).then_inc(s_rt, 1)
                return
            v = nc.vector
            link(v.tensor_reduce(mean[:, :], X[:, :, :], AX, ALU.add))
            link(v.tensor_scalar(mean[:, :], mean[:, :], 1.0 / D, None, ALU.mult))
            link(v.tensor_tensor(cen[:, :, :], X[:, :, :], mean[:, :].unsqueeze(2).to_broadcast([BN, NB, D]), ALU.subtract))
            link(v.tensor_tensor(sq[:, :, :], cen[:, :, :], cen[:, :, :], ALU.mult))
            link(v.tensor_reduce(var[:, :], sq[:, :, :], AX, ALU.add))
            v.tensor_scalar(var[:, :], var[:, :], 1.0 / D, EPS, ALU.mult, ALU.add).then_inc(s_sq, 1)
            dve.wait_ge(s_rt, n + 1)
            link(v.reciprocal(var[:, :], var[:, :]))
            link(v.tensor_tensor(cen[:, :, :], cen[:, :, :], var[:, :].unsqueeze(2).to_broadcast([BN, NB, D]), ALU.mult))
            link(v.tensor_scalar(H[:, :, :], cen[:, :, :], 0.0, None, ALU.max))

        def norm_phase():
            phase[0] += 1
            ns = ExitStack()
            with ns:
                tiles = (sb("mean", [BN, NB], F32, ns), sb("cen", [BN, NB, D], F32, ns),
                         sb("sq", [BN, NB, D], F32, ns), sb("var", [BN, NB], F32, ns))
                with nc.Block() as block:
                    @block.scalar
                    def _(act):
                        norm(act, None, "scalar", tiles)

                    @block.vector
                    def _(dve):
                        norm(None, dve, "vector", tiles)
            n_norm[0] += 1

        class Counted:

            def __init__(self, name, credit=0):
                self.sem, self.base, self.credit = sem(name), 0, credit

            def at(self, n):
                return self.base + self.credit + n

            def over(self, n):
                self.base += self.credit + n

        staged = [Counted(f"staged_{h}") for h in range(2)]
        gathered = [Counted(f"gathered_{j}") for j in range(U)]
        stashed = [Counted(f"stashed_{h}", 16) for h in range(2)]
        loaded = [Counted(f"loaded_{h}") for h in range(2)]
        attr_loaded = [Counted(f"attr_loaded_{j}") for j in range(U)]
        msg_made = Counted("messages_made")
        onehot_made = Counted("onehots_made")
        chunk_done = Counted("chunks_done", U)
        turned = Counted("onehots_turned")
        turned_copied = Counted("turned_copied")
        dest_made = Counted("dest_rows_made")
        z_made = Counted("z_made", 2)
        self_kept = Counted("self_scores_kept", 2)
        leaky_made = Counted("leaky_made")
        pool_seen = sem("pool_saw_stage")

        sp_seen = sem("sp_saw_stash")
        pe_seen = sem("pe_saw_stage")

        def load_blocks(i_stage, q):
            return nc.values_load_multi_w_load_instructions(
                i_stage[0:1, BLOCK, q:q + 4], engines=[mybir.EngineType.PE], min_val=0, max_val=NB - 1,
                skip_runtime_bounds_check_because="blocks are counted below NB")[1]

        def stage_half(sp, stage, i, h, others=()):
            sp.wait_ge(chunk_done.sem, chunk_done.at((i - 1) * U + HALF * (h + 1)))
            for c in others:
                sp.sem_inc(sp_seen, 1)
                sp.wait_ge(c.sem, c.at(16 * i))
                sp.sem_inc(sp_seen, 1)
            sp.dma_start(stage[:, h, :, :].rearrange("p a e -> p (a e)"),
                         slots[bass.ds(2 * i + h, 1), :, :].rearrange("o p r -> (o p) r")).then_inc(staged[h].sem, 16)

        def gather_loop(pool, stage, G, width, table, field):
            with pool.Fori(0, TURNS) as i:
                for h in range(2):
                    pool.wait_ge(staged[h].sem, staged[h].at(16 * i + 16))
                    pool.sem_inc(pool_seen, 1)
                    for j in range(HALF * h, HALF * (h + 1)):
                        pool.indirect_dma_start(G[:, j, 0:width], None, table,
                                                bass.IndirectOffsetOnAxis(stage[:, h, field, j % HALF:j % HALF + 1], 0)
                                                ).then_inc(gathered[j].sem, 16)

        def make_onehots(dve, stage_f, S, h):
            return nc.vector.tensor_tensor(
                S[:, HALF * h:HALF * (h + 1), :], pos[:, 0:BN].unsqueeze(1).to_broadcast([P, HALF, BN]),
                stage_f[:, h, DLOC, :].unsqueeze(2).to_broadcast([P, HALF, BN]), ALU.is_equal)

        def zero_sums(ps, zero, banks):
            for k in range(banks):
                nc.tensor.matmul(ps[:, k * BANK:(k + 1) * BANK], zero[:, 0:P], zero[:, :], start=True, stop=True)

        def sum_chunk(ps_sum, S, j, M, width, block):
            return nc.tensor.matmul(ps_sum[0:BN, bass.ds(block * P, width)], S[:, j, :], M,
                                    start=False, stop=True, skip_group_check=True)

        def sums(ps_sum, width):
            return ps_sum[0:BN, 0:NB * P].rearrange("p (b f) -> p b f", f=P)[:, :, 0:width]

        def once(name):
            return sem(f"{name}_{phase[0]}")

        dense_ready = Counted("dense_ready")
        turned_b = Counted("blocks_turned")
        copied_b = Counted("blocks_copied")
        multiplied_b = Counted("blocks_multiplied")
        taken_b = Counted("blocks_taken")

        def dense(cat, k, pieces, take, before=None, after=None, sp_program=None):
            phase[0] += 1
            es = ExitStack()
            with es:
                catT = sb("catT", [P, 2, P], F32, es)
                ps_t = pb("ps_t", [P, 2, BANK], F32, es)
                ps_o = pb("ps_o", [P, 2, 2, BANK], F32, es)
                with nc.Block() as block:
                    @block.vector
                    def _(dve):
                        if before is not None:
                            before(dve)
                        dve.sem_inc(dense_ready.sem, 1)
                        for b in range(NB):
                            dve.wait_ge(multiplied_b.sem, multiplied_b.at(b + 1))
                            take(dve, b, ps_o[0:BN, b % 2, :, :]).then_inc(taken_b.sem, 1)
                        if after is not None:
                            dve.wait_ge(taken_b.sem, taken_b.at(NB))
                            after(dve)

                    @block.tensor
                    def _(pe):
                        pe.wait_ge(dense_ready.sem, dense_ready.at(1))

                        def turn(b):
                            if b >= 2:
                                pe.wait_ge(copied_b.sem, copied_b.at(b - 1))
                            nc.tensor.transpose(ps_t[0:k, b % 2, 0:BN], cat[:, b, :], ident[0:BN, 0:BN]).then_inc(turned_b.sem, 1)

                        turn(0)
                        for b in range(NB):
                            if b + 1 < NB:
                                turn(b + 1)
                            pe.wait_ge(copied_b.sem, copied_b.at(b + 1))
                            if b >= 2:
                                pe.wait_ge(taken_b.sem, taken_b.at(b - 1))
                            for n, w in enumerate(pieces):
                                last = nc.tensor.matmul(ps_o[0:BN, b % 2, n, 0:w.shape[1]], catT[0:k, b % 2, 0:BN], w,
                                                        start=True, stop=True)
                            last.then_inc(multiplied_b.sem, 1)

                    @block.scalar
                    def _(act):
                        for b in range(NB):
                            act.wait_ge(turned_b.sem, turned_b.at(b + 1))
                            if b >= 2:
                                act.wait_ge(multiplied_b.sem, multiplied_b.at(b - 1))
                            nc.scalar.activation(catT[0:k, b % 2, 0:BN], ps_t[0:k, b % 2, 0:BN], ACT.Copy).then_inc(copied_b.sem, 1)

                    if sp_program is not None:
                        @block.sync
                        def _(sp):
                            sp_program(sp)
                dense_ready.over(1)
                for c in (turned_b, copied_b, multiplied_b, taken_b):
                    c.over(NB)

        def bcn(ap):
            return ap.unsqueeze(1).to_broadcast([BN, NB, D])

        def bcd(ap):
            return ap.unsqueeze(2).to_broadcast([BN, NB, D])

        def write_table(tile):
            phase[0] += 1
            written = once("table_written")
            with nc.Block() as block:
                @block.sync
                def _(sp):
                    sp.dma_start(node_table.rearrange("(b p) f -> p b f", p=BN), tile).then_inc(written, 16)
                    sp.wait_ge(written, 16)

        def weighted_sums(SUM, hist):
            phase[0] += 1
            es = ExitStack()
            with es:
                stage = sb("stage", [P, 2, R, HALF], I32, es)
                stage_f = stage[:, :, :, :].bitcast(F32)
                G = sb("gathered_rows", [P, U, D], F32, es)
                M = sb("messages", [P, U, D + 1], F32, es)
                S = sb("onehots", [P, U, BN], F32, es)
                Lo = sb("onehots_low", [P, U, P], F32, es)
                Hi = sb("onehots_high", [P, U, NB], F32, es)
                zero = sb("zero_bank", [P, BANK], F32, es)
                HIST = sb("hist_sb", [P, NB], F32, es)
                ps_sum = pb("ps_sum", [P, 7 * BANK], F32, es)
                ps_hist = pb("ps_hist", [P, BANK], F32, es)
                ready, finished, hist_made, hist_stored, hist_loaded = (once(x) for x in (
                    "set_up", "loop_over", "hist_made", "hist_stored", "hist_loaded"))
                with nc.Block() as block:
                    @block.sync
                    def _(sp):
                        with sp.Fori(0, TURNS) as i:
                            for h in range(2):
                                stage_half(sp, stage, i, h)
                        if hist:
                            sp.wait_ge(hist_made, 1)
                            sp.dma_start(hist_dram.rearrange("(h l) -> l h", l=P), HIST[:, :],
                                         allow_slow_non_contiguous=True).then_inc(hist_stored, 16)
                            sp.wait_ge(hist_stored, 16)
                            sp.dma_start(deg_out[:, :], hist_dram[0:N].rearrange("(b p) -> p b", p=BN),
                                         allow_slow_non_contiguous=True).then_inc(hist_loaded, 16)
                            sp.wait_ge(hist_loaded, 16)

                    @block.gpsimd
                    def _(pool):
                        gather_loop(pool, stage, G, D, node_table, SRC)

                    @block.scalar
                    def _(act):
                        with act.Fori(0, TURNS) as i:
                            for h in range(2):
                                act.wait_ge(staged[h].sem, staged[h].at(16 * i + 16))
                                for j in range(HALF * h, HALF * (h + 1)):
                                    act.wait_ge(gathered[j].sem, gathered[j].at(16 * i + 16))
                                    nc.scalar.activation(M[:, j, 0:D], G[:, j, :], ACT.Copy,
                                                         scale=stage_f[:, h, WEIGHT, j % HALF:j % HALF + 1]).then_inc(msg_made.sem, 1)

                    @block.vector
                    def _(dve):
                        v = nc.vector
                        v.memset(zero[:, :], 0.0)
                        v.memset(M[:, :, D:D + 1], 1.0).then_inc(ready, 1)
                        with dve.Fori(0, TURNS) as i:
                            for h in range(2):
                                dve.wait_ge(staged[h].sem, staged[h].at(16 * i + 16))
                                if hist:
                                    for tile, field, w in ((Lo, SRC_LO, P), (Hi, SRC_HI, NB)):
                                        v.tensor_tensor(tile[:, HALF * h:HALF * (h + 1), :],
                                                        pos[:, 0:w].unsqueeze(1).to_broadcast([P, HALF, w]),
                                                        stage_f[:, h, field, :].unsqueeze(2).to_broadcast([P, HALF, w]), ALU.is_equal)
                                make_onehots(dve, stage_f, S, h).then_inc(onehot_made.sem, 1)
                        dve.wait_ge(finished, 1)
                        if hist:
                            v.tensor_copy(HIST[:, :], ps_hist[:, 0:NB]).then_inc(hist_made, 1)
                        link(v.tensor_copy(SUM[:, :, :], sums(ps_sum, D + 1)))
                        if hist:
                            link(v.tensor_copy(deg_in[:, :], SUM[:, :, D]))

                    @block.tensor
                    def _(pe):
                        nc.tensor.nop().then_inc(chunk_done.sem, U)
                        pe.wait_ge(ready, 1)
                        zero_sums(ps_sum, zero, 7)
                        zero_sums(ps_hist, zero, 1)
                        with pe.Fori(0, TURNS) as i:
                            for j in range(U):
                                h = j // HALF
                                if j % HALF == 0:
                                    pe.wait_ge(staged[h].sem, staged[h].at(16 * i + 16))
                                    pe.sem_inc(pe_seen, 1)
                                if j % 4 == 0:
                                    at = load_blocks(stage[:, h], j % HALF)
                                if j % HALF == 0:
                                    pe.wait_ge(onehot_made.sem, onehot_made.at(2 * i + h + 1))
                                if hist:
                                    nc.tensor.matmul(ps_hist[:, 0:NB], Lo[:, j, :], Hi[:, j, :], start=False, stop=True,
                                                     skip_group_check=True)
                                pe.wait_ge(msg_made.sem, msg_made.at(i * U + j + 1))
                                sum_chunk(ps_sum, S, j, M[:, j, :], D + 1, at[j % 4]).then_inc(chunk_done.sem, 1)
                        nc.tensor.matmul(ps_hist[:, 0:1], zero[:, 0:P], zero[:, 0:1], start=False, stop=True,
                                         skip_group_check=True).then_inc(finished, 1)
                for c in (*staged, *gathered):
                    c.over(16 * TURNS)
                msg_made.over(NCH)
                onehot_made.over(2 * TURNS)
                chunk_done.over(NCH)

        def attribute_sums(SUM, attr):
            phase[0] += 1
            es = ExitStack()
            with es:
                stage = sb("stage", [P, 2, R, HALF], I32, es)
                stage_f = stage[:, :, :, :].bitcast(F32)
                G = sb("gathered_rows", [P, U, 2 * D], F32, es)
                A = sb("attributes", [P, U, D], F32, es)
                S = sb("onehots", [P, U, BN], F32, es)
                zero = sb("zero_bank", [P, BANK], F32, es)
                ps_sum = pb("ps_sum", [P, 7 * BANK], F32, es)
                ready, finished = (once(x) for x in ("set_up", "loop_over"))
                with nc.Block() as block:
                    @block.sync
                    def _(sp):
                        with sp.Fori(0, TURNS) as i:
                            for h in range(2):
                                stage_half(sp, stage, i, h)
                                for q in range(0, HALF, 4):
                                    first = nc.values_load_multi_w_load_instructions(
                                        rows[0:1, 1, bass.ds(i * U + HALF * h + q, 4)], engines=[mybir.EngineType.SP],
                                        min_val=0, max_val=E - 1, skip_runtime_bounds_check_because="clipped to E - 1")[1]
                                    for k in range(4):
                                        j = HALF * h + q + k
                                        sp.dma_start(A[:, j, :], attr[bass.ds(first[k], C), :]).then_inc(attr_loaded[j].sem, 16)

                    @block.gpsimd
                    def _(pool):
                        gather_loop(pool, stage, G, D, node_table, SRC)

                    @block.vector
                    def _(dve):
                        v = nc.vector
                        v.memset(zero[:, :], 0.0).then_inc(ready, 1)
                        with dve.Fori(0, TURNS) as i:
                            for h in range(2):
                                dve.wait_ge(staged[h].sem, staged[h].at(16 * i + 16))
                                make_onehots(dve, stage_f, S, h).then_inc(onehot_made.sem, 1)
                                for j in range(HALF * h, HALF * (h + 1)):
                                    dve.wait_ge(gathered[j].sem, gathered[j].at(16 * i + 16))
                                    dve.wait_ge(attr_loaded[j].sem, attr_loaded[j].at(16 * i + 16))
                                    v.tensor_tensor(G[:, j, D:2 * D], G[:, j, 0:D], A[:, j, :], ALU.mult).then_inc(msg_made.sem, 1)
                        dve.wait_ge(finished, 1)
                        link(v.tensor_copy(SUM[:, :, :], sums(ps_sum, 2 * D)))

                    @block.tensor
                    def _(pe):
                        nc.tensor.nop().then_inc(chunk_done.sem, U)
                        pe.wait_ge(ready, 1)
                        zero_sums(ps_sum, zero, 7)
                        with pe.Fori(0, TURNS) as i:
                            for j in range(U):
                                h = j // HALF
                                if j % HALF == 0:
                                    pe.wait_ge(staged[h].sem, staged[h].at(16 * i + 16))
                                    pe.sem_inc(pe_seen, 1)
                                if j % 4 == 0:
                                    at = load_blocks(stage[:, h], j % HALF)
                                if j % HALF == 0:
                                    pe.wait_ge(onehot_made.sem, onehot_made.at(2 * i + h + 1))
                                pe.wait_ge(msg_made.sem, msg_made.at(i * U + j + 1))
                                sum_chunk(ps_sum, S, j, G[:, j, :], 2 * D, at[j % 4]).then_inc(chunk_done.sem, 1)
                        nc.tensor.matmul(ps_sum[:, 6 * BANK + 3 * P:7 * BANK], zero[:, 0:P], zero[:, 0:P], start=False, stop=True,
                                         skip_group_check=True).then_inc(finished, 1)
                for c in (*staged, *gathered, *attr_loaded):
                    c.over(16 * TURNS)
                msg_made.over(NCH)
                onehot_made.over(2 * TURNS)
                chunk_done.over(NCH)

        norm_phase()
        write_table(H[:, :, :])
        ls = ExitStack()
        with ls:
            CAT = sb("cat", [BN, NB, 2 * D], F32, ls)
            SUM = sb("sums", [BN, NB, D + 1], F32, ls)
            inv_deg = sb("inv_deg", [BN, NB], F32, ls)
            has = sb("has", [BN, NB], F32, ls)
            for l in range(2):
                weighted_sums(SUM, l == 0)

                def before(dve, l=l):
                    v = nc.vector
                    if l == 0:
                        link(v.tensor_scalar(has[:, :], deg_in[:, :], 0.0, None, ALU.is_gt))
                        link(v.tensor_scalar(inv_deg[:, :], deg_in[:, :], 1.0, None, ALU.max))
                        link(v.reciprocal(inv_deg[:, :], inv_deg[:, :]))
                        link(v.tensor_tensor(inv_deg[:, :], inv_deg[:, :], has[:, :], ALU.mult))
                    link(v.tensor_copy(CAT[:, :, 0:D], H[:, :, :]))
                    link(v.tensor_tensor(CAT[:, :, D:2 * D], SUM[:, :, 0:D], bcd(inv_deg[:, :]), ALU.mult))

                def take(dve, b, ps):
                    return nc.vector.tensor_copy(H[:, b, :], ps[:, 0, 0:D])

                def after(dve, l=l):
                    v = nc.vector
                    link(v.tensor_tensor(H[:, :, :], H[:, :, :], bcn(bc_n[:, l, :]), ALU.add))
                    if l == 0:
                        link(v.tensor_scalar(H[:, :, :], H[:, :, :], 0.0, None, ALU.max))
                    else:
                        link(v.tensor_tensor(X[:, :, :], X[:, :, :], H[:, :, :], ALU.add))

                dense(CAT[:, :, :], 2 * D, [w0[:, l, :]], take, before, after)
                if l == 0:
                    write_table(H[:, :, :])

        norm_phase()
        ls = ExitStack()
        with ls:
            SUM = sb("sums", [BN, NB, 2 * D], F32, ls)
            AGG = sb("agg", [BN, NB, D], F32, ls)
            norm_of = sb("norm_of", [BN, 2, NB], F32, ls)
            has = sb("has", [BN, NB], F32, ls)
            red = sb("red", [BN, NB], F32, ls)
            roots = sem("norm_roots")
            with nc.Block() as block:
                @block.vector
                def _(dve):
                    v = nc.vector
                    link(v.tensor_scalar(norm_of[:, 0, :], deg_out[:, :], 1.0, None, ALU.max))
                    v.tensor_scalar(norm_of[:, 1, :], deg_in[:, :], 1.0, None, ALU.max).then_inc(roots, 1)
                    dve.wait_ge(roots, 2)
                    link(v.reciprocal(norm_of[:, :, :], norm_of[:, :, :]))
                    for k, deg in enumerate((deg_out, deg_in)):
                        link(v.tensor_scalar(has[:, :], deg[:, :], 0.0, None, ALU.is_gt))
                        link(v.tensor_tensor(norm_of[:, k, :], norm_of[:, k, :], has[:, :], ALU.mult))
                    link(v.tensor_tensor(H[:, :, :], H[:, :, :], bcd(norm_of[:, 0, :]), ALU.mult))

                @block.scalar
                def _(act):
                    act.wait_ge(roots, 1)
                    nc.scalar.activation(norm_of[:, :, :], norm_of[:, :, :], ACT.Sqrt).then_inc(roots, 1)
            for l in range(2):
                write_table(H[:, :, :])
                attribute_sums(SUM, io["edge_attr_64" if l == 0 else "edge_attr_64_n2"])
                exps = sem(f"softmax_exps_{l}")

                def before(dve, l=l):
                    v = nc.vector
                    link(v.tensor_tensor(AGG[:, :, :], SUM[:, :, 0:D], bcn(e_ls[:, 2 * l, :]), ALU.mult))
                    link(v.tensor_tensor(H[:, :, :], SUM[:, :, D:2 * D], bcn(e_ls[:, 2 * l + 1, :]), ALU.mult))
                    link(v.tensor_tensor(AGG[:, :, :], AGG[:, :, :], H[:, :, :], ALU.add))
                    link(v.tensor_tensor(AGG[:, :, :], AGG[:, :, :], bcd(norm_of[:, 1, :]), ALU.mult))

                def take(dve, b, ps):
                    return nc.vector.tensor_copy(H[:, b, :], ps[:, 0, 0:D])

                def after(dve, l=l):
                    v = nc.vector
                    link(v.tensor_tensor(H[:, :, :], H[:, :, :], bcn(bc_n[:, 2 + l, :]), ALU.add))
                    if l == 0:
                        link(v.tensor_scalar(H[:, :, :], H[:, :, :], 0.0, None, ALU.max))
                        link(v.tensor_tensor(H[:, :, :], H[:, :, :], bcd(norm_of[:, 0, :]), ALU.mult))
                    else:
                        link(v.tensor_reduce(red[:, :], H[:, :, :], AX, ALU.max))
                        link(v.tensor_tensor(H[:, :, :], H[:, :, :], bcd(red[:, :]), ALU.subtract))

                dense(AGG[:, :, :], D, [w1[:, l, :]], take, before, after)
            with nc.Block() as block:
                @block.scalar
                def _(act):
                    nc.scalar.activation(H[:, :, :], H[:, :, :], ACT.Exp).then_inc(exps, 1)

                @block.vector
                def _(dve):
                    v = nc.vector
                    dve.wait_ge(exps, 1)
                    link(v.tensor_reduce(red[:, :], H[:, :, :], AX, ALU.add))
                    link(v.reciprocal(red[:, :], red[:, :]))
                    link(v.tensor_tensor(H[:, :, :], H[:, :, :], bcd(red[:, :]), ALU.mult))
                    link(v.tensor_tensor(X[:, :, :], X[:, :, :], H[:, :, :], ALU.add))


        masks_dram = nc.dram_tensor("masks", [P, 4 * NS], F32, kind="Internal").ap()
        row_masks_dram = nc.dram_tensor("row_masks", [HA, 6 * NS], F32, kind="Internal").ap()
        PEN_L, PEN_R, CONT, LAST = range(4)
        ROW_L, ROW_R, ROW_C, LINK_L, LINK_R, LINK_C = range(6)

        def segments_phase():
            phase[0] += 1
            es = ExitStack()
            with es:
                masks = sb("masks", [P, 4, NT, C], F32, es)
                row_m = sb("row_masks", [HA, 6, NS], F32, es)
                ends = sb("ends", [P, 2, NT, HA], F32, es)
                ends_r = sb("ends_r", [HA, 2, NS], F32, es)
                single = sb("single", [HA, NS], F32, es)
                link_n = sb("link_n", [HA, NS], F32, es)
                ps_r = pb("ps_r", [P, 2, 2 * BANK], F32, es)
                ps_c = pb("ps_c", [P, BANK], F32, es)
                ps_w = pb("ps_w", [P, BANK], F32, es)
                ends_made, ends_turned, links_made, links_turned, masks_made, masks_stored, products = (once(x) for x in (
                    "ends_made", "ends_turned", "links_made", "links_turned", "masks_made", "masks_stored", "weight_products"))
                with nc.Block() as block:
                    @block.vector
                    def _(dve):
                        v = nc.vector
                        link(v.tensor_copy(ends[:, 0, :, :], key[:, :, 0].unsqueeze(2).to_broadcast([P, NT, HA])))
                        v.tensor_copy(ends[:, 1, :, :], key[:, :, C - 1].unsqueeze(2).to_broadcast([P, NT, HA])).then_inc(ends_made, 1)
                        v.memset(masks[:, CONT, :, 0:1], 0.0)
                        link(v.tensor_tensor(masks[:, CONT, :, 1:C], key[:, :, 1:C], key[:, :, 0:C - 1], ALU.is_equal))
                        link(v.tensor_scalar(masks[:, PEN_L, :, :], masks[:, CONT, :, :], -1.0, -FAR, ALU.add, ALU.mult))
                        v.memset(masks[:, PEN_R, :, C - 1:C], FAR)
                        link(v.tensor_copy(masks[:, PEN_R, :, 0:C - 1], masks[:, PEN_L, :, 1:C]))
                        link(v.tensor_scalar(masks[:, LAST, :, 0:C - 1], masks[:, CONT, :, 1:C], -1.0, 1.0, ALU.mult, ALU.add))
                        dve.wait_ge(ends_turned, 1)
                        link(v.tensor_copy(ends_r[:, :, :], ps_r[0:HA, :, 0:NS]))
                        link(v.tensor_tensor(single[:, :], ends_r[:, 0, :], ends_r[:, 1, :], ALU.is_equal))
                        v.memset(row_m[:, LINK_C, 0:1], 0.0)
                        v.memset(link_n[:, NS - 1:NS], 0.0)
                        link(v.tensor_tensor(row_m[:, LINK_C, 1:NS], ends_r[:, 0, 1:NS], ends_r[:, 1, 0:NS - 1], ALU.is_equal))
                        link(v.tensor_copy(link_n[:, 0:NS - 1], row_m[:, LINK_C, 1:NS]))
                        link(v.tensor_tensor(row_m[:, ROW_C, :], row_m[:, LINK_C, :], single[:, :], ALU.mult))
                        link(v.tensor_scalar(row_m[:, ROW_L, :], row_m[:, ROW_C, :], -1.0, -FAR, ALU.add, ALU.mult))
                        link(v.tensor_scalar(row_m[:, LINK_L, :], row_m[:, LINK_C, :], -1.0, -FAR, ALU.add, ALU.mult))
                        link(v.tensor_scalar(row_m[:, LINK_R, :], link_n[:, :], -1.0, -FAR, ALU.add, ALU.mult))
                        link(v.tensor_tensor(single[:, :], single[:, :], link_n[:, :], ALU.mult))
                        link(v.tensor_scalar(row_m[:, ROW_R, :], single[:, :], -1.0, -FAR, ALU.add, ALU.mult))
                        dve.sem_inc(links_made, 1)
                        dve.wait_ge(links_turned, 1)
                        link(v.tensor_scalar(masks[:, LAST, :, C - 1], ps_c[:, 0:NT * HA].rearrange("p (t h) -> p t h", h=HA)[:, :, 0],
                                             -1.0, 1.0, ALU.mult, ALU.add))
                        dve.sem_inc(masks_made, 1)
                        dve.wait_ge(products, 1)
                        link(v.tensor_copy(wkq[:, :, :, :, :].rearrange("p l k r h -> p (l k r h)"), ps_w[0:D, 0:4 * R * HR]))

                    @block.tensor
                    def _(pe):
                        pe.wait_ge(ends_made, 1)
                        for k in range(2):
                            for t in range(NT):
                                last = nc.tensor.transpose(ps_r[0:HA, k, t * P:(t + 1) * P], ends[:, k, t, :], ident[:, :])
                        last.then_inc(ends_turned, 1)
                        for l in range(2):
                            for k in range(2):
                                for r in range(R):
                                    n = ((l * 2 + k) * R + r) * HR
                                    last = nc.tensor.matmul(ps_w[0:D, n:n + HR], w3t[:, l, r, :], kq[:, l, r, k, :], start=True, stop=True)
                        last.then_inc(products, 1)
                        pe.wait_ge(links_made, 1)
                        for t in range(NT):
                            last = nc.tensor.transpose(ps_c[:, t * HA:(t + 1) * HA], link_n[:, t * P:(t + 1) * P], ident[0:HA, 0:HA])
                        last.then_inc(links_turned, 1)

                    @block.sync
                    def _(sp):
                        sp.wait_ge(masks_made, 1)
                        sp.dma_start(masks_dram, masks[:, :, :, :].rearrange("p m t c -> p (m t c)")).then_inc(masks_stored, 16)
                        sp.dma_start(row_masks_dram, row_m[:, :, :].rearrange("p m c -> p (m c)")).then_inc(masks_stored, 16)
                        sp.wait_ge(masks_stored, 32)

        sm_masks_in = Counted("masks_loaded")
        sm_turned_in = Counted("scores_turned")
        sm_copied_in = Counted("scores_copied")
        sm_exp_asked = Counted("exps_asked_for")
        sm_exp_made = Counted("exps_made")
        sm_ends_made = Counted("ends_made")
        sm_ends_turned = Counted("ends_turned")
        sm_carry_made = Counted("carries_made")
        sm_carry_turned = Counted("carries_turned")
        sm_out_made = Counted("shares_made")
        sm_turned_out = Counted("shares_turned")
        sm_copied_out = Counted("shares_copied")

        def softmax_phase(SCORE, heads, leaky, with_self):
            phase[0] += 1
            es = ExitStack()
            with es:
                masks = sb("masks", [P, 4, NS], F32, es)
                row_m = sb("row_masks", [HA, 6, NS], F32, es)
                A = sb("scores", [P, heads, NS], F32, es)
                AS = sb("self_scores", [P, heads, NS], F32, es) if with_self else None
                W = sb("running", [P, heads, NS], F32, es)
                B = sb("running_back", [P, heads, NS], F32, es)
                row = sb("row", [heads, NS], F32, es)
                carry = sb("carry", [heads, NS], F32, es)
                ps_t = pb("ps_t", [P, 2, 2 * BANK], F32, es)
                ps_r = pb("ps_r", [P, 2 * BANK], F32, es)
                ps_c = pb("ps_c", [P, BANK], F32, es)
                fields = [(A, h) for h in range(heads)] + [(AS, h) for h in range(heads) if with_self]
                rounds = [(W, C - 1), (B, 0), (W, C - 1), (B, 0)]

                def by_chunk(x):
                    return x[:, :, :].rearrange("p h (t c) -> p h t c", c=C)

                with nc.Block() as block:
                    @block.sync
                    def _(sp):
                        sp.dma_start(masks[:, :, :].rearrange("p m c -> p (m c)"), masks_dram).then_inc(sm_masks_in.sem, 16)
                        sp.dma_start(row_m[:, :, :].rearrange("p m c -> p (m c)"), row_masks_dram).then_inc(sm_masks_in.sem, 16)
                        sp.wait_ge(sm_masks_in.sem, sm_masks_in.at(32))

                    @block.tensor
                    def _(pe):
                        for n in range(len(fields)):
                            if n >= 2:
                                pe.wait_ge(sm_copied_in.sem, sm_copied_in.at(n - 1))
                            for t in range(NT):
                                last = nc.tensor.transpose(ps_t[:, n % 2, t * P:(t + 1) * P], SCORE[:, t * P:(t + 1) * P, n], ident[:, :])
                            last.then_inc(sm_turned_in.sem, 1)
                        for n, (tile, at) in enumerate(rounds):
                            pe.wait_ge(sm_ends_made.sem, sm_ends_made.at(n + 1))
                            for t in range(NT):
                                last = nc.tensor.transpose(ps_r[0:heads, t * P:(t + 1) * P], by_chunk(tile)[:, :, t, at], ident[:, :])
                            last.then_inc(sm_ends_turned.sem, 1)
                            pe.wait_ge(sm_carry_made.sem, sm_carry_made.at(n + 1))
                            for t in range(NT):
                                last = nc.tensor.transpose(ps_c[:, t * heads:(t + 1) * heads], carry[:, t * P:(t + 1) * P],
                                                           ident[0:heads, 0:heads])
                            last.then_inc(sm_carry_turned.sem, 1)
                        pe.wait_ge(sm_out_made.sem, sm_out_made.at(1))
                        for n, (tile, h) in enumerate(fields):
                            if n >= 2:
                                pe.wait_ge(sm_copied_out.sem, sm_copied_out.at(n - 1))
                            for t in range(NT):
                                last = nc.tensor.transpose(ps_t[:, n % 2, t * P:(t + 1) * P], tile[:, h, t * P:(t + 1) * P], ident[:, :])
                            last.then_inc(sm_turned_out.sem, 1)

                    @block.scalar
                    def _(act):
                        for n, (tile, h) in enumerate(fields):
                            act.wait_ge(sm_turned_in.sem, sm_turned_in.at(n + 1))
                            nc.scalar.activation(tile[:, h, :], ps_t[:, n % 2, 0:NS], ACT.Copy).then_inc(sm_copied_in.sem, 1)
                        for n, tile in enumerate((A, AS) if with_self else (A,)):
                            act.wait_ge(sm_exp_asked.sem, sm_exp_asked.at(n + 1))
                            nc.scalar.activation(tile[:, :, :], tile[:, :, :], ACT.Exp).then_inc(sm_exp_made.sem, 1)
                        for n in range(len(fields)):
                            act.wait_ge(sm_turned_out.sem, sm_turned_out.at(n + 1))
                            nc.scalar.activation(SCORE[:, :, n], ps_t[:, n % 2, 0:NS], ACT.Copy).then_inc(sm_copied_out.sem, 1)

                    @block.vector
                    def _(dve):
                        v = nc.vector
                        back = slice(None, None, -1)
                        done = [0]

                        def from_left(out_t, in_t, mask, op0, op1, start):
                            for h in range(heads):
                                last = v.tensor_tensor_scan(out_t[:, h, :], masks[:, mask, :], in_t[:, h, :], start, op0, op1)
                            link(last)

                        def from_right(out_t, in_t):
                            for h in range(heads):
                                last = v.tensor_tensor_scan(out_t[:, h, back], masks[:, PEN_R, back], in_t[:, h, back], FAR, ALU.add, ALU.max)
                            link(last)

                        def carries(to_right, mask, link_mask, op0, op1, start):
                            n = done[0] = done[0] + 1
                            dve.sem_inc(sm_ends_made.sem, 1)
                            dve.wait_ge(sm_ends_turned.sem, sm_ends_turned.at(n))
                            if to_right:
                                link(v.tensor_tensor_scan(row[:, :], row_m[0:heads, mask, :], ps_r[0:heads, 0:NS], start, op0, op1))
                                v.memset(carry[:, 0:1], start)
                                link(v.tensor_tensor(carry[:, 1:NS], row[:, 0:NS - 1], row_m[0:heads, link_mask, 1:NS], op0))
                            else:
                                link(v.tensor_tensor_scan(row[:, back], row_m[0:heads, mask, back], ps_r[0:heads, 0:NS][:, back], start, op0, op1))
                                v.memset(carry[:, NS - 1:NS], start)
                                link(v.tensor_tensor(carry[:, 0:NS - 1], row[:, 1:NS], row_m[0:heads, link_mask, 0:NS - 1], op0))
                            dve.sem_inc(sm_carry_made.sem, 1)
                            dve.wait_ge(sm_carry_turned.sem, sm_carry_turned.at(n))

                        def hand_over(tile, at, op):
                            ends = by_chunk(tile)[:, :, :, at]
                            link(v.tensor_tensor(ends, ends, ps_c[:, 0:NT * heads].rearrange("p (t h) -> p h t", h=heads), op))

                        def spread_back():
                            from_right(B, W)
                            carries(False, ROW_R, LINK_R, ALU.add, ALU.max, FAR)
                            hand_over(W, C - 1, ALU.max)
                            from_right(B, W)

                        dve.wait_ge(sm_copied_in.sem, sm_copied_in.at(len(fields)))
                        dve.wait_ge(sm_masks_in.sem, sm_masks_in.at(32))
                        if leaky:
                            link(v.scalar_tensor_tensor(A[:, :, :], A[:, :, :], SLOPE, A[:, :, :], ALU.mult, ALU.max))
                        from_left(W, A, PEN_L, ALU.add, ALU.max, FAR)
                        carries(True, ROW_L, LINK_L, ALU.add, ALU.max, FAR)
                        link(v.tensor_copy(B[:, :, :], A[:, :, :]))
                        hand_over(B, 0, ALU.max)
                        from_left(W, B, PEN_L, ALU.add, ALU.max, FAR)
                        spread_back()
                        if with_self:
                            link(v.tensor_tensor(B[:, :, :], B[:, :, :], AS[:, :, :], ALU.max))
                        v.tensor_tensor(A[:, :, :], A[:, :, :], B[:, :, :], ALU.subtract).then_inc(sm_exp_asked.sem, 1)
                        if with_self:
                            v.tensor_tensor(AS[:, :, :], AS[:, :, :], B[:, :, :], ALU.subtract).then_inc(sm_exp_asked.sem, 1)
                        dve.wait_ge(sm_exp_made.sem, sm_exp_made.at(1))
                        from_left(W, A, CONT, ALU.mult, ALU.add, 0.0)
                        carries(True, ROW_C, LINK_C, ALU.mult, ALU.add, 0.0)
                        link(v.tensor_copy(B[:, :, :], A[:, :, :]))
                        hand_over(B, 0, ALU.add)
                        from_left(W, B, CONT, ALU.mult, ALU.add, 0.0)
                        spread_back()
                        if with_self:
                            dve.wait_ge(sm_exp_made.sem, sm_exp_made.at(2))
                            link(v.tensor_tensor(B[:, :, :], B[:, :, :], AS[:, :, :], ALU.add))
                        link(v.tensor_scalar(B[:, :, :], B[:, :, :], TINY, None, ALU.add))
                        link(v.reciprocal(B[:, :, :], B[:, :, :]))
                        link(v.tensor_tensor(A[:, :, :], A[:, :, :], B[:, :, :], ALU.mult))
                        if with_self:
                            link(v.tensor_tensor(AS[:, :, :], AS[:, :, :], B[:, :, :], ALU.mult))
                            link(v.tensor_tensor(AS[:, :, :], AS[:, :, :], masks[:, LAST, :].unsqueeze(1).to_broadcast([P, heads, NS]), ALU.mult))
                        dve.sem_inc(sm_out_made.sem, 1)
                sm_masks_in.over(32)
                sm_out_made.over(1)
                for c in (sm_turned_in, sm_copied_in, sm_turned_out, sm_copied_out):
                    c.over(len(fields))
                for c in (sm_exp_asked, sm_exp_made):
                    c.over(2 if with_self else 1)
                for c in (sm_ends_made, sm_ends_turned, sm_carry_made, sm_carry_turned):
                    c.over(len(rounds))

        mult_made = Counted("products_made")
        reduced = Counted("scores_reduced", 4)
        linear_made = Counted("linear_parts_made")

        def turn_onehots(pe, S, ps_T, h):
            for k in range(2):
                for q in range(4):
                    last = nc.tensor.transpose(ps_T[0:BN, k, q, :], S[:, HALF * h + 4 * k + q, :], ident[:, :])
                last.then_inc(turned.sem, 1)

        def copy_turned(act, ST, ps_T, i, h, k):
            act.wait_ge(turned.sem, turned.at(4 * i + 2 * h + k + 1))
            nc.scalar.activation(ST[0:BN, HALF * h + 4 * k:HALF * h + 4 * k + 4, :], ps_T[0:BN, k, :, :], ACT.Copy).then_inc(turned_copied.sem, 1)

        def stash_half(act, G, width, stash, i, h):
            for j in range(HALF * h, HALF * (h + 1)):
                act.wait_ge(gathered[j].sem, gathered[j].at(16 * i + 16))
            act.dma_start(stash[bass.ds(2 * i + h, 1), :, :].rearrange("o p r -> (o p) r"),
                          G[:, HALF * h:HALF * (h + 1), 0:width].rearrange("p c f -> p (c f)")).then_inc(stashed[h].sem, 16)

        def pair_scores(SCORE, XR, l):
            phase[0] += 1
            FA = HA * D
            GW = FA + HA
            PW = FA + 2 * HA
            es = ExitStack()
            with es:
                stage = sb("stage", [P, 2, R, HALF], I32, es)
                stage_f = stage[:, :, :, :].bitcast(F32)
                G = sb("gathered_rows", [P, U, GW], F32, es)
                S = sb("onehots", [P, U, BN], F32, es)
                ST = sb("onehots_turned", [P, U, P], F32, es)
                Z = sb("z", [P, 4, 2, FA], F32, es)
                RED = sb("scores_half", [P, U, 3, HA], F32, es)
                ps_T = pb("ps_T", [P, 2, 4, P], F32, es)
                ps_Z = pb("ps_Z", [P, 2, 2, BANK], F32, es)
                with nc.Block() as block:
                    @block.sync
                    def _(sp):
                        with sp.Fori(0, TURNS) as i:
                            for h in range(2):
                                stage_half(sp, stage, i, h, (stashed[h],))
                        for c in stashed:
                            sp.wait_ge(c.sem, c.at(16 * TURNS))

                    @block.gpsimd
                    def _(pool):
                        gather_loop(pool, stage, G, GW, xl_table, SRC)

                    @block.tensor
                    def _(pe):
                        for c, n in ((chunk_done, U), (z_made, 2), (self_kept, 2), (reduced, 4), (stashed[0], 16), (stashed[1], 16)):
                            nc.tensor.nop().then_inc(c.sem, n)
                        with pe.Fori(0, TURNS) as i:
                            for h in range(2):
                                pe.wait_ge(staged[h].sem, staged[h].at(16 * i + 16))
                                pe.sem_inc(pe_seen, 1)
                                pe.wait_ge(onehot_made.sem, onehot_made.at(2 * i + h + 1))
                                turn_onehots(pe, S, ps_T, h)
                                for q in range(HALF):
                                    j = HALF * h + q
                                    if q % 4 == 0:
                                        at = load_blocks(stage[:, h], q)
                                    if q % 2 == 0:
                                        pair = 8 * i + j // 2
                                        pe.wait_ge(z_made.sem, z_made.at(pair - 1))
                                        pe.wait_ge(self_kept.sem, self_kept.at(pair - 1))
                                    if q % 4 == 0:
                                        pe.wait_ge(turned_copied.sem, turned_copied.at(4 * i + 2 * h + q // 4 + 1))
                                    last = nc.tensor.matmul(ps_Z[:, (j // 2) % 2, j % 2, 0:PW], ST[0:BN, j, :],
                                                            XR[:, bass.ds(at[q % 4] * PW, PW)], start=True, stop=True)
                                    if q % 2:
                                        last.then_inc(dest_made.sem, 1)

                    @block.scalar
                    def _(act):
                        with act.Fori(0, TURNS) as i:
                            for h in range(2):
                                def keep_self(p):
                                    act.wait_ge(dest_made.sem, dest_made.at(8 * i + 4 * h + p + 1))
                                    j = HALF * h + 2 * p
                                    nc.scalar.activation(RED[:, j:j + 2, 1:3, :], ps_Z[:, p % 2, :, FA:PW].rearrange("p c (k h) -> p c k h", h=HA), ACT.Copy).then_inc(self_kept.sem, 1)

                                def leaky(p):
                                    act.wait_ge(z_made.sem, z_made.at(8 * i + 4 * h + p + 1))
                                    nc.scalar.activation(Z[:, p, :, :], Z[:, p, :, :], ACT.Relu, scale=1.0 - SLOPE).then_inc(leaky_made.sem, 1)

                                copy_turned(act, ST, ps_T, i, h, 0)
                                copy_turned(act, ST, ps_T, i, h, 1)
                                keep_self(0)
                                for p in range(4):
                                    if p < 3:
                                        keep_self(p + 1)
                                    leaky(p)
                                stash_half(act, G, GW, stash_a, i, h)

                    @block.vector
                    def _(dve):
                        v = nc.vector
                        link(v.memset(SCORE[:, NCH:NS, :], 0.0))
                        with dve.Fori(0, TURNS) as i:
                            for h in range(2):
                                dve.wait_ge(staged[h].sem, staged[h].at(16 * i + 16))
                                make_onehots(dve, stage_f, S, h).then_inc(onehot_made.sem, 1)

                                def add(p):
                                    j = HALF * h + 2 * p
                                    for k in (j, j + 1):
                                        dve.wait_ge(gathered[k].sem, gathered[k].at(16 * i + 16))
                                    dve.wait_ge(reduced.sem, reduced.at(8 * i + 4 * h + p - 3))
                                    dve.wait_ge(self_kept.sem, self_kept.at(8 * i + 4 * h + p + 1))
                                    v.tensor_tensor(Z[:, p, :, :], G[:, j:j + 2, 0:FA], ps_Z[:, p % 2, :, 0:FA], ALU.add).then_inc(z_made.sem, 1)

                                def score(p):
                                    j = HALF * h + 2 * p
                                    dve.wait_ge(leaky_made.sem, leaky_made.at(8 * i + 4 * h + p + 1))
                                    v.tensor_tensor(Z[:, p, :, :], Z[:, p, :, :],
                                                    att_bc[:, l, :].unsqueeze(1).to_broadcast([P, 2, FA]), ALU.mult).then_inc(mult_made.sem, 1)
                                    dve.wait_ge(mult_made.sem, mult_made.at(8 * i + 4 * h + p + 1))
                                    v.tensor_reduce(RED[:, j:j + 2, 0, :], Z[:, p, :, :].rearrange("p c (h f) -> p c h f", f=D), AX, ALU.add).then_inc(reduced.sem, 1)

                                add(0)
                                for p in range(1, 4):
                                    add(p)
                                    score(p - 1)
                                score(3)
                                dve.wait_ge(self_kept.sem, self_kept.at(8 * i + 4 * h + 4))
                                half = slice(HALF * h, HALF * (h + 1))
                                v.tensor_tensor(RED[:, half, 1, :], RED[:, half, 1, :], G[:, half, FA:GW], ALU.add).then_inc(linear_made.sem, 1)
                                v.tensor_scalar(SCORE[:, bass.ds(i * U + HALF * h, HALF), HA:2 * HA], RED[:, half, 2, :], 1.0, None, ALU.mult)
                                dve.wait_ge(reduced.sem, reduced.at(8 * i + 4 * h + 4))
                                dve.wait_ge(linear_made.sem, linear_made.at(2 * i + h + 1))
                                v.tensor_tensor(SCORE[:, bass.ds(i * U + HALF * h, HALF), 0:HA], RED[:, half, 0, :], RED[:, half, 1, :],
                                                ALU.add).then_inc(chunk_done.sem, HALF)
                for c in (*staged, *gathered, *stashed):
                    c.over(16 * TURNS)
                for c, n in ((onehot_made, 2 * TURNS), (chunk_done, NCH), (turned, 4 * TURNS), (turned_copied, 4 * TURNS), (dest_made, NCH // 2),
                             (z_made, NCH // 2), (self_kept, NCH // 2), (leaky_made, NCH // 2), (mult_made, NCH // 2), (reduced, NCH // 2),
                             (linear_made, 2 * TURNS)):
                    c.over(n)

        def relation_scores(SCORE, XQ):
            phase[0] += 1
            FR = D + HR
            es = ExitStack()
            with es:
                stage = sb("stage", [P, 2, R, HALF], I32, es)
                stage_f = stage[:, :, :, :].bitcast(F32)
                G = sb("gathered_rows", [P, U, FR], F32, es)
                S = sb("onehots", [P, U, BN], F32, es)
                ST = sb("onehots_turned", [P, U, P], F32, es)
                T1 = sb("onehots_type", [P, 2, HALF, R], F32, es)
                PQ = sb("picked", [P, 2, HALF, R, HR], F32, es)
                RED = sb("query_scores", [P, 2, HALF, HR], F32, es)
                ps_T = pb("ps_T", [P, 2, 4, P], F32, es)
                ps_Q = pb("ps_Q", [P, 2, BANK], F32, es)
                with nc.Block() as block:
                    @block.sync
                    def _(sp):
                        with sp.Fori(0, TURNS) as i:
                            for h in range(2):
                                stage_half(sp, stage, i, h, (stashed[h],))
                        for c in stashed:
                            sp.wait_ge(c.sem, c.at(16 * TURNS))

                    @block.gpsimd
                    def _(pool):
                        gather_loop(pool, stage, G, FR, rel_table, SRC_TYPE)

                    @block.tensor
                    def _(pe):
                        for c, n in ((chunk_done, U), (reduced, 4), (stashed[0], 16), (stashed[1], 16)):
                            nc.tensor.nop().then_inc(c.sem, n)
                        with pe.Fori(0, TURNS) as i:
                            for h in range(2):
                                pe.wait_ge(staged[h].sem, staged[h].at(16 * i + 16))
                                pe.sem_inc(pe_seen, 1)
                                pe.wait_ge(onehot_made.sem, onehot_made.at(2 * i + h + 1))
                                turn_onehots(pe, S, ps_T, h)
                                for q in range(HALF):
                                    j = HALF * h + q
                                    if q % 4 == 0:
                                        at = load_blocks(stage[:, h], q)
                                    if q % 4 == 0:
                                        pe.wait_ge(turned_copied.sem, turned_copied.at(4 * i + 2 * h + q // 4 + 1))
                                    last = nc.tensor.matmul(ps_Q[:, h, q * R * HR:(q + 1) * R * HR], ST[0:BN, j, :],
                                                            XQ[:, bass.ds(at[q % 4] * (R * HR), R * HR)], start=True, stop=True)
                                last.then_inc(dest_made.sem, 1)

                    @block.scalar
                    def _(act):
                        with act.Fori(0, TURNS) as i:
                            for h in range(2):
                                copy_turned(act, ST, ps_T, i, h, 0)
                                copy_turned(act, ST, ps_T, i, h, 1)
                                stash_half(act, G, FR, stash_r, i, h)

                    @block.vector
                    def _(dve):
                        v = nc.vector
                        link(v.memset(SCORE[:, NCH:NS, :], 0.0))
                        with dve.Fori(0, TURNS) as i:
                            for h in range(2):
                                dve.wait_ge(staged[h].sem, staged[h].at(16 * i + 16))
                                make_onehots(dve, stage_f, S, h).then_inc(onehot_made.sem, 1)
                                v.tensor_tensor(T1[:, h, :, :], pos[:, 0:R].unsqueeze(1).to_broadcast([P, HALF, R]),
                                                stage_f[:, h, TYPE, :].unsqueeze(2).to_broadcast([P, HALF, R]), ALU.is_equal).then_inc(leaky_made.sem, 1)
                                dve.wait_ge(leaky_made.sem, leaky_made.at(2 * i + h + 1))
                                dve.wait_ge(dest_made.sem, dest_made.at(2 * i + h + 1))
                                v.tensor_tensor(PQ[:, h, :, :, :], ps_Q[:, h, 0:HALF * R * HR].rearrange("p (c r h) -> p c r h", r=R, h=HR),
                                                T1[:, h, :, :].unsqueeze(3).to_broadcast([P, HALF, R, HR]), ALU.mult).then_inc(mult_made.sem, 1)
                                dve.wait_ge(mult_made.sem, mult_made.at(2 * i + h + 1))
                                v.tensor_reduce(RED[:, h, :, :], PQ[:, h, :, :, :].rearrange("p c r h -> p c h r"), AX, ALU.add).then_inc(reduced.sem, 1)
                                for j in range(HALF * h, HALF * (h + 1)):
                                    dve.wait_ge(gathered[j].sem, gathered[j].at(16 * i + 16))
                                dve.wait_ge(reduced.sem, reduced.at(2 * i + h + 1))
                                v.tensor_tensor(SCORE[:, bass.ds(i * U + HALF * h, HALF), :], RED[:, h, :, :],
                                                G[:, HALF * h:HALF * (h + 1), D:FR], ALU.add).then_inc(chunk_done.sem, HALF)
                for c in (*staged, *gathered, *stashed):
                    c.over(16 * TURNS)
                for c, n in ((onehot_made, 2 * TURNS), (chunk_done, NCH), (turned, 4 * TURNS), (turned_copied, 4 * TURNS), (dest_made, 2 * TURNS),
                             (leaky_made, 2 * TURNS), (mult_made, 2 * TURNS), (reduced, 2 * TURNS)):
                    c.over(n)

        def shared_sums(SUM, SCORE, heads, width, stash, with_self):
            phase[0] += 1
            out_w = D + (heads if with_self else 0)
            es = ExitStack()
            with es:
                stage = sb("stage", [P, 2, R, HALF], I32, es)
                stage_f = stage[:, :, :, :].bitcast(F32)
                G = sb("kept_rows", [P, U, width], F32, es)
                S = sb("onehots", [P, U, BN], F32, es)
                M = sb("messages", [P, U, out_w], F32, es)
                PR = sb("products", [P, 2, HALF, heads, D], F32, es) if with_self else None
                zero = sb("zero_bank", [P, BANK], F32, es)
                ps_sum = pb("ps_sum", [P, 7 * BANK], F32, es)
                ready, finished = (once(x) for x in ("set_up", "loop_over"))
                with nc.Block() as block:
                    @block.sync
                    def _(sp):
                        with sp.Fori(0, TURNS) as i:
                            for h in range(2):
                                stage_half(sp, stage, i, h)
                                sp.dma_start(G[:, HALF * h:HALF * (h + 1), :].rearrange("p c f -> p (c f)"),
                                             stash[bass.ds(2 * i + h, 1), :, :].rearrange("o p r -> (o p) r")).then_inc(loaded[h].sem, 16)

                    @block.vector
                    def _(dve):
                        v = nc.vector
                        v.memset(zero[:, :], 0.0).then_inc(ready, 1)
                        with dve.Fori(0, TURNS) as i:
                            for h in range(2):
                                half = slice(HALF * h, HALF * (h + 1))
                                share = SCORE[:, bass.ds(i * U + HALF * h, HALF), :]
                                dve.wait_ge(staged[h].sem, staged[h].at(16 * i + 16))
                                make_onehots(dve, stage_f, S, h).then_inc(onehot_made.sem, 1)
                                dve.wait_ge(loaded[h].sem, loaded[h].at(16 * i + 16))
                                if with_self:
                                    v.tensor_tensor(PR[:, h, :, :, :], G[:, half, 0:heads * D].rearrange("p c (h f) -> p c h f", f=D),
                                                    share[:, :, 0:heads].unsqueeze(3).to_broadcast([P, HALF, heads, D]), ALU.mult).then_inc(mult_made.sem, 1)
                                    v.tensor_scalar(M[:, half, D:out_w], share[:, :, heads:2 * heads], 1.0, None, ALU.mult)
                                    dve.wait_ge(mult_made.sem, mult_made.at(2 * i + h + 1))
                                    v.tensor_reduce(M[:, half, 0:D], PR[:, h, :, :, :].rearrange("p c h f -> p c f h"), AX, ALU.add).then_inc(msg_made.sem, 1)
                                else:
                                    v.tensor_tensor(M[:, half, :].rearrange("p c (h f) -> p c h f", h=heads),
                                                    G[:, half, 0:D].rearrange("p c (h f) -> p c h f", h=heads),
                                                    share.unsqueeze(3).to_broadcast([P, HALF, heads, D // heads]), ALU.mult).then_inc(msg_made.sem, 1)
                        dve.wait_ge(finished, 1)
                        link(v.tensor_copy(SUM[:, :, :], sums(ps_sum, out_w)))

                    @block.tensor
                    def _(pe):
                        nc.tensor.nop().then_inc(chunk_done.sem, U)
                        pe.wait_ge(ready, 1)
                        zero_sums(ps_sum, zero, 7)
                        with pe.Fori(0, TURNS) as i:
                            for h in range(2):
                                pe.wait_ge(staged[h].sem, staged[h].at(16 * i + 16))
                                pe.sem_inc(pe_seen, 1)
                                for q in range(HALF):
                                    j = HALF * h + q
                                    if q % 4 == 0:
                                        at = load_blocks(stage[:, h], q)
                                    if q == 0:
                                        pe.wait_ge(onehot_made.sem, onehot_made.at(2 * i + h + 1))
                                        pe.wait_ge(msg_made.sem, msg_made.at(2 * i + h + 1))
                                    sum_chunk(ps_sum, S, j, M[:, j, :], out_w, at[q % 4]).then_inc(chunk_done.sem, 1)
                        nc.tensor.matmul(ps_sum[:, 6 * BANK + 3 * P:7 * BANK], zero[:, 0:P], zero[:, 0:P], start=False, stop=True,
                                         skip_group_check=True).then_inc(finished, 1)
                for c in (*staged, *loaded):
                    c.over(16 * TURNS)
                for c, n in ((onehot_made, 2 * TURNS), (msg_made, 2 * TURNS), (chunk_done, NCH)):
                    c.over(n)
                if with_self:
                    mult_made.over(2 * TURNS)

        segments_phase()

        norm_phase()
        for l in range(2):
            FA = HA * D
            GW = FA + HA
            PW = FA + 2 * HA
            ls = ExitStack()
            with ls:
                phase[0] += 1
                SCORE = sb("score", [P, NS, 2 * HA], F32, ls)
                xs = ExitStack()
                with xs:
                    XR = sb("xr", [BN, NB * PW], F32, xs)
                    XRv = XR[:, :].rearrange("p (b f) -> p b f", f=PW)
                    xt = ExitStack()
                    with xt:
                        XL = sb("xl", [BN, NB, GW], F32, xt)
                        TMP = sb("own_z", [BN, NB // 5, FA], F32, xt)
                        xl_stored = once("xl_stored")
                        xl_made = once("xl_made")

                        def take(dve, b, ps, l=l, XL=XL, XRv=XRv):
                            nc.vector.tensor_tensor(XL[:, b, 0:FA], ps[:, 0, 0:FA], bc_big[:, 2 * l, :], ALU.add)
                            return nc.vector.tensor_tensor(XRv[:, b, 0:FA], ps[:, 1, 0:FA], bc_big[:, 2 * l + 1, :], ALU.add)

                        def after(dve, l=l, XL=XL, XRv=XRv, TMP=TMP, xl_made=xl_made):
                            v = nc.vector
                            n = NB // 5
                            for g in range(5):
                                bs = slice(g * n, (g + 1) * n)
                                for rows_of in (XL, XRv):
                                    link(v.tensor_tensor(TMP[:, :, :], rows_of[:, bs, 0:FA], att_bc[0:BN, l, :].unsqueeze(1).to_broadcast([BN, n, FA]), ALU.mult))
                                    link(v.tensor_reduce(rows_of[:, bs, FA:GW], TMP[:, :, :].rearrange("p b (h f) -> p b h f", f=D), AX, ALU.add))
                                    link(v.tensor_scalar(rows_of[:, bs, FA:GW], rows_of[:, bs, FA:GW], SLOPE, None, ALU.mult))
                                link(v.tensor_tensor(TMP[:, :, :], XL[:, bs, 0:FA], XRv[:, bs, 0:FA], ALU.add))
                                link(v.scalar_tensor_tensor(TMP[:, :, :], TMP[:, :, :], SLOPE, TMP[:, :, :], ALU.mult, ALU.max))
                                link(v.tensor_tensor(TMP[:, :, :], TMP[:, :, :], att_bc[0:BN, l, :].unsqueeze(1).to_broadcast([BN, n, FA]), ALU.mult))
                                link(v.tensor_reduce(XRv[:, bs, GW:PW], TMP[:, :, :].rearrange("p b (h f) -> p b h f", f=D), AX, ALU.add))
                            dve.sem_inc(xl_made, 1)

                        def store(sp, XL=XL, xl_made=xl_made, xl_stored=xl_stored):
                            sp.wait_ge(xl_made, 1)
                            sp.dma_start(xl_table.rearrange("(b p) f -> p b f", p=BN), XL[:, :, :]).then_inc(xl_stored, 16)
                            sp.wait_ge(xl_stored, 16)

                        dense(H[:, :, :], D, [w2[:, 2 * l, :], w2[:, 2 * l + 1, :]], take, None, after, store)
                    pair_scores(SCORE, XR, l)
                softmax_phase(SCORE, HA, False, True)
                SUM = sb("sums", [BN, NB, D + HA], F32, ls)
                shared_sums(SUM, SCORE, HA, GW, stash_a, True)
                phase[0] += 1
                xt = ExitStack()
                with xt:
                    XL = sb("xl_again", [BN, NB, GW], F32, xt)
                    lone = sb("lone", [BN, NB], F32, xt)
                    own = sb("own", [BN, NB, D], F32, xt)
                    xl_back = once("xl_back")
                    with nc.Block() as block:
                        @block.sync
                        def _(sp):
                            sp.dma_start(XL[:, :, :], xl_table.rearrange("(b p) f -> p b f", p=BN)).then_inc(xl_back, 16)

                        @block.vector
                        def _(dve):
                            v = nc.vector
                            link(v.tensor_scalar(lone[:, :], deg_in[:, :], 0.0, None, ALU.is_equal))
                            link(v.tensor_tensor(SUM[:, :, D:], SUM[:, :, D:], lone[:, :].unsqueeze(2).to_broadcast([BN, NB, HA]), ALU.add))
                            dve.wait_ge(xl_back, 16)
                            link(v.tensor_tensor(XL[:, :, 0:FA].rearrange("p b (h f) -> p b h f", f=D), XL[:, :, 0:FA].rearrange("p b (h f) -> p b h f", f=D),
                                                 SUM[:, :, D:].unsqueeze(3).to_broadcast([BN, NB, HA, D]), ALU.mult))
                            link(v.tensor_reduce(own[:, :, :], XL[:, :, 0:FA].rearrange("p b (h f) -> p b f h", f=D), AX, ALU.add))
                            link(v.tensor_tensor(own[:, :, :], own[:, :, :], SUM[:, :, 0:D], ALU.add))
                            link(v.tensor_scalar(own[:, :, :], own[:, :, :], 1.0 / HA, None, ALU.mult))
                            link(v.tensor_tensor(own[:, :, :], own[:, :, :], bcn(bc_n[:, 4 + l, :]), ALU.add))
                            link(v.tensor_scalar(H[:, :, :], own[:, :, :], 0.0, None, ALU.max))

        AGG_s = ExitStack()
        with AGG_s:
            def take(dve, b, ps):
                v = nc.vector
                return v.tensor_tensor(H[:, b, :], ps[:, 0, 0:D], bc_n[:, 6, :], ALU.add)

            def after(dve):
                link(nc.vector.tensor_tensor(X[:, :, :], X[:, :, :], H[:, :, :], ALU.add))

            dense(H[:, :, :], D, [wfc[:, :]], take, None, after)

        norm_phase()
        for l in range(2):
            FR = D + HR
            ls = ExitStack()
            with ls:
                phase[0] += 1
                SCORE = sb("score", [P, NS, HR], F32, ls)
                xs = ExitStack()
                with xs:
                    XQ = sb("queries", [BN, NB * R * HR], F32, xs)
                    XQv = XQ[:, :].rearrange("p (b f) -> p b f", b=NB)
                    xt = ExitStack()
                    with xt:
                        T3 = sb("rel_rows", [BN, NB, R, FR], F32, xt)
                        rel_made = once("rel_made")
                        rel_stored = once("rel_stored")

                        def take(dve, b, ps, T3=T3, XQv=XQv):
                            v = nc.vector
                            v.tensor_copy(T3[:, b, :, 0:D], ps[:, 0, :].rearrange("p (r f) -> p r f", f=D))
                            v.tensor_copy(T3[:, b, :, D:FR], ps[:, 1, 0:R * HR].rearrange("p (r h) -> p r h", h=HR))
                            return v.tensor_copy(XQv[:, b, :], ps[:, 1, R * HR:2 * R * HR])

                        def after(dve, rel_made=rel_made):
                            dve.sem_inc(rel_made, 1)

                        def store(sp, T3=T3, rel_made=rel_made, rel_stored=rel_stored):
                            sp.wait_ge(rel_made, 1)
                            sp.dma_start(rel_table.rearrange("(b p r) w -> p b (r w)", p=BN, r=R),
                                         T3[:, :, :, :].rearrange("p b r w -> p b (r w)")).then_inc(rel_stored, 16)
                            sp.wait_ge(rel_stored, 16)

                        dense(H[:, :, :], D, [w3[:, l, :, :].rearrange("p r f -> p (r f)"), wkq[:, l, :, :, :].rearrange("p k r h -> p (k r h)")],
                              take, None, after, store)
                    relation_scores(SCORE, XQ)
                softmax_phase(SCORE, HR, True, False)
                SUM = sb("sums", [BN, NB, D], F32, ls)
                shared_sums(SUM, SCORE, HR, FR, stash_r, False)
                with nc.Block() as block:
                    @block.vector
                    def _(dve):
                        v = nc.vector
                        link(v.tensor_tensor(H[:, :, :], SUM[:, :, :], bcn(bc_n[:, 7 + l, :]), ALU.add))
                        if l == 0:
                            link(v.tensor_scalar(H[:, :, :], H[:, :, :], 0.0, None, ALU.max))
                        else:
                            link(v.tensor_tensor(X[:, :, :], X[:, :, :], H[:, :, :], ALU.add))

        s_out = sem("out_stored")
        with nc.Block() as block:
            @block.sync
            def _(sp):
                sp.dma_start(out.rearrange("(b p) f -> p b f", p=BN), X[:, :, :]).then_inc(s_out, 16)
                sp.wait_ge(s_out, 16)


_INS = ['x', 'src', 'dst', 'edge_attr_64', 'edge_attr_64_n2', 'edge_type_8', 'edge_weight', 'L0_gnn_W_self', 'L0_gnn_W_neigh', 'L0_gnn_b_neigh', 'L1_gnn_a_mu0', 'L1_gnn_a_ls0', 'L1_gnn_a_mu1', 'L1_gnn_a_ls1', 'L1_gnn_W0', 'L1_gnn_b0', 'L1_gnn_W1', 'L1_gnn_b1', 'L2_gnn_W1l', 'L2_gnn_b1l', 'L2_gnn_W1r', 'L2_gnn_b1r', 'L2_gnn_att1', 'L2_gnn_bias1', 'L2_gnn_W2l', 'L2_gnn_b2l', 'L2_gnn_W2r', 'L2_gnn_b2r', 'L2_gnn_att2', 'L2_gnn_bias2', 'L2_gnn_Wfc', 'L2_gnn_bfc', 'L3_gnn_W1', 'L3_gnn_Q1', 'L3_gnn_K1', 'L3_gnn_b1', 'L3_gnn_W2', 'L3_gnn_Q2', 'L3_gnn_K2', 'L3_gnn_b2']
_TURNED = ('L0_gnn_W_self', 'L0_gnn_W_neigh', 'L3_gnn_W1', 'L3_gnn_W2')


def kernel(**inputs):
    import numpy as _np
    import concourse.bacc as _bacc
    from concourse import mybir as _mybir
    from concourse.bass_utils import run_bass_kernel_spmd as _run

    nc = _bacc.Bacc("TRN2", target_bir_lowering=False, num_devices=1)
    arrays, io = {}, {}

    def give(name, a):
        a = _np.ascontiguousarray(a)
        arrays[f"in_{name}_dram"] = a
        io[name] = nc.dram_tensor(f"in_{name}_dram", a.shape, _mybir.dt.from_np(a.dtype), kind="ExternalInput").ap()

    for name in _INS:
        a = _np.asarray(inputs[name])
        if name.startswith("edge_attr"):
            a = _np.concatenate([a, _np.zeros((C, D), a.dtype)])
        give(name, a)
        if name in _TURNED:
            give(name + "_T", _np.swapaxes(_np.asarray(inputs[name]), -1, -2))
    out = nc.dram_tensor("out_0_dram", (N, D), F32, kind="ExternalOutput").ap()
    build(nc, io, out)
    r = _run(nc, [arrays], core_ids=[0])
    return r.results[0]["out_0_dram"]
```

```python
import concourse.bass as bass
from concourse import mybir
from concourse.alu_op_type import AluOpType as ALU
from contextlib import ExitStack

F32 = mybir.dt.float32
BF16 = mybir.dt.bfloat16
I32 = mybir.dt.int32
ACT = mybir.ActivationFunctionType
AX = mybir.AxisListType.X

P = 128
N = 3125
E = 103125
D = 64
BN = 125
NB = N // BN
C = 128
NCH = 832
NT = 7
NS = NT * P
EP = 125
HALF = 8
U = 2 * HALF
TURNS = NCH // U
NG = NS // HALF
MROWS = E // C + 2
BANK = 512
R = 8
HA = 5
HR = 4
DR = D // HR
EPS = 1e-5
TINY = 1e-16
SLOPE = 0.2
FAR = -1e30
SRC, SRC_TYPE, BLOCK, DLOC, WEIGHT, SRC_LO, SRC_HI, TYPE = range(8)
assert NCH * C >= E + NB * C and NCH % U == 0 and NS >= NCH


def build(nc, io, out):
    ctx = ExitStack()
    with ctx:
        phase = [0]

        def sb(name, shape, dt=F32, stack=ctx):
            return stack.enter_context(nc.sbuf_tensor(f"{name}_{phase[0]}", shape, dt))

        def pb(name, shape, dt=F32, stack=ctx):
            return stack.enter_context(nc.psum_tensor(f"{name}_{phase[0]}", shape, dt))

        def sem(name):
            return ctx.enter_context(nc.semaphore(name))

        meta = nc.dram_tensor("meta", [MROWS, 4, C], I32, kind="Internal").ap()
        chunk_row_dram = nc.dram_tensor("chunk_rows", [2, NS], I32, kind="Internal").ap()
        hist_dram = nc.dram_tensor("hist", [NB * C], F32, kind="Internal").ap()
        slots = nc.dram_tensor("slots", [NG, P, R * HALF], I32, kind="Internal").ap()
        node_table = nc.dram_tensor("node_table", [N, D], F32, kind="Internal").ap()
        xl_table = nc.dram_tensor("xl_table", [N, HA * D + HA], F32, kind="Internal").ap()
        rel_table = nc.dram_tensor("rel_table", [N * R, D + HR], F32, kind="Internal").ap()
        turned_dram = nc.dram_tensor("onehots_turned", [NG, BN, HALF * P], BF16, kind="Internal").ap()
        stash_a = nc.dram_tensor("stash_a", [NG, P, HALF * (HA * D + HA)], F32, kind="Internal").ap()
        stash_r = nc.dram_tensor("stash_r", [NG, P, HALF * (D + HR)], F32, kind="Internal").ap()

        X = sb("X", [BN, NB, D])
        H = sb("H", [BN, NB, D])
        ident = sb("ident", [P, P])
        ident_b = sb("ident_b", [P, P], BF16)
        ones = sb("ones", [P, P])
        pos = sb("pos", [P, P])
        part = sb("part", [P, 1])
        key = sb("key", [P, NT, C])
        dloc = sb("dloc", [P, NS])
        rows = sb("rows", [1, 2, NS], I32)
        bc_n = sb("bc_n", [BN, 9, D])
        bc_big = sb("bc_big", [BN, 4, HA * D])
        att_bc = sb("att_bc", [P, 2, HA * D])
        e_ls = sb("e_ls", [BN, 4, D])
        w0 = sb("w0", [P, 2, D])
        w1 = sb("w1", [D, 2, D])
        w2 = sb("w2", [D, 4, HA * D])
        wfc = sb("wfc", [D, D])
        w3 = sb("w3", [D, 2, R, D])
        w3t = sb("w3t", [D, 2, R, D])
        kq = sb("kq", [D, 2, R, 2, HR])
        wkq = sb("wkq", [D, 2, 2, R, HR])
        deg_in = sb("deg_in", [BN, NB])
        deg_out = sb("deg_out", [BN, NB])

        dve_step = sem("dve_step")
        steps = [0]

        def link(ins):
            steps[0] += 1
            ins.then_inc(dve_step, 1)
            nc.vector.wait_ge(dve_step, steps[0])

        s_const = sem("constants_made")
        s_dst = sem("dst_loaded")
        s_meta = sem("meta_packed")
        s_zero = sem("zeros_made")
        s_tail = sem("meta_tail_zeroed")
        s_cnt = sem("counts_made")
        s_sum = sem("counts_summed")
        s_idx = sem("row_indices_made")
        s_rowsT = sem("chunk_rows_turned")
        s_rowsC = sem("chunk_rows_copied")
        s_rowsD = sem("chunk_rows_in_dram")
        s_rowsS = sem("chunk_rows_loaded")
        s_got = sem("meta_gathered")
        s_slotT = sem("slots_turned")
        s_slotA = sem("slots_arranged")
        s_slotC = sem("slots_copied")
        s_slotD = sem("slots_in_dram")
        s_x = sem("x_loaded")

        st = ExitStack()
        with st:
            NREC = 8
            dst_l = sb("dst_l", [EP, E // EP], I32, st)
            dst_f = sb("dst_f", [EP, E // EP], F32, st)
            cmp_l = sb("cmp_l", [EP, E // EP], F32, st)
            zrow = sb("zrow", [2, 4, C], I32, st)
            cnt = sb("cnt", [EP, NB + 1], F32, st)
            first = sb("first", [P, NB + 1], F32, st)
            nb = sb("nb", [P, NB], F32, st)
            t_f = sb("t_f", [P, NB], F32, st)
            t_i = sb("t_i", [P, NB], I32, st)
            t_j = sb("t_j", [P, NB], I32, st)
            nch = sb("nch", [P, NB], F32, st)
            cs = sb("cs", [P, NB], F32, st)
            pad = sb("pad", [P, NB], F32, st)
            dpad = sb("dpad", [P, NB], F32, st)
            cid = sb("cid", [P, NT], F32, st)
            cmp = sb("cmp", [P, NT, NB], F32, st)
            prod = sb("prod", [P, NT, NB], F32, st)
            be = sb("be", [P, 2, NT], F32, st)
            padc = sb("padc", [P, NT], F32, st)
            endc = sb("endc", [P, NT], F32, st)
            nv = sb("nv", [P, NT], F32, st)
            e0c = sb("e0c", [P, NT], F32, st)
            e0i = sb("e0i", [P, NT], I32, st)
            ridx = sb("ridx", [P, 2, NT], I32, st)
            off = sb("off", [P, NT], I32, st)
            bit_i = sb("bit_i", [P, NT], I32, st)
            bit = sb("bit", [P, 7, NT], F32, st)
            nbit = sb("nbit", [P, 7, NT], F32, st)
            base = sb("base", [P, NT], F32, st)
            rows7 = sb("rows7", [NT, 2, C], I32, st)
            got = sb("got", [P, NT, 2, 4, C], I32, st)
            wa = sb("wa", [P, NT, 4, 2 * C], F32, st)
            wb = sb("wb", [P, NT, 4, 2 * C], F32, st)
            fin = wa[:, :, :, :].rearrange("p t a k -> p (t a k)").rearrange("p (r t c) -> p r t c", r=NREC, t=NT)
            rec = got[:, :, :, :, :].rearrange("p t h a k -> p (t h a k)").rearrange("p (g r e) -> p g r e", g=NG, r=NREC)
            valid = sb("valid", [P, NT, C], F32, st)
            src_c = sb("src_c", [P, NT, C], I32, st)
            lo_i = sb("lo_i", [P, NT, C], I32, st)
            ps_cnt = pb("ps_cnt", [P, BANK], F32, st)
            ps_row = pb("ps_row", [P, BANK], F32, st)
            ps_turn = pb("ps_turn", [P, 2, 2 * BANK], F32, st)

            with nc.Block() as block:
                @block.sync
                def _(sp):
                    sp.dma_start(dst_l[:, :], io["dst"].rearrange("(p k) -> p k", p=EP)).then_inc(s_dst, 16)
                    full = (MROWS - 2) * C
                    for a, name in enumerate(("src", "dst", "edge_type_8", "edge_weight")):
                        v = io[name]
                        if name == "edge_weight":
                            v = v.bitcast(I32)
                        sp.dma_start(meta[0:MROWS - 2, a, :], v[0:full].rearrange("(r k) -> r k", k=C)).then_inc(s_meta, 16)
                        sp.dma_start(meta[MROWS - 2:MROWS - 1, a, 0:E - full],
                                     v[full:E].rearrange("(r k) -> r k", r=1)).then_inc(s_meta, 16)
                    for n, name in enumerate(("L0_gnn_b_neigh", "L1_gnn_b0", "L1_gnn_b1", "L2_gnn_bias1", "L2_gnn_bias2", "L2_gnn_bfc", "L3_gnn_b1", "L3_gnn_b2")):
                        for k in range(2 if n == 0 else 1):
                            v = io[name][k] if n == 0 else io[name]
                            sp.dma_start(bc_n[:, n + (k if n == 0 else 1), :], v.partition_broadcast(BN)).then_inc(s_x, 16)
                    for n, name in enumerate(("L1_gnn_a_mu0", "L1_gnn_a_ls0", "L1_gnn_a_mu1", "L1_gnn_a_ls1")):
                        sp.dma_start(e_ls[:, n, :], io[name].partition_broadcast(BN)).then_inc(s_x, 16)
                    for n, name in enumerate(("L2_gnn_b1l", "L2_gnn_b1r", "L2_gnn_b2l", "L2_gnn_b2r")):
                        sp.dma_start(bc_big[:, n, :], io[name].partition_broadcast(BN)).then_inc(s_x, 16)
                    for n, name in enumerate(("L2_gnn_W1l", "L2_gnn_W1r", "L2_gnn_W2l", "L2_gnn_W2r")):
                        sp.dma_start(w2[:, n, :], io[name]).then_inc(s_x, 16)
                    for n in range(2):
                        sp.dma_start(att_bc[:, n, :], io[f"L2_gnn_att{n + 1}"].rearrange("h f -> (h f)").partition_broadcast(P)).then_inc(s_x, 16)
                        sp.dma_start(w0[0:D, n, :], io["L0_gnn_W_self_T"][n]).then_inc(s_x, 16)
                        sp.dma_start(w0[D:P, n, :], io["L0_gnn_W_neigh_T"][n]).then_inc(s_x, 16)
                        sp.dma_start(w1[:, n, :], io[f"L1_gnn_W{n}"]).then_inc(s_x, 16)
                        sp.dma_start(w3[:, n, :, :], io[f"L3_gnn_W{n + 1}"].rearrange("r i o -> i r o")).then_inc(s_x, 16)
                        sp.dma_start(w3t[:, n, :, :], io[f"L3_gnn_W{n + 1}_T"].rearrange("r i o -> i r o")).then_inc(s_x, 16)
                        sp.dma_start(kq[:, n, :, 0, :], io[f"L3_gnn_K{n + 1}"].rearrange("r i o -> i r o")).then_inc(s_x, 16)
                        sp.dma_start(kq[:, n, :, 1, :], io[f"L3_gnn_Q{n + 1}"].rearrange("r i o -> i r o")).then_inc(s_x, 16)
                    sp.dma_start(wfc[:, :], io["L2_gnn_Wfc"]).then_inc(s_x, 16)
                    sp.dma_start(X[:, :, :], io["x"].rearrange("(b p) f -> p b f", p=BN)).then_inc(s_x, 16)
                    sp.wait_ge(s_zero, 1)
                    sp.dma_start(meta[MROWS - 2:MROWS - 1, :, E - full:C],
                                 zrow[0:1, :, E - full:C]).then_inc(s_tail, 16)
                    sp.dma_start(meta[MROWS - 1:MROWS, :, :], zrow[1:2, :, :]).then_inc(s_tail, 16)
                    sp.wait_ge(s_rowsC, 1)
                    for k in range(2):
                        sp.dma_start(chunk_row_dram[k, :].rearrange("(t c) -> t c", t=NT),
                                     rows7[:, k, :]).then_inc(s_rowsD, 16)
                    sp.wait_ge(s_rowsD, 32)
                    sp.dma_start(rows[0:1, :, :], chunk_row_dram.rearrange("k n -> (k n)").rearrange("(a k n) -> a k n", a=1, k=2)).then_inc(s_rowsS, 16)
                    sp.wait_ge(s_rowsS, 16)
                    sp.wait_ge(s_x, 16 * 39)
                    sp.wait_ge(s_slotC, NREC + 1)
                    sp.dma_start(slots.rearrange("g p r -> p g r"), rec[:, :, :, :].rearrange("p g a e -> p g (a e)")).then_inc(s_slotD, 16)
                    sp.wait_ge(s_slotD, 16)

                @block.gpsimd
                def _(pool):
                    nc.gpsimd.iota(pos[:, :], [[1, P]], base=0, channel_multiplier=0,
                                   allow_small_or_imprecise_dtypes=True).then_inc(s_const, 1)
                    nc.gpsimd.iota(part[:, :], [[1, 1]], base=0, channel_multiplier=1,
                                   allow_small_or_imprecise_dtypes=True).then_inc(s_const, 1)
                    nc.gpsimd.iota(cid[:, :], [[P, NT]], base=0, channel_multiplier=1,
                                   allow_small_or_imprecise_dtypes=True).then_inc(s_const, 1)
                    nc.gpsimd.memset(ones[:, :], 1.0).then_inc(s_const, 1)
                    nc.gpsimd.memset(zrow[:, :, :], 0).then_inc(s_zero, 1)
                    pool.wait_ge(s_meta, 16 * 8)
                    pool.wait_ge(s_tail, 32)
                    pool.wait_ge(s_idx, 1)
                    for t in range(NT):
                        for h in range(2):
                            pool.indirect_dma_start(
                                got[:, t, h, :, :].rearrange("p a k -> p (a k)"), None,
                                meta.rearrange("r a k -> r (a k)"),
                                bass.IndirectOffsetOnAxis(ridx[:, h, t:t + 1], 0)).then_inc(s_got, 16)

                @block.tensor
                def _(pe):
                    pe.wait_ge(s_const, 4)
                    pe.wait_ge(s_cnt, 1)
                    nc.tensor.matmul(ps_cnt[:, 0:NB + 1], ones[0:EP, :], cnt[:, :], start=True, stop=True).then_inc(s_sum, 1)
                    pe.wait_ge(s_idx, 1)
                    for k in range(2):
                        last = nc.tensor.transpose(ps_row[0:NT, k * P:(k + 1) * P], be[:, k, :], ident[:, :])
                    last.then_inc(s_rowsT, 1)
                    pe.wait_ge(s_slotA, 1)
                    for a in range(NREC):
                        if a >= 2:
                            pe.wait_ge(s_slotC, a - 1)
                        for t in range(NT):
                            last = nc.tensor.transpose(ps_turn[:, a % 2, t * P:(t + 1) * P], fin[:, a, t, :], ident[:, :])
                        last.then_inc(s_slotT, 1)

                @block.scalar
                def _(act):
                    act.wait_ge(s_rowsT, 1)
                    nc.scalar.activation(rows7[:, :, :], ps_row[0:NT, 0:2 * P].rearrange("t (k c) -> t k c", k=2),
                                         ACT.Copy).then_inc(s_rowsC, 1)
                    for a in range(NREC):
                        act.wait_ge(s_slotT, a + 1)
                        if a == DLOC:
                            nc.scalar.activation(dloc[:, :], ps_turn[:, a % 2, 0:NS], ACT.Copy)
                        dest = rec[:, :, a, :] if a in (SRC, SRC_TYPE, BLOCK) else rec[:, :, a, :].bitcast(F32)
                        nc.scalar.activation(dest, ps_turn[:, a % 2, 0:NS].rearrange("p (g e) -> p g e", e=HALF), ACT.Copy).then_inc(s_slotC, 1)
                    act.wait_ge(s_x, 16 * 39)
                    for k in (1, 3):
                        last = nc.scalar.activation(e_ls[:, k, :], e_ls[:, k, :], ACT.Exp)
                    last.then_inc(s_slotC, 1)

                @block.vector
                def _(dve):
                    v = nc.vector
                    dve.wait_ge(s_const, 4)
                    link(v.tensor_scalar(ident[:, :], pos[:, :], part[:, 0:1], None, ALU.is_equal))
                    link(v.tensor_copy(ident_b[:, :], ident[:, :]))
                    dve.wait_ge(s_dst, 16)
                    v.memset(cnt[:, 0:1], 0.0)
                    v.memset(cnt[:, NB:NB + 1], float(E // EP))
                    link(v.tensor_copy(dst_f[:, :], dst_l[:, :]))
                    for b in range(1, NB):
                        link(v.tensor_scalar(cmp_l[:, :], dst_f[:, :], float(BN * b), None, ALU.is_lt, ALU.add,
                                             accum_out=cnt[:, b:b + 1]))
                    v.tensor_copy(t_f[:, 0:1], part[:, 0:1]).then_inc(s_cnt, 1)
                    dve.wait_ge(s_sum, 1)
                    link(v.tensor_copy(first[:, :], ps_cnt[:, 0:NB + 1]))
                    link(v.tensor_tensor(nb[:, :], first[:, 1:NB + 1], first[:, 0:NB], ALU.subtract))
                    link(v.tensor_scalar(t_i[:, :], nb[:, :], float(C - 1), None, ALU.add))
                    link(v.tensor_scalar(t_j[:, :], t_i[:, :], 7, None, ALU.arith_shift_right))
                    link(v.tensor_scalar(nch[:, :], t_j[:, :], 1.0, None, ALU.max))
                    link(v.tensor_tensor_scan(cs[:, :], ones[:, 0:NB], nch[:, :], 0.0, ALU.mult, ALU.add))
                    link(v.tensor_tensor(cs[:, :], cs[:, :], nch[:, :], ALU.subtract))
                    link(v.scalar_tensor_tensor(pad[:, :], cs[:, :], float(C), first[:, 0:NB], ALU.mult, ALU.subtract))
                    v.memset(dpad[:, 0:1], 0.0)
                    link(v.tensor_tensor(dpad[:, 1:NB], pad[:, 1:NB], pad[:, 0:NB - 1], ALU.subtract))
                    link(v.tensor_tensor(cmp[:, :, :], cid[:, :].unsqueeze(2).to_broadcast([P, NT, NB]),
                                         cs[:, :].unsqueeze(1).to_broadcast([P, NT, NB]), ALU.is_ge))
                    link(v.tensor_reduce(be[:, 0, :], cmp[:, :, :], AX, ALU.add))
                    link(v.tensor_scalar(be[:, 0, :], be[:, 0, :], -1.0, None, ALU.add))
                    link(v.tensor_tensor(prod[:, :, :], cmp[:, :, :], dpad[:, :].unsqueeze(1).to_broadcast([P, NT, NB]), ALU.mult))
                    link(v.tensor_reduce(padc[:, :], prod[:, :, :], AX, ALU.add))
                    link(v.tensor_tensor(prod[:, :, :], cmp[:, :, :], nb[:, :].unsqueeze(1).to_broadcast([P, NT, NB]), ALU.mult))
                    link(v.tensor_reduce(endc[:, :], prod[:, :, :], AX, ALU.add))
                    link(v.scalar_tensor_tensor(e0c[:, :], cid[:, :], float(C), padc[:, :], ALU.mult, ALU.subtract))
                    link(v.tensor_tensor(nv[:, :], endc[:, :], e0c[:, :], ALU.subtract))
                    link(v.tensor_scalar(be[:, 1, :], e0c[:, :], float(E - 1), None, ALU.min))
                    link(v.tensor_scalar(e0c[:, :], e0c[:, :], float((MROWS - 1) * C - 1), None, ALU.min))
                    link(v.tensor_copy(e0i[:, :], e0c[:, :]))
                    link(v.tensor_scalar(ridx[:, 0, :], e0i[:, :], 7, None, ALU.arith_shift_right))
                    link(v.tensor_scalar(ridx[:, 1, :], ridx[:, 0, :], 1.0, None, ALU.add))
                    v.tensor_scalar(off[:, :], e0i[:, :], C - 1, None, ALU.bitwise_and).then_inc(s_idx, 1)
                    dve.wait_ge(s_idx, 1)
                    for k in range(7):
                        link(v.tensor_scalar(bit_i[:, :], off[:, :], k, 1, ALU.arith_shift_right, ALU.bitwise_and))
                        link(v.tensor_copy(bit[:, k, :], bit_i[:, :]))
                    link(v.tensor_scalar(nbit[:, :, :], bit[:, :, :], -1.0, 1.0, ALU.mult, ALU.add))
                    dve.wait_ge(s_got, 16 * 2 * NT)
                    for h in range(2):
                        link(v.tensor_copy(wa[:, :, 0:3, h * C:(h + 1) * C], got[:, :, h, 0:3, :]))
                        link(v.tensor_copy(wa[:, :, 3, h * C:(h + 1) * C], got[:, :, h, 3, :].bitcast(F32)))
                    now, nxt, width = wa, wb, 2 * C
                    for k in range(6, -1, -1):
                        s = 1 << k
                        width = max(width - s, C)
                        for t in range(NT):
                            link(v.tensor_scalar(nxt[:, t, :, 0:width], now[:, t, :, 0:width], nbit[:, k, t:t + 1], None, ALU.mult))
                            link(v.scalar_tensor_tensor(nxt[:, t, :, 0:width], now[:, t, :, s:s + width], bit[:, k, t:t + 1],
                                                        nxt[:, t, :, 0:width], ALU.mult, ALU.add))
                        now, nxt = nxt, now
                    for t in range(NT):
                        v.tensor_scalar(valid[:, t, :], pos[:, :], nv[:, t:t + 1], None, ALU.is_lt)
                    link(v.tensor_scalar(base[:, :], be[:, 0, :], float(BN), -1.0, ALU.mult, ALU.add))
                    a_src, a_dst = now[:, :, 0, 0:C], now[:, :, 1, 0:C]
                    link(v.scalar_tensor_tensor(key[:, :, :], a_dst, 1.0, valid[:, :, :], ALU.add, ALU.mult))
                    link(v.tensor_scalar(key[:, :, :], key[:, :, :], -1.0, None, ALU.add))
                    for t in range(NT):
                        link(v.scalar_tensor_tensor(fin[:, DLOC, t, :], now[:, t, 1, 0:C], base[:, t:t + 1], valid[:, t, :],
                                                    ALU.subtract, ALU.mult))
                    link(v.tensor_scalar(fin[:, DLOC, :, :], fin[:, DLOC, :, :], -1.0, None, ALU.add))
                    link(v.tensor_copy(fin[:, SRC, :, :], a_src))
                    link(v.tensor_copy(fin[:, TYPE, :, :], now[:, :, 2, 0:C]))
                    link(v.tensor_copy(fin[:, WEIGHT, :, :], now[:, :, 3, 0:C]))
                    link(v.tensor_copy(src_c[:, :, :], a_src))
                    link(v.tensor_scalar(lo_i[:, :, :], src_c[:, :, :], C - 1, None, ALU.bitwise_and))
                    link(v.scalar_tensor_tensor(fin[:, SRC_LO, :, :], lo_i[:, :, :], 1.0, valid[:, :, :], ALU.add, ALU.mult))
                    link(v.tensor_scalar(fin[:, SRC_LO, :, :], fin[:, SRC_LO, :, :], -1.0, None, ALU.add))
                    link(v.tensor_scalar(lo_i[:, :, :], src_c[:, :, :], 7, None, ALU.arith_shift_right))
                    link(v.tensor_copy(fin[:, SRC_HI, :, :], lo_i[:, :, :]))
                    link(v.tensor_copy(fin[:, BLOCK, :, :], be[:, 0, :].unsqueeze(2).to_broadcast([P, NT, C])))
                    v.scalar_tensor_tensor(fin[:, SRC_TYPE, :, :], fin[:, SRC, :, :], float(R), fin[:, TYPE, :, :],
                                           ALU.mult, ALU.add).then_inc(s_slotA, 1)

        s_sq = sem("variances_made")
        s_rt = sem("roots_made")
        n_norm = [0]

        def norm(act, dve, part_of, st_tiles):
            mean, cen, sq, var = st_tiles
            n = n_norm[0]
            if part_of == "scalar":
                act.wait_ge(s_sq, n + 1)
                nc.scalar.activation(var[:, :], var[:, :], ACT.Sqrt).then_inc(s_rt, 1)
                return
            v = nc.vector
            link(v.tensor_reduce(mean[:, :], X[:, :, :], AX, ALU.add))
            link(v.tensor_scalar(mean[:, :], mean[:, :], 1.0 / D, None, ALU.mult))
            link(v.tensor_tensor(cen[:, :, :], X[:, :, :], mean[:, :].unsqueeze(2).to_broadcast([BN, NB, D]), ALU.subtract))
            link(v.tensor_tensor(sq[:, :, :], cen[:, :, :], cen[:, :, :], ALU.mult))
            link(v.tensor_reduce(var[:, :], sq[:, :, :], AX, ALU.add))
            v.tensor_scalar(var[:, :], var[:, :], 1.0 / D, EPS, ALU.mult, ALU.add).then_inc(s_sq, 1)
            dve.wait_ge(s_rt, n + 1)
            link(v.reciprocal(var[:, :], var[:, :]))
            link(v.tensor_tensor(cen[:, :, :], cen[:, :, :], var[:, :].unsqueeze(2).to_broadcast([BN, NB, D]), ALU.mult))
            link(v.tensor_scalar(H[:, :, :], cen[:, :, :], 0.0, None, ALU.max))

        def norm_phase():
            phase[0] += 1
            ns = ExitStack()
            with ns:
                tiles = (sb("mean", [BN, NB], F32, ns), sb("cen", [BN, NB, D], F32, ns),
                         sb("sq", [BN, NB, D], F32, ns), sb("var", [BN, NB], F32, ns))
                with nc.Block() as block:
                    @block.scalar
                    def _(act):
                        norm(act, None, "scalar", tiles)

                    @block.vector
                    def _(dve):
                        norm(None, dve, "vector", tiles)
            n_norm[0] += 1

        class Counted:

            def __init__(self, name, credit=0):
                self.sem, self.base, self.credit = sem(name), 0, credit

            def at(self, n):
                return self.base + self.credit + n

            def over(self, n):
                self.base += self.credit + n

        staged = [Counted(f"staged_{h}") for h in range(2)]
        gathered = [Counted(f"gathered_{j}") for j in range(U)]
        stashed = [Counted(f"stashed_{h}", 16) for h in range(2)]
        loaded = [Counted(f"loaded_{h}") for h in range(2)]
        attr_loaded = [Counted(f"attr_loaded_{j}") for j in range(U)]
        msg_made = Counted("messages_made", 2)
        onehot_made = Counted("onehots_made")
        chunk_done = Counted("chunks_done", 2 * U)
        narrow_made = Counted("narrow_onehots_made")
        turned = Counted("onehots_turned")
        turned_copied = Counted("turned_copied", 1)
        dest_made = Counted("dest_rows_made")
        z_made = Counted("z_made", 2)
        self_kept = Counted("self_scores_kept", 2)
        leaky_made = Counted("leaky_made")
        pool_seen = sem("pool_saw_stage")

        sp_seen = sem("sp_saw_stash")

        def blocks_of(chunk, n):
            return nc.values_load_multi_w_load_instructions(
                rows[0:1, 0, bass.ds(chunk, n)], engines=[mybir.EngineType.PE], min_val=0, max_val=NB - 1,
                skip_runtime_bounds_check_because="blocks are counted below NB")[1]

        def stage_half(sp, stage, i, h, others=()):
            sp.wait_ge(chunk_done.sem, chunk_done.at((i - 1) * U + HALF * (h + 1)))
            for c in others:
                sp.sem_inc(sp_seen, 1)
                sp.wait_ge(c.sem, c.at(16 * i))
                sp.sem_inc(sp_seen, 1)
            sp.dma_start(stage[:, h, :, :].rearrange("p a e -> p (a e)"),
                         slots[bass.ds(2 * i + h, 1), :, :].rearrange("o p r -> (o p) r")).then_inc(staged[h].sem, 16)

        def gather_loop(pool, stage, G, width, table, field):
            with pool.Fori(0, TURNS) as i:
                for h in range(2):
                    pool.wait_ge(staged[h].sem, staged[h].at(16 * i + 16))
                    pool.sem_inc(pool_seen, 1)
                    for j in range(HALF * h, HALF * (h + 1)):
                        pool.indirect_dma_start(G[:, j, 0:width], None, table,
                                                bass.IndirectOffsetOnAxis(stage[:, h, field, j % HALF:j % HALF + 1], 0)
                                                ).then_inc(gathered[j].sem, 16)

        def make_onehots(S, i, h, halves=2):
            return nc.vector.tensor_tensor(
                S[:, HALF * h:HALF * (h + 1), :], pos[:, 0:BN].unsqueeze(1).to_broadcast([P, HALF, BN]),
                dloc[:, bass.ds(i * halves * HALF + HALF * h, HALF)].unsqueeze(2).to_broadcast([P, HALF, BN]), ALU.is_equal)

        def zero_sums(ps, zero, banks):
            for k in range(banks):
                nc.tensor.matmul(ps[:, k * BANK:(k + 1) * BANK], zero[:, 0:P], zero[:, :], start=True, stop=True)

        def sum_chunk(ps_sum, S, j, M, width, block):
            return nc.tensor.matmul(ps_sum[0:BN, bass.ds(block * P, width)], S[:, j, :], M,
                                    start=False, stop=True, skip_group_check=True)

        def sums(ps_sum, width):
            return ps_sum[0:BN, 0:NB * P].rearrange("p (b f) -> p b f", f=P)[:, :, 0:width]

        def once(name):
            return sem(f"{name}_{phase[0]}")

        dense_ready = Counted("dense_ready")
        after_done = Counted("dense_after_done")
        nodes_written = Counted("nodes_written")
        turned_b = Counted("blocks_turned")
        copied_b = Counted("blocks_copied")
        multiplied_b = Counted("blocks_multiplied")
        taken_b = Counted("blocks_taken")

        def dense(cat, k, pieces, take, before=None, after=None, sp_program=None, between=None, act_between=None):
            phase[0] += 1
            es = ExitStack()
            with es:
                catT = sb("catT", [P, 2, P], F32, es)
                ps_t = pb("ps_t", [P, 2, BANK], F32, es)
                ps_o = pb("ps_o", [P, 2, 2, BANK], F32, es)
                with nc.Block() as block:
                    @block.vector
                    def _(dve):
                        if before is not None:
                            before(dve)
                        dve.sem_inc(dense_ready.sem, 1)
                        for b in range(NB):
                            dve.wait_ge(multiplied_b.sem, multiplied_b.at(b + 1))
                            take(dve, b, ps_o[0:BN, b % 2, :, :]).then_inc(taken_b.sem, 1)
                            if between is not None:
                                between(dve, b)
                        if after is not None:
                            dve.wait_ge(taken_b.sem, taken_b.at(NB))
                            after(dve)
                            dve.sem_inc(after_done.sem, 1)

                    @block.tensor
                    def _(pe):
                        pe.wait_ge(dense_ready.sem, dense_ready.at(1))

                        def turn(b):
                            if b >= 2:
                                pe.wait_ge(copied_b.sem, copied_b.at(b - 1))
                            nc.tensor.transpose(ps_t[0:k, b % 2, 0:BN], cat[:, b, :], ident[0:BN, 0:BN]).then_inc(turned_b.sem, 1)

                        turn(0)
                        for b in range(NB):
                            if b + 1 < NB:
                                turn(b + 1)
                            pe.wait_ge(copied_b.sem, copied_b.at(b + 1))
                            if b >= 2:
                                pe.wait_ge(taken_b.sem, taken_b.at(b - 1))
                            for n, w in enumerate(pieces):
                                last = nc.tensor.matmul(ps_o[0:BN, b % 2, n, 0:w.shape[1]], catT[0:k, b % 2, 0:BN], w,
                                                        start=True, stop=True)
                            last.then_inc(multiplied_b.sem, 1)

                    @block.scalar
                    def _(act):
                        for b in range(NB):
                            act.wait_ge(turned_b.sem, turned_b.at(b + 1))
                            if b >= 2:
                                act.wait_ge(multiplied_b.sem, multiplied_b.at(b - 1))
                            nc.scalar.activation(catT[0:k, b % 2, 0:BN], ps_t[0:k, b % 2, 0:BN], ACT.Copy).then_inc(copied_b.sem, 1)
                            if act_between is not None:
                                act_between(act, b)

                    if sp_program is not None:
                        @block.sync
                        def _(sp):
                            sp_program(sp)
                dense_ready.over(1)
                if after is not None:
                    after_done.over(1)
                for c in (turned_b, copied_b, multiplied_b, taken_b):
                    c.over(NB)

        def bcn(ap):
            return ap.unsqueeze(1).to_broadcast([BN, NB, D])

        def bcd(ap):
            return ap.unsqueeze(2).to_broadcast([BN, NB, D])

        def write_nodes(sp):
            sp.wait_ge(after_done.sem, after_done.at(1))
            sp.dma_start(node_table.rearrange("(b p) f -> p b f", p=BN), H[:, :, :]).then_inc(nodes_written.sem, 16)
            sp.wait_ge(nodes_written.sem, nodes_written.at(16))
            nodes_written.over(16)

        def write_table(tile):
            phase[0] += 1
            written = once("table_written")
            with nc.Block() as block:
                @block.sync
                def _(sp):
                    sp.dma_start(node_table.rearrange("(b p) f -> p b f", p=BN), tile).then_inc(written, 16)
                    sp.wait_ge(written, 16)

        def weighted_sums(SUM, hist):
            phase[0] += 1
            es = ExitStack()
            with es:
                stage = sb("stage", [P, 2, R, HALF], I32, es)
                stage_f = stage[:, :, :, :].bitcast(F32)
                G = sb("gathered_rows", [P, U, D], F32, es)
                M = sb("messages", [P, U, D + 1], F32, es)
                S = sb("onehots", [P, U, BN], F32, es)
                if hist:
                    Lo = sb("onehots_low", [P, U, P], F32, es)
                    Hi = sb("onehots_high", [P, U, NB], F32, es)
                else:
                    SN = sb("onehots_narrow", [P, U, BN], BF16, es)
                    ST = sb("onehots_turned", [P, U, P], BF16, es)
                zero = sb("zero_bank", [P, BANK], F32, es)
                HIST = sb("hist_sb", [P, NB], F32, es)
                ps_sum = pb("ps_sum", [P, 7 * BANK], F32, es)
                ps_hist = pb("ps_hist", [P, BANK], F32, es) if hist else None
                ps_T = pb("ps_T", [P, HALF, P], BF16, es) if not hist else None
                ready, finished, hist_made, hist_stored, hist_loaded = (once(x) for x in (
                    "set_up", "loop_over", "hist_made", "hist_stored", "hist_loaded"))
                with nc.Block() as block:
                    @block.sync
                    def _(sp):
                        with sp.Fori(0, TURNS) as i:
                            for h in range(2):
                                stage_half(sp, stage, i, h)
                        if not hist:
                            for h in range(2):
                                sp.wait_ge(stashed[h].sem, stashed[h].at(16 * TURNS))
                        if hist:
                            sp.wait_ge(hist_made, 1)
                            sp.dma_start(hist_dram.rearrange("(h l) -> l h", l=P), HIST[:, :],
                                         allow_slow_non_contiguous=True).then_inc(hist_stored, 16)
                            sp.wait_ge(hist_stored, 16)
                            sp.dma_start(deg_out[:, :], hist_dram[0:N].rearrange("(b p) -> p b", p=BN),
                                         allow_slow_non_contiguous=True).then_inc(hist_loaded, 16)
                            sp.wait_ge(hist_loaded, 16)

                    @block.gpsimd
                    def _(pool):
                        gather_loop(pool, stage, G, D, node_table, SRC)

                    @block.scalar
                    def _(act):
                        with act.Fori(0, TURNS) as i:
                            for h in range(2):
                                act.wait_ge(staged[h].sem, staged[h].at(16 * i + 16))
                                for j in range(HALF * h, HALF * (h + 1)):
                                    act.wait_ge(gathered[j].sem, gathered[j].at(16 * i + 16))
                                    nc.scalar.activation(M[:, j, 0:D], G[:, j, :], ACT.Copy,
                                                         scale=stage_f[:, h, WEIGHT, j % HALF:j % HALF + 1]).then_inc(msg_made.sem, 1)
                                if not hist:
                                    half = slice(HALF * h, HALF * (h + 1))
                                    act.wait_ge(turned.sem, turned.at(2 * i + h + 1))
                                    act.wait_ge(stashed[h].sem, stashed[h].at(16 * i))
                                    nc.scalar.activation(ST[0:BN, half, :], ps_T[0:BN, :, :], ACT.Copy).then_inc(turned_copied.sem, 1)
                                    act.wait_ge(turned_copied.sem, turned_copied.at(2 * i + h + 1))
                                    act.dma_start(turned_dram[bass.ds(2 * i + h, 1), :, :].rearrange("o p r -> (o p) r"),
                                                  ST[0:BN, half, :].rearrange("p c s -> p (c s)")).then_inc(stashed[h].sem, 16)

                    @block.vector
                    def _(dve):
                        v = nc.vector
                        v.memset(zero[:, :], 0.0)
                        v.memset(M[:, :, D:D + 1], 1.0).then_inc(ready, 1)
                        with dve.Fori(0, TURNS) as i:
                            for h in range(2):
                                dve.wait_ge(staged[h].sem, staged[h].at(16 * i + 16))
                                if hist:
                                    for tile, field, w in ((Lo, SRC_LO, P), (Hi, SRC_HI, NB)):
                                        v.tensor_tensor(tile[:, HALF * h:HALF * (h + 1), :],
                                                        pos[:, 0:w].unsqueeze(1).to_broadcast([P, HALF, w]),
                                                        stage_f[:, h, field, :].unsqueeze(2).to_broadcast([P, HALF, w]), ALU.is_equal)
                                make_onehots(S, i, h).then_inc(onehot_made.sem, 1)
                                if not hist:
                                    make_onehots(SN, i, h).then_inc(narrow_made.sem, 1)
                        dve.wait_ge(finished, 1)
                        if hist:
                            v.tensor_copy(HIST[:, :], ps_hist[:, 0:NB]).then_inc(hist_made, 1)
                        link(v.tensor_copy(SUM[:, :, :], sums(ps_sum, D + 1)))
                        if hist:
                            link(v.tensor_copy(deg_in[:, :], SUM[:, :, D]))

                    @block.tensor
                    def _(pe):
                        for c in (msg_made, *(() if hist else (turned_copied, *stashed)), chunk_done):
                            nc.tensor.nop().then_inc(c.sem, c.credit)
                        pe.wait_ge(ready, 1)
                        zero_sums(ps_sum, zero, 7)
                        if hist:
                            zero_sums(ps_hist, zero, 1)
                        with pe.Fori(0, TURNS) as i:
                            for j in range(U):
                                h = j // HALF
                                if j == 0:
                                    at = blocks_of(i * U, U)
                                if j % HALF == 0:
                                    pe.wait_ge(onehot_made.sem, onehot_made.at(2 * i + h + 1))
                                if not hist and j % HALF == 0:
                                    pe.wait_ge(narrow_made.sem, narrow_made.at(2 * i + h + 1))
                                    pe.wait_ge(turned_copied.sem, turned_copied.at(2 * i + h))
                                    for q in range(HALF):
                                        last = nc.tensor.transpose(ps_T[0:BN, q, :], SN[:, j + q, :], ident_b[:, :])
                                    last.then_inc(turned.sem, 1)
                                if hist:
                                    nc.tensor.matmul(ps_hist[:, 0:NB], Lo[:, j, :], Hi[:, j, :], start=False, stop=True,
                                                     skip_group_check=True)
                                pe.wait_ge(msg_made.sem, msg_made.at(i * U + j + 1))
                                sum_chunk(ps_sum, S, j, M[:, j, :], D + 1, at[j]).then_inc(chunk_done.sem, 1)
                        if hist:
                            nc.tensor.matmul(ps_hist[:, 0:1], zero[:, 0:P], zero[:, 0:1], start=False, stop=True,
                                             skip_group_check=True).then_inc(finished, 1)
                        else:
                            nc.tensor.matmul(ps_sum[:, 6 * BANK + 3 * P:7 * BANK], zero[:, 0:P], zero[:, 0:P], start=False, stop=True,
                                             skip_group_check=True).then_inc(finished, 1)
                for c in (*staged, *gathered):
                    c.over(16 * TURNS)
                msg_made.over(NCH)
                onehot_made.over(2 * TURNS)
                chunk_done.over(NCH)
                if not hist:
                    for c in (narrow_made, turned, turned_copied):
                        c.over(2 * TURNS)
                    for c in stashed:
                        c.over(16 * TURNS)

        def attribute_sums(SUM, attr):
            phase[0] += 1
            es = ExitStack()
            with es:
                stage = sb("stage", [P, 2, R, HALF], I32, es)
                stage_f = stage[:, :, :, :].bitcast(F32)
                G = sb("gathered_rows", [P, U, 2 * D], F32, es)
                A = sb("attributes", [P, U, D], F32, es)
                S = sb("onehots", [P, U, BN], F32, es)
                zero = sb("zero_bank", [P, BANK], F32, es)
                ps_sum = pb("ps_sum", [P, 7 * BANK], F32, es)
                ready, finished = (once(x) for x in ("set_up", "loop_over"))
                with nc.Block() as block:
                    @block.sync
                    def _(sp):
                        with sp.Fori(0, TURNS) as i:
                            for h in range(2):
                                stage_half(sp, stage, i, h)
                                for q in range(0, HALF, 4):
                                    first = nc.values_load_multi_w_load_instructions(
                                        rows[0:1, 1, bass.ds(i * U + HALF * h + q, 4)], engines=[mybir.EngineType.SP],
                                        min_val=0, max_val=E - 1, skip_runtime_bounds_check_because="clipped to E - 1")[1]
                                    for k in range(4):
                                        j = HALF * h + q + k
                                        sp.dma_start(A[:, j, :], attr[bass.ds(first[k], C), :]).then_inc(attr_loaded[j].sem, 16)

                    @block.gpsimd
                    def _(pool):
                        gather_loop(pool, stage, G, D, node_table, SRC)

                    @block.vector
                    def _(dve):
                        v = nc.vector
                        v.memset(zero[:, :], 0.0).then_inc(ready, 1)
                        with dve.Fori(0, TURNS) as i:
                            for h in range(2):
                                dve.wait_ge(staged[h].sem, staged[h].at(16 * i + 16))
                                make_onehots(S, i, h).then_inc(onehot_made.sem, 1)
                                for j in range(HALF * h, HALF * (h + 1)):
                                    dve.wait_ge(gathered[j].sem, gathered[j].at(16 * i + 16))
                                    dve.wait_ge(attr_loaded[j].sem, attr_loaded[j].at(16 * i + 16))
                                    v.tensor_tensor(G[:, j, D:2 * D], G[:, j, 0:D], A[:, j, :], ALU.mult).then_inc(msg_made.sem, 1)
                        dve.wait_ge(finished, 1)
                        link(v.tensor_copy(SUM[:, :, :], sums(ps_sum, 2 * D)))

                    @block.tensor
                    def _(pe):
                        for c in (msg_made, chunk_done):
                            nc.tensor.nop().then_inc(c.sem, c.credit)
                        pe.wait_ge(ready, 1)
                        zero_sums(ps_sum, zero, 7)
                        with pe.Fori(0, TURNS) as i:
                            for j in range(U):
                                h = j // HALF
                                if j == 0:
                                    at = blocks_of(i * U, U)
                                if j % HALF == 0:
                                    pe.wait_ge(onehot_made.sem, onehot_made.at(2 * i + h + 1))
                                pe.wait_ge(msg_made.sem, msg_made.at(i * U + j + 1))
                                sum_chunk(ps_sum, S, j, G[:, j, :], 2 * D, at[j]).then_inc(chunk_done.sem, 1)
                        nc.tensor.matmul(ps_sum[:, 6 * BANK + 3 * P:7 * BANK], zero[:, 0:P], zero[:, 0:P], start=False, stop=True,
                                         skip_group_check=True).then_inc(finished, 1)
                for c in (*staged, *gathered, *attr_loaded):
                    c.over(16 * TURNS)
                msg_made.over(NCH)
                onehot_made.over(2 * TURNS)
                chunk_done.over(NCH)

        norm_phase()
        write_table(H[:, :, :])
        ls = ExitStack()
        with ls:
            CAT = sb("cat", [BN, NB, 2 * D], F32, ls)
            SUM = sb("sums", [BN, NB, D + 1], F32, ls)
            inv_deg = sb("inv_deg", [BN, NB], F32, ls)
            has = sb("has", [BN, NB], F32, ls)
            for l in range(2):
                weighted_sums(SUM, l == 0)

                def before(dve, l=l):
                    v = nc.vector
                    if l == 0:
                        link(v.tensor_scalar(has[:, :], deg_in[:, :], 0.0, None, ALU.is_gt))
                        link(v.tensor_scalar(inv_deg[:, :], deg_in[:, :], 1.0, None, ALU.max))
                        link(v.reciprocal(inv_deg[:, :], inv_deg[:, :]))
                        link(v.tensor_tensor(inv_deg[:, :], inv_deg[:, :], has[:, :], ALU.mult))
                    link(v.tensor_copy(CAT[:, :, 0:D], H[:, :, :]))
                    link(v.tensor_tensor(CAT[:, :, D:2 * D], SUM[:, :, 0:D], bcd(inv_deg[:, :]), ALU.mult))

                def take(dve, b, ps):
                    return nc.vector.tensor_copy(H[:, b, :], ps[:, 0, 0:D])

                def after(dve, l=l):
                    v = nc.vector
                    link(v.tensor_tensor(H[:, :, :], H[:, :, :], bcn(bc_n[:, l, :]), ALU.add))
                    if l == 0:
                        link(v.tensor_scalar(H[:, :, :], H[:, :, :], 0.0, None, ALU.max))
                    else:
                        link(v.tensor_tensor(X[:, :, :], X[:, :, :], H[:, :, :], ALU.add))

                dense(CAT[:, :, :], 2 * D, [w0[:, l, :]], take, before, after, write_nodes if l == 0 else None)

        norm_phase()
        ls = ExitStack()
        with ls:
            SUM = sb("sums", [BN, NB, 2 * D], F32, ls)
            AGG = sb("agg", [BN, NB, D], F32, ls)
            norm_of = sb("norm_of", [BN, 2, NB], F32, ls)
            has = sb("has", [BN, NB], F32, ls)
            red = sb("red", [BN, NB], F32, ls)
            roots = sem("norm_roots")
            with nc.Block() as block:
                @block.vector
                def _(dve):
                    v = nc.vector
                    link(v.tensor_scalar(norm_of[:, 0, :], deg_out[:, :], 1.0, None, ALU.max))
                    v.tensor_scalar(norm_of[:, 1, :], deg_in[:, :], 1.0, None, ALU.max).then_inc(roots, 1)
                    dve.wait_ge(roots, 2)
                    link(v.reciprocal(norm_of[:, :, :], norm_of[:, :, :]))
                    for k, deg in enumerate((deg_out, deg_in)):
                        link(v.tensor_scalar(has[:, :], deg[:, :], 0.0, None, ALU.is_gt))
                        link(v.tensor_tensor(norm_of[:, k, :], norm_of[:, k, :], has[:, :], ALU.mult))
                    link(v.tensor_tensor(H[:, :, :], H[:, :, :], bcd(norm_of[:, 0, :]), ALU.mult))

                @block.scalar
                def _(act):
                    act.wait_ge(roots, 1)
                    nc.scalar.activation(norm_of[:, :, :], norm_of[:, :, :], ACT.Sqrt).then_inc(roots, 1)
            write_table(H[:, :, :])
            for l in range(2):
                attribute_sums(SUM, io["edge_attr_64" if l == 0 else "edge_attr_64_n2"])
                exps = sem(f"softmax_exps_{l}")

                def before(dve, l=l):
                    v = nc.vector
                    link(v.tensor_tensor(AGG[:, :, :], SUM[:, :, 0:D], bcn(e_ls[:, 2 * l, :]), ALU.mult))
                    link(v.tensor_tensor(H[:, :, :], SUM[:, :, D:2 * D], bcn(e_ls[:, 2 * l + 1, :]), ALU.mult))
                    link(v.tensor_tensor(AGG[:, :, :], AGG[:, :, :], H[:, :, :], ALU.add))
                    link(v.tensor_tensor(AGG[:, :, :], AGG[:, :, :], bcd(norm_of[:, 1, :]), ALU.mult))

                def take(dve, b, ps):
                    return nc.vector.tensor_copy(H[:, b, :], ps[:, 0, 0:D])

                def after(dve, l=l):
                    v = nc.vector
                    link(v.tensor_tensor(H[:, :, :], H[:, :, :], bcn(bc_n[:, 2 + l, :]), ALU.add))
                    if l == 0:
                        link(v.tensor_scalar(H[:, :, :], H[:, :, :], 0.0, None, ALU.max))
                        link(v.tensor_tensor(H[:, :, :], H[:, :, :], bcd(norm_of[:, 0, :]), ALU.mult))
                    else:
                        link(v.tensor_reduce(red[:, :], H[:, :, :], AX, ALU.max))
                        link(v.tensor_tensor(H[:, :, :], H[:, :, :], bcd(red[:, :]), ALU.subtract))

                dense(AGG[:, :, :], D, [w1[:, l, :]], take, before, after, write_nodes if l == 0 else None)
            with nc.Block() as block:
                @block.scalar
                def _(act):
                    nc.scalar.activation(H[:, :, :], H[:, :, :], ACT.Exp).then_inc(exps, 1)

                @block.vector
                def _(dve):
                    v = nc.vector
                    dve.wait_ge(exps, 1)
                    link(v.tensor_reduce(red[:, :], H[:, :, :], AX, ALU.add))
                    link(v.reciprocal(red[:, :], red[:, :]))
                    link(v.tensor_tensor(H[:, :, :], H[:, :, :], bcd(red[:, :]), ALU.mult))
                    link(v.tensor_tensor(X[:, :, :], X[:, :, :], H[:, :, :], ALU.add))


        masks_dram = nc.dram_tensor("masks", [P, 4 * NS], F32, kind="Internal").ap()
        row_masks_dram = nc.dram_tensor("row_masks", [HA, 6 * NS], F32, kind="Internal").ap()
        PEN_L, PEN_R, CONT, LAST = range(4)
        ROW_L, ROW_R, ROW_C, LINK_L, LINK_R, LINK_C = range(6)

        def segments_phase():
            phase[0] += 1
            es = ExitStack()
            with es:
                masks = sb("masks", [P, 4, NT, C], F32, es)
                row_m = sb("row_masks", [HA, 6, NS], F32, es)
                ends = sb("ends", [P, 2, NT, HA], F32, es)
                ends_r = sb("ends_r", [HA, 2, NS], F32, es)
                single = sb("single", [HA, NS], F32, es)
                link_n = sb("link_n", [HA, NS], F32, es)
                ps_r = pb("ps_r", [P, 2, 2 * BANK], F32, es)
                ps_c = pb("ps_c", [P, BANK], F32, es)
                ps_w = pb("ps_w", [P, BANK], F32, es)
                ends_made, ends_turned, links_made, links_turned, masks_made, masks_stored, products = (once(x) for x in (
                    "ends_made", "ends_turned", "links_made", "links_turned", "masks_made", "masks_stored", "weight_products"))
                with nc.Block() as block:
                    @block.vector
                    def _(dve):
                        v = nc.vector
                        link(v.tensor_copy(ends[:, 0, :, :], key[:, :, 0].unsqueeze(2).to_broadcast([P, NT, HA])))
                        v.tensor_copy(ends[:, 1, :, :], key[:, :, C - 1].unsqueeze(2).to_broadcast([P, NT, HA])).then_inc(ends_made, 1)
                        v.memset(masks[:, CONT, :, 0:1], 0.0)
                        link(v.tensor_tensor(masks[:, CONT, :, 1:C], key[:, :, 1:C], key[:, :, 0:C - 1], ALU.is_equal))
                        link(v.tensor_scalar(masks[:, PEN_L, :, :], masks[:, CONT, :, :], -1.0, -FAR, ALU.add, ALU.mult))
                        v.memset(masks[:, PEN_R, :, C - 1:C], FAR)
                        link(v.tensor_copy(masks[:, PEN_R, :, 0:C - 1], masks[:, PEN_L, :, 1:C]))
                        link(v.tensor_scalar(masks[:, LAST, :, 0:C - 1], masks[:, CONT, :, 1:C], -1.0, 1.0, ALU.mult, ALU.add))
                        dve.wait_ge(ends_turned, 1)
                        link(v.tensor_copy(ends_r[:, :, :], ps_r[0:HA, :, 0:NS]))
                        link(v.tensor_tensor(single[:, :], ends_r[:, 0, :], ends_r[:, 1, :], ALU.is_equal))
                        v.memset(row_m[:, LINK_C, 0:1], 0.0)
                        v.memset(link_n[:, NS - 1:NS], 0.0)
                        link(v.tensor_tensor(row_m[:, LINK_C, 1:NS], ends_r[:, 0, 1:NS], ends_r[:, 1, 0:NS - 1], ALU.is_equal))
                        link(v.tensor_copy(link_n[:, 0:NS - 1], row_m[:, LINK_C, 1:NS]))
                        link(v.tensor_tensor(row_m[:, ROW_C, :], row_m[:, LINK_C, :], single[:, :], ALU.mult))
                        link(v.tensor_scalar(row_m[:, ROW_L, :], row_m[:, ROW_C, :], -1.0, -FAR, ALU.add, ALU.mult))
                        link(v.tensor_scalar(row_m[:, LINK_L, :], row_m[:, LINK_C, :], -1.0, -FAR, ALU.add, ALU.mult))
                        link(v.tensor_scalar(row_m[:, LINK_R, :], link_n[:, :], -1.0, -FAR, ALU.add, ALU.mult))
                        link(v.tensor_tensor(single[:, :], single[:, :], link_n[:, :], ALU.mult))
                        link(v.tensor_scalar(row_m[:, ROW_R, :], single[:, :], -1.0, -FAR, ALU.add, ALU.mult))
                        dve.sem_inc(links_made, 1)
                        dve.wait_ge(links_turned, 1)
                        link(v.tensor_scalar(masks[:, LAST, :, C - 1], ps_c[:, 0:NT * HA].rearrange("p (t h) -> p t h", h=HA)[:, :, 0],
                                             -1.0, 1.0, ALU.mult, ALU.add))
                        dve.sem_inc(masks_made, 1)
                        dve.wait_ge(products, 1)
                        link(v.tensor_copy(wkq[:, :, :, :, :].rearrange("p l k r h -> p (l k r h)"), ps_w[0:D, 0:4 * R * HR]))

                    @block.tensor
                    def _(pe):
                        pe.wait_ge(ends_made, 1)
                        for k in range(2):
                            for t in range(NT):
                                last = nc.tensor.transpose(ps_r[0:HA, k, t * P:(t + 1) * P], ends[:, k, t, :], ident[:, :])
                        last.then_inc(ends_turned, 1)
                        for l in range(2):
                            for k in range(2):
                                for r in range(R):
                                    n = ((l * 2 + k) * R + r) * HR
                                    last = nc.tensor.matmul(ps_w[0:D, n:n + HR], w3t[:, l, r, :], kq[:, l, r, k, :], start=True, stop=True)
                        last.then_inc(products, 1)
                        pe.wait_ge(links_made, 1)
                        for t in range(NT):
                            last = nc.tensor.transpose(ps_c[:, t * HA:(t + 1) * HA], link_n[:, t * P:(t + 1) * P], ident[0:HA, 0:HA])
                        last.then_inc(links_turned, 1)

                    @block.sync
                    def _(sp):
                        sp.wait_ge(masks_made, 1)
                        sp.dma_start(masks_dram, masks[:, :, :, :].rearrange("p m t c -> p (m t c)")).then_inc(masks_stored, 16)
                        sp.dma_start(row_masks_dram, row_m[:, :, :].rearrange("p m c -> p (m c)")).then_inc(masks_stored, 16)
                        sp.wait_ge(masks_stored, 32)

        sm_masks_in = Counted("masks_loaded")
        sm_turned_in = Counted("scores_turned")
        sm_copied_in = Counted("scores_copied")
        sm_exp_asked = Counted("exps_asked_for")
        sm_exp_made = Counted("exps_made")
        sm_ends_made = Counted("ends_made")
        sm_ends_turned = Counted("ends_turned")
        sm_carry_made = Counted("carries_made")
        sm_carry_turned = Counted("carries_turned")
        sm_out_made = Counted("shares_made")
        sm_turned_out = Counted("shares_turned")
        sm_copied_out = Counted("shares_copied")

        def softmax_phase(SCORE, heads, leaky, with_self):
            phase[0] += 1
            es = ExitStack()
            with es:
                masks = sb("masks", [P, 4, NS], F32, es)
                row_m = sb("row_masks", [HA, 6, NS], F32, es)
                A = sb("scores", [P, heads, NS], F32, es)
                AS = sb("self_scores", [P, heads, NS], F32, es) if with_self else None
                W = sb("running", [P, heads, NS], F32, es)
                B = sb("running_back", [P, heads, NS], F32, es)
                edge = sb("edge", [P, heads, NT], F32, es)
                row = sb("row", [heads, NS], F32, es)
                carry = sb("carry", [heads, NS], F32, es)
                ps_t = pb("ps_t", [P, 2, 2 * BANK], F32, es)
                ps_r = pb("ps_r", [P, 2 * BANK], F32, es)
                ps_c = pb("ps_c", [P, BANK], F32, es)
                fields = [(A, h) for h in range(heads)] + [(AS, h) for h in range(heads) if with_self]
                rounds = [(W, C - 1), (B, 0)] * (2 if with_self else 1)

                def by_chunk(x):
                    return x[:, :, :].rearrange("p h (t c) -> p h t c", c=C)

                with nc.Block() as block:
                    @block.sync
                    def _(sp):
                        sp.dma_start(masks[:, :, :].rearrange("p m c -> p (m c)"), masks_dram).then_inc(sm_masks_in.sem, 16)
                        sp.dma_start(row_m[:, :, :].rearrange("p m c -> p (m c)"), row_masks_dram).then_inc(sm_masks_in.sem, 16)
                        sp.wait_ge(sm_masks_in.sem, sm_masks_in.at(32))

                    @block.tensor
                    def _(pe):
                        for n in range(len(fields)):
                            if n >= 2:
                                pe.wait_ge(sm_copied_in.sem, sm_copied_in.at(n - 1))
                            for t in range(NT):
                                last = nc.tensor.transpose(ps_t[:, n % 2, t * P:(t + 1) * P], SCORE[:, t * P:(t + 1) * P, n], ident[:, :])
                            last.then_inc(sm_turned_in.sem, 1)
                        for n, (tile, at) in enumerate(rounds):
                            pe.wait_ge(sm_ends_made.sem, sm_ends_made.at(n + 1))
                            for t in range(NT):
                                last = nc.tensor.transpose(ps_r[0:heads, t * P:(t + 1) * P], by_chunk(tile)[:, :, t, at], ident[:, :])
                            last.then_inc(sm_ends_turned.sem, 1)
                            pe.wait_ge(sm_carry_made.sem, sm_carry_made.at(n + 1))
                            for t in range(NT):
                                last = nc.tensor.transpose(ps_c[:, t * heads:(t + 1) * heads], carry[:, t * P:(t + 1) * P],
                                                           ident[0:heads, 0:heads])
                            last.then_inc(sm_carry_turned.sem, 1)
                        pe.wait_ge(sm_out_made.sem, sm_out_made.at(1))
                        for n, (tile, h) in enumerate(fields):
                            if n >= 2:
                                pe.wait_ge(sm_copied_out.sem, sm_copied_out.at(n - 1))
                            for t in range(NT):
                                last = nc.tensor.transpose(ps_t[:, n % 2, t * P:(t + 1) * P], tile[:, h, t * P:(t + 1) * P], ident[:, :])
                            last.then_inc(sm_turned_out.sem, 1)

                    @block.scalar
                    def _(act):
                        for n, (tile, h) in enumerate(fields):
                            act.wait_ge(sm_turned_in.sem, sm_turned_in.at(n + 1))
                            nc.scalar.activation(tile[:, h, :], ps_t[:, n % 2, 0:NS], ACT.Copy).then_inc(sm_copied_in.sem, 1)
                        for n, tile in enumerate((A, AS) if with_self else (A,)):
                            act.wait_ge(sm_exp_asked.sem, sm_exp_asked.at(n + 1))
                            nc.scalar.activation(tile[:, :, :], tile[:, :, :], ACT.Exp).then_inc(sm_exp_made.sem, 1)
                        for n in range(len(fields)):
                            act.wait_ge(sm_turned_out.sem, sm_turned_out.at(n + 1))
                            nc.scalar.activation(SCORE[:, :, n], ps_t[:, n % 2, 0:NS], ACT.Copy).then_inc(sm_copied_out.sem, 1)

                    @block.vector
                    def _(dve):
                        v = nc.vector
                        back = slice(None, None, -1)
                        done = [0]

                        def from_left(out_t, in_t, mask, op0, op1, start):
                            for h in range(heads):
                                last = v.tensor_tensor_scan(out_t[:, h, :], masks[:, mask, :], in_t[:, h, :], start, op0, op1)
                            link(last)

                        def from_right(out_t, in_t):
                            for h in range(heads):
                                last = v.tensor_tensor_scan(out_t[:, h, back], masks[:, PEN_R, back], in_t[:, h, back], FAR, ALU.add, ALU.max)
                            link(last)

                        def carries(to_right, mask, link_mask, op0, op1, start):
                            n = done[0] = done[0] + 1
                            dve.sem_inc(sm_ends_made.sem, 1)
                            dve.wait_ge(sm_ends_turned.sem, sm_ends_turned.at(n))
                            if to_right:
                                link(v.tensor_tensor_scan(row[:, :], row_m[0:heads, mask, :], ps_r[0:heads, 0:NS], start, op0, op1))
                                v.memset(carry[:, 0:1], start)
                                link(v.tensor_tensor(carry[:, 1:NS], row[:, 0:NS - 1], row_m[0:heads, link_mask, 1:NS], op0))
                            else:
                                link(v.tensor_tensor_scan(row[:, back], row_m[0:heads, mask, back], ps_r[0:heads, 0:NS][:, back], start, op0, op1))
                                v.memset(carry[:, NS - 1:NS], start)
                                link(v.tensor_tensor(carry[:, 0:NS - 1], row[:, 1:NS], row_m[0:heads, link_mask, 0:NS - 1], op0))
                            dve.sem_inc(sm_carry_made.sem, 1)
                            dve.wait_ge(sm_carry_turned.sem, sm_carry_turned.at(n))

                        def hand_over(tile, at, op):
                            ends = by_chunk(tile)[:, :, :, at]
                            link(v.tensor_tensor(ends, ends, ps_c[:, 0:NT * heads].rearrange("p (t h) -> p h t", h=heads), op))

                        def again_from_left(mask, op0, op1, start):
                            first = by_chunk(A)[:, :, :, 0]
                            link(v.tensor_copy(edge[:, :, :], first))
                            hand_over(A, 0, op1)
                            from_left(W, A, mask, op0, op1, start)
                            link(v.tensor_copy(first, edge[:, :, :]))

                        def spread_back():
                            from_right(B, W)
                            carries(False, ROW_R, LINK_R, ALU.add, ALU.max, FAR)
                            hand_over(W, C - 1, ALU.max)
                            from_right(B, W)

                        dve.wait_ge(sm_copied_in.sem, sm_copied_in.at(len(fields)))
                        dve.wait_ge(sm_masks_in.sem, sm_masks_in.at(32))
                        if leaky:
                            link(v.scalar_tensor_tensor(A[:, :, :], A[:, :, :], SLOPE, A[:, :, :], ALU.mult, ALU.max))
                        from_left(W, A, PEN_L, ALU.add, ALU.max, FAR)
                        carries(True, ROW_L, LINK_L, ALU.add, ALU.max, FAR)
                        again_from_left(PEN_L, ALU.add, ALU.max, FAR)
                        spread_back()
                        if with_self:
                            link(v.tensor_tensor(B[:, :, :], B[:, :, :], AS[:, :, :], ALU.max))
                        v.tensor_tensor(A[:, :, :], A[:, :, :], B[:, :, :], ALU.subtract).then_inc(sm_exp_asked.sem, 1)
                        if with_self:
                            v.tensor_tensor(AS[:, :, :], AS[:, :, :], B[:, :, :], ALU.subtract).then_inc(sm_exp_asked.sem, 1)
                        dve.wait_ge(sm_exp_made.sem, sm_exp_made.at(1))
                        if with_self:
                            from_left(W, A, CONT, ALU.mult, ALU.add, 0.0)
                            carries(True, ROW_C, LINK_C, ALU.mult, ALU.add, 0.0)
                            again_from_left(CONT, ALU.mult, ALU.add, 0.0)
                            spread_back()
                            dve.wait_ge(sm_exp_made.sem, sm_exp_made.at(2))
                            link(v.scalar_tensor_tensor(B[:, :, :], B[:, :, :], TINY, AS[:, :, :], ALU.add, ALU.add))
                            link(v.reciprocal(B[:, :, :], B[:, :, :]))
                            link(v.tensor_tensor(A[:, :, :], A[:, :, :], B[:, :, :], ALU.mult))
                            link(v.tensor_tensor(AS[:, :, :], AS[:, :, :], B[:, :, :], ALU.mult))
                            link(v.tensor_tensor(AS[:, :, :], AS[:, :, :], masks[:, LAST, :].unsqueeze(1).to_broadcast([P, heads, NS]), ALU.mult))
                        dve.sem_inc(sm_out_made.sem, 1)
                sm_masks_in.over(32)
                sm_out_made.over(1)
                for c in (sm_turned_in, sm_copied_in, sm_turned_out, sm_copied_out):
                    c.over(len(fields))
                for c in (sm_exp_asked, sm_exp_made):
                    c.over(2 if with_self else 1)
                for c in (sm_ends_made, sm_ends_turned, sm_carry_made, sm_carry_turned):
                    c.over(len(rounds))

        mult_made = Counted("products_made")
        act_multiplied = Counted("products_of_scalar")
        last_added = Counted("last_heads_added")
        folded = Counted("heads_folded")
        own_copied = Counted("own_shares_copied")
        shares_kept = Counted("shares_kept")
        reduced = Counted("scores_reduced", 4)
        scored = Counted("scores_kept", 4)

        def load_turned(sp, ST, i, h):
            sp.dma_start(ST[0:BN, HALF * h:HALF * (h + 1), :].rearrange("p c s -> p (c s)"),
                         turned_dram[bass.ds(2 * i + h, 1), :, :].rearrange("o p r -> (o p) r")).then_inc(loaded[h].sem, 16)

        def stash_half(act, G, width, stash, i, h):
            for j in range(HALF * h, HALF * (h + 1)):
                act.wait_ge(gathered[j].sem, gathered[j].at(16 * i + 16))
            act.dma_start(stash[bass.ds(2 * i + h, 1), :, :].rearrange("o p r -> (o p) r"),
                          G[:, HALF * h:HALF * (h + 1), 0:width].rearrange("p c f -> p (c f)")).then_inc(stashed[h].sem, 16)

        def pair_scores(SCORE, XR, l):
            phase[0] += 1
            FA = HA * D
            GW = FA + HA
            PW = FA + 2 * HA
            es = ExitStack()
            with es:
                stage = sb("stage", [P, 2, R, HALF], I32, es)
                G = sb("gathered_rows", [P, U, GW], F32, es)
                ST = sb("onehots_turned", [P, U, P], BF16, es)
                Z = sb("z", [P, 4, 2, FA], F32, es)
                RED = sb("scores_half", [P, U, 3, HA], F32, es)
                ps_Z = pb("ps_Z", [P, 2, 2, BANK], F32, es)
                with nc.Block() as block:
                    @block.sync
                    def _(sp):
                        def stage_next(i, h):
                            sp.dma_start(stage[:, h, :, :].rearrange("p a e -> p (a e)"),
                                         slots[bass.ds(2 * i + h, 1), :, :].rearrange("o p r -> (o p) r")).then_inc(staged[h].sem, 16)

                        def turn(i, last_turn):
                            for h in range(2):
                                for j in range(HALF * h, HALF * (h + 1)):
                                    sp.wait_ge(gathered[j].sem, gathered[j].at(16 * i + 16))
                                    sp.sem_inc(sp_seen, 1)
                                sp.dma_start(stash_a[bass.ds(2 * i + h, 1), :, :].rearrange("o p r -> (o p) r"),
                                             G[:, HALF * h:HALF * (h + 1), :].rearrange("p c f -> p (c f)")).then_inc(stashed[h].sem, 16)
                                if not last_turn:
                                    stage_next(i + 1, h)
                                    sp.wait_ge(dest_made.sem, dest_made.at(8 * i + 4 * h + 4))
                                    sp.sem_inc(sp_seen, 1)
                                    load_turned(sp, ST, i + 1, h)

                        for h in range(2):
                            stage_next(0, h)
                            load_turned(sp, ST, 0, h)
                        with sp.Fori(0, TURNS - 1) as i:
                            turn(i, False)
                        turn(TURNS - 1, True)
                        for h in range(2):
                            sp.wait_ge(stashed[h].sem, stashed[h].at(16 * TURNS))

                    @block.gpsimd
                    def _(pool):
                        with pool.Fori(0, TURNS) as i:
                            for h in range(2):
                                pool.wait_ge(staged[h].sem, staged[h].at(16 * i + 16))
                                pool.sem_inc(pool_seen, 1)
                                pool.wait_ge(chunk_done.sem, chunk_done.at((i - 1) * U + HALF * (h + 1)))
                                pool.sem_inc(pool_seen, 1)
                                pool.wait_ge(stashed[h].sem, stashed[h].at(16 * i))
                                pool.sem_inc(pool_seen, 1)
                                for j in range(HALF * h, HALF * (h + 1)):
                                    pool.indirect_dma_start(G[:, j, :], None, xl_table,
                                                            bass.IndirectOffsetOnAxis(stage[:, h, SRC, j % HALF:j % HALF + 1], 0)
                                                            ).then_inc(gathered[j].sem, 16)

                    @block.tensor
                    def _(pe):
                        for c, n in ((chunk_done, 2 * U), (z_made, 2), (self_kept, 2), (reduced, 4), (scored, 4), (stashed[0], 16), (stashed[1], 16)):
                            nc.tensor.nop().then_inc(c.sem, n)

                        with pe.Fori(0, TURNS) as i:
                            for h in range(2):
                                for q in range(HALF):
                                    j = HALF * h + q
                                    if j == 0:
                                        at = blocks_of(i * U, U)
                                    if q % 2 == 0:
                                        pair = 8 * i + j // 2
                                        pe.wait_ge(z_made.sem, z_made.at(pair - 1))
                                        pe.wait_ge(self_kept.sem, self_kept.at(pair - 1))
                                    if q == 0:
                                        pe.wait_ge(loaded[h].sem, loaded[h].at(16 * i + 16))
                                    for k in range(3):
                                        last = nc.tensor.matmul(ps_Z[:, (j // 2) % 2, j % 2, 0:PW], ST[0:BN, j, :],
                                                                XR[:, k, bass.ds(at[j] * PW, PW)], start=k == 0, stop=k == 2)
                                    if q % 2:
                                        last.then_inc(dest_made.sem, 1)

                    @block.scalar
                    def _(act):
                        def keep_self(i, p):
                            i, p = i + p // 8, p % 8
                            if p % 4 == 0:
                                act.wait_ge(scored.sem, scored.at(2 * (2 * i + p // 4 - 1)))
                            act.wait_ge(dest_made.sem, dest_made.at(8 * i + p + 1))
                            nc.scalar.activation(RED[:, 2 * p:2 * p + 2, 1:3, :], ps_Z[:, p % 2, :, FA:PW].rearrange("p c (k h) -> p c k h", h=HA),
                                                 ACT.Copy).then_inc(self_kept.sem, 1)

                        def turn(i, last_turn):
                            for p in range(8):
                                if not (last_turn and p == 7):
                                    keep_self(i, p + 1)
                                act.wait_ge(z_made.sem, z_made.at(8 * i + p + 1))
                                nc.scalar.activation(Z[:, p % 4, :, :], Z[:, p % 4, :, :], ACT.Relu, scale=1.0 - SLOPE).then_inc(leaky_made.sem, 1)

                        keep_self(0, 0)
                        with act.Fori(0, TURNS - 1) as i:
                            turn(i, False)
                        turn(TURNS - 1, True)

                    @block.vector
                    def _(dve):
                        v = nc.vector

                        def add(i, p):
                            i, p = i + p // 8, p % 8
                            j = 2 * p
                            for k in (j, j + 1):
                                dve.wait_ge(gathered[k].sem, gathered[k].at(16 * i + 16))
                            dve.wait_ge(reduced.sem, reduced.at(8 * i + p - 3))
                            dve.wait_ge(self_kept.sem, self_kept.at(8 * i + p + 1))
                            v.tensor_tensor(Z[:, p % 4, :, :], G[:, j:j + 2, 0:FA], ps_Z[:, p % 2, :, 0:FA], ALU.add).then_inc(z_made.sem, 1)

                        def source_part(i, p):
                            i, h = i + p // 8, p % 8 // 4
                            half = slice(HALF * h, HALF * (h + 1))
                            dve.wait_ge(z_made.sem, z_made.at(8 * i + 4 * h + 4))
                            v.tensor_tensor(RED[:, half, 1, :], RED[:, half, 1, :], G[:, half, FA:GW], ALU.add).then_inc(chunk_done.sem, HALF)

                        def weigh(i, p):
                            i, p = i + p // 8, p % 8
                            dve.wait_ge(leaky_made.sem, leaky_made.at(8 * i + p + 1))
                            v.tensor_tensor(Z[:, p % 4, :, :], Z[:, p % 4, :, :],
                                            att_bc[:, l, :].unsqueeze(1).to_broadcast([P, 2, FA]), ALU.mult).then_inc(mult_made.sem, 1)

                        def reduce(i, p):
                            dve.wait_ge(scored.sem, scored.at(2 * (2 * i + p // 4 - 1)))
                            dve.wait_ge(mult_made.sem, mult_made.at(8 * i + p + 1))
                            v.tensor_reduce(RED[:, 2 * p:2 * p + 2, 0, :], Z[:, p % 4, :, :].rearrange("p c (h f) -> p c h f", f=D), AX, ALU.add).then_inc(reduced.sem, 1)

                        def score(i, h):
                            half = slice(HALF * h, HALF * (h + 1))
                            chunks = bass.ds(i * U + HALF * h, HALF)
                            dve.wait_ge(reduced.sem, reduced.at(8 * i + 4 * h + 4))
                            dve.wait_ge(chunk_done.sem, chunk_done.at(U * i + HALF * (h + 1)))
                            v.tensor_tensor(SCORE[:, chunks, 0:HA], RED[:, half, 0, :], RED[:, half, 1, :], ALU.add).then_inc(scored.sem, 1)
                            v.tensor_scalar(SCORE[:, chunks, HA:2 * HA], RED[:, half, 2, :], 1.0, None, ALU.mult).then_inc(scored.sem, 1)

                        def turn(i, last_turn):
                            for p in range(8):
                                if not (last_turn and p >= 6):
                                    add(i, p + 2)
                                reduce(i, p)
                                if not (last_turn and p == 7):
                                    weigh(i, p + 1)
                                if p % 4 == 1:
                                    source_part(i, p + 2)
                                if p % 4 == 3:
                                    score(i, p // 4)

                        link(v.memset(SCORE[:, NCH:NS, :], 0.0))
                        add(0, 0)
                        add(0, 1)
                        weigh(0, 0)
                        with dve.Fori(0, TURNS - 1) as i:
                            turn(i, False)
                        turn(TURNS - 1, True)
                for c in (*staged, *loaded, *gathered, *stashed):
                    c.over(16 * TURNS)
                for c, n in ((chunk_done, NCH), (dest_made, NCH // 2),
                             (z_made, NCH // 2), (self_kept, NCH // 2), (leaky_made, NCH // 2), (mult_made, NCH // 2), (reduced, NCH // 2),
                             (scored, 4 * TURNS)):
                    c.over(n)

        def relation_scores(SCORE, XQ):
            phase[0] += 1
            FR = D + HR
            es = ExitStack()
            with es:
                stage = sb("stage", [P, 2, R, HALF], I32, es)
                stage_f = stage[:, :, :, :].bitcast(F32)
                G = sb("gathered_rows", [P, U, FR], F32, es)
                ST = sb("onehots_turned", [P, U, P], BF16, es)
                T1 = sb("onehots_type", [P, 2, HALF, R], F32, es)
                PQ = sb("picked", [P, 2, HALF, R, HR], F32, es)
                RED = sb("query_scores", [P, 2, HALF, HR], F32, es)
                ps_Q = pb("ps_Q", [P, 2, BANK], F32, es)
                with nc.Block() as block:
                    @block.sync
                    def _(sp):
                        with sp.Fori(0, TURNS) as i:
                            for h in range(2):
                                stage_half(sp, stage, i, h, (stashed[h],))
                                load_turned(sp, ST, i, h)
                        for c in stashed:
                            sp.wait_ge(c.sem, c.at(16 * TURNS))

                    @block.gpsimd
                    def _(pool):
                        gather_loop(pool, stage, G, FR, rel_table, SRC_TYPE)

                    @block.tensor
                    def _(pe):
                        for c, n in ((chunk_done, 2 * U), (reduced, 4), (stashed[0], 16), (stashed[1], 16)):
                            nc.tensor.nop().then_inc(c.sem, n)
                        with pe.Fori(0, TURNS) as i:
                            for h in range(2):
                                if h == 0:
                                    at = blocks_of(i * U, U)
                                pe.wait_ge(loaded[h].sem, loaded[h].at(16 * i + 16))
                                for q in range(HALF):
                                    j = HALF * h + q
                                    for k in range(3):
                                        last = nc.tensor.matmul(ps_Q[:, h, q * R * HR:(q + 1) * R * HR], ST[0:BN, j, :],
                                                                XQ[:, k, bass.ds(at[j] * (R * HR), R * HR)], start=k == 0, stop=k == 2)
                                last.then_inc(dest_made.sem, 1)

                    @block.scalar
                    def _(act):
                        with act.Fori(0, TURNS) as i:
                            for h in range(2):
                                stash_half(act, G, FR, stash_r, i, h)

                    @block.vector
                    def _(dve):
                        v = nc.vector
                        link(v.memset(SCORE[:, NCH:NS, :], 0.0))
                        with dve.Fori(0, TURNS) as i:
                            for h in range(2):
                                dve.wait_ge(staged[h].sem, staged[h].at(16 * i + 16))
                                v.tensor_tensor(T1[:, h, :, :], pos[:, 0:R].unsqueeze(1).to_broadcast([P, HALF, R]),
                                                stage_f[:, h, TYPE, :].unsqueeze(2).to_broadcast([P, HALF, R]), ALU.is_equal).then_inc(leaky_made.sem, 1)
                                dve.wait_ge(leaky_made.sem, leaky_made.at(2 * i + h + 1))
                                dve.wait_ge(dest_made.sem, dest_made.at(2 * i + h + 1))
                                v.tensor_tensor(PQ[:, h, :, :, :], ps_Q[:, h, 0:HALF * R * HR].rearrange("p (c r h) -> p c r h", r=R, h=HR),
                                                T1[:, h, :, :].unsqueeze(3).to_broadcast([P, HALF, R, HR]), ALU.mult).then_inc(mult_made.sem, 1)
                                dve.wait_ge(mult_made.sem, mult_made.at(2 * i + h + 1))
                                v.tensor_reduce(RED[:, h, :, :], PQ[:, h, :, :, :].rearrange("p c r h -> p c h r"), AX, ALU.add).then_inc(reduced.sem, 1)
                                for j in range(HALF * h, HALF * (h + 1)):
                                    dve.wait_ge(gathered[j].sem, gathered[j].at(16 * i + 16))
                                dve.wait_ge(reduced.sem, reduced.at(2 * i + h + 1))
                                v.tensor_tensor(SCORE[:, bass.ds(i * U + HALF * h, HALF), :], RED[:, h, :, :],
                                                G[:, HALF * h:HALF * (h + 1), D:FR], ALU.add).then_inc(chunk_done.sem, HALF)
                for c in (*staged, *loaded, *gathered, *stashed):
                    c.over(16 * TURNS)
                for c, n in ((chunk_done, NCH), (dest_made, 2 * TURNS),
                             (leaky_made, 2 * TURNS), (mult_made, 2 * TURNS), (reduced, 2 * TURNS)):
                    c.over(n)

        def shared_sums(SUM, SCORE, heads, width, stash, with_self):
            phase[0] += 1
            out_w = D + heads
            HT = 4
            LT = TURNS * 2 // HT
            arrived = (*loaded, *staged)
            es = ExitStack()
            with es:
                G = sb("kept_rows", [P, HT * HALF, width], F32, es)
                S = sb("onehots", [P, HT * HALF, BN], F32, es)
                M = sb("messages", [P, HT * HALF, out_w], F32, es)
                PR = sb("products", [P, 2, HALF, heads, D], F32, es) if with_self else None
                SH = sb("shares_half", [P, 2, HALF, 2 * heads], F32, es) if with_self else None
                DH = heads - 2
                zero = sb("zero_bank", [P, BANK], F32, es)
                ps_sum = pb("ps_sum", [P, 7 * BANK], F32, es)
                ready, finished = (once(x) for x in ("set_up", "loop_over"))
                with nc.Block() as block:
                    @block.sync
                    def _(sp):
                        def load_rows(i, h):
                            sp.dma_start(G[:, HALF * h:HALF * (h + 1), :].rearrange("p c f -> p (c f)"),
                                         stash[bass.ds(HT * i + h, 1), :, :].rearrange("o p r -> (o p) r")).then_inc(arrived[h].sem, 16)

                        def turn(i):
                            for h in range(HT):
                                if with_self:
                                    sp.wait_ge(mult_made.sem, mult_made.at(HT * i + h + 1))
                                    sp.sem_inc(sp_seen, 1)
                                    sp.wait_ge(act_multiplied.sem, act_multiplied.at(2 * HALF * (HT * i + h + 1)))
                                else:
                                    sp.wait_ge(msg_made.sem, msg_made.at(HT * i + h + 1))
                                sp.sem_inc(sp_seen, 1)
                                load_rows(i + 1, h)

                        for h in range(HT):
                            load_rows(0, h)
                        with sp.Fori(0, LT - 1) as i:
                            turn(i)

                    @block.vector
                    def _(dve):
                        v = nc.vector
                        v.memset(zero[:, :], 0.0).then_inc(ready, 1)
                        with dve.Fori(0, LT) as i:
                            for h in range(HT):
                                n = HT * i + h + 1
                                half = slice(HALF * h, HALF * (h + 1))
                                share = SCORE[:, bass.ds(HALF * (HT * i + h), HALF), :]
                                dve.wait_ge(chunk_done.sem, chunk_done.at(HALF * (HT * (i - 1) + h + 1)))
                                make_onehots(S, i, h, HT).then_inc(onehot_made.sem, 1)
                                dve.wait_ge(arrived[h].sem, arrived[h].at(16 * i + 16))
                                if with_self:
                                    dve.wait_ge(msg_made.sem, msg_made.at(n - 2))
                                    v.tensor_tensor(PR[:, h % 2, :, 0:DH, :], G[:, half, 0:DH * D].rearrange("p c (h f) -> p c h f", f=D),
                                                    share[:, :, 0:DH].unsqueeze(3).to_broadcast([P, HALF, DH, D]), ALU.mult).then_inc(mult_made.sem, 1)
                                    v.tensor_scalar(M[:, half, D:out_w], share[:, :, heads:2 * heads], 1.0, None, ALU.mult).then_inc(own_copied.sem, 1)
                                    dve.wait_ge(mult_made.sem, mult_made.at(n))
                                    dve.wait_ge(last_added.sem, last_added.at(n))
                                    v.tensor_tensor(PR[:, h % 2, :, 0:2, :], PR[:, h % 2, :, 0:2, :], PR[:, h % 2, :, 2:4, :], ALU.add).then_inc(folded.sem, 1)
                                    dve.wait_ge(folded.sem, folded.at(n))
                                    v.tensor_tensor(M[:, half, 0:D], PR[:, h % 2, :, 0, :], PR[:, h % 2, :, 1, :], ALU.add).then_inc(msg_made.sem, 1)
                                else:
                                    v.tensor_scalar(M[:, half, D:out_w], share, 1.0, None, ALU.mult).then_inc(own_copied.sem, 1)
                                    v.tensor_tensor(M[:, half, 0:D].rearrange("p c (h f) -> p c h f", h=heads),
                                                    G[:, half, 0:D].rearrange("p c (h f) -> p c h f", h=heads),
                                                    share.unsqueeze(3).to_broadcast([P, HALF, heads, D // heads]), ALU.mult).then_inc(msg_made.sem, 1)
                        dve.wait_ge(finished, 1)
                        link(v.tensor_copy(SUM[:, :, :], sums(ps_sum, out_w)))

                    if with_self:
                        @block.gpsimd
                        def _(pool):
                            with pool.Fori(0, LT) as i:
                                for h in range(HT):
                                    pool.wait_ge(act_multiplied.sem, act_multiplied.at(2 * HALF * (HT * i + h + 1)))
                                    nc.gpsimd.tensor_tensor(PR[:, h % 2, :, 3, :], PR[:, h % 2, :, 3, :], PR[:, h % 2, :, 4, :], ALU.add).then_inc(last_added.sem, 1)

                        @block.scalar
                        def _(act):
                            with act.Fori(0, LT) as i:
                                for h in range(HT):
                                    act.wait_ge(msg_made.sem, msg_made.at(HT * i + h - 1))
                                    nc.scalar.activation(SH[:, h % 2, :, :], SCORE[:, bass.ds(HALF * (HT * i + h), HALF), :], ACT.Copy).then_inc(shares_kept.sem, 1)
                                    act.wait_ge(shares_kept.sem, shares_kept.at(HT * i + h + 1))
                                    act.wait_ge(arrived[h].sem, arrived[h].at(16 * i + 16))
                                    for q in range(HALF):
                                        for k in range(DH, heads):
                                            nc.scalar.activation(PR[:, h % 2, q, k, :], G[:, HALF * h + q, k * D:(k + 1) * D], ACT.Copy,
                                                                 scale=SH[:, h % 2, q, k:k + 1]).then_inc(act_multiplied.sem, 1)

                    @block.tensor
                    def _(pe):
                        for c in (msg_made, chunk_done):
                            nc.tensor.nop().then_inc(c.sem, c.credit)
                        pe.wait_ge(ready, 1)
                        zero_sums(ps_sum, zero, 7)
                        with pe.Fori(0, LT) as i:
                            for h in range(HT):
                                for q in range(HALF):
                                    j = HALF * h + q
                                    if q == 0 and h % 2 == 0:
                                        at = blocks_of(HALF * (HT * i + h), U)
                                    if q == 0:
                                        pe.wait_ge(onehot_made.sem, onehot_made.at(HT * i + h + 1))
                                        pe.wait_ge(msg_made.sem, msg_made.at(HT * i + h + 1))
                                        pe.wait_ge(own_copied.sem, own_copied.at(HT * i + h + 1))
                                    sum_chunk(ps_sum, S, j, M[:, j, :], out_w, at[j % U]).then_inc(chunk_done.sem, 1)
                        nc.tensor.matmul(ps_sum[:, 6 * BANK + 3 * P:7 * BANK], zero[:, 0:P], zero[:, 0:P], start=False, stop=True,
                                         skip_group_check=True).then_inc(finished, 1)
                for c in arrived:
                    c.over(16 * LT)
                for c, n in ((onehot_made, 2 * TURNS), (msg_made, 2 * TURNS), (own_copied, 2 * TURNS), (chunk_done, NCH)):
                    c.over(n)
                if with_self:
                    for c in (mult_made, last_added, folded, shares_kept):
                        c.over(2 * TURNS)
                    act_multiplied.over(2 * NCH)

        segments_phase()

        norm_phase()
        for l in range(2):
            FA = HA * D
            GW = FA + HA
            PW = FA + 2 * HA
            ls = ExitStack()
            with ls:
                phase[0] += 1
                SCORE = sb("score", [P, NS, 2 * HA], F32, ls)
                xs = ExitStack()
                with xs:
                    XR = sb("xr_parts", [BN, 3, NB * PW], BF16, xs)
                    BG = 5
                    xt = ExitStack()
                    with xt:
                        XLg = sb("xl", [BN, 2, BG, GW], F32, xt)
                        XRg = sb("xr", [BN, 2, BG, PW], F32, xt)
                        TMP = sb("own_z", [BN, BG, FA], F32, xt)
                        WA = sb("weights_att", [D, 2, GW], F32, xt)
                        BA = sb("biases_att", [BN, 2, GW], F32, xt)
                        xl_stored, own_made, high_made, high_off, mid_made, mid_off, low_made = (once(x) for x in (
                            "xl_stored", "own_scores_made", "high_parts_made", "high_parts_off", "mid_parts_made", "mid_parts_off", "low_parts_made"))

                        def parts(k, g):
                            return XR[:, k, g * BG * PW:(g + 1) * BG * PW].rearrange("p (b f) -> p b f", f=PW)

                        def before(dve):
                            v = nc.vector
                            for k in range(2):
                                for wide, given, n in ((WA, w2, D), (BA, bc_big, BN)):
                                    link(v.tensor_copy(wide[:, k, 0:FA], given[:, 2 * l + k, :]))
                                    link(v.tensor_tensor(TMP[0:n, 0, :], wide[:, k, 0:FA], att_bc[0:n, l, :], ALU.mult))
                                    link(v.tensor_reduce(wide[:, k, FA:GW], TMP[0:n, 0, :].rearrange("p (h f) -> p h f", f=D), AX, ALU.add))
                                    link(v.tensor_scalar(wide[:, k, FA:GW], wide[:, k, FA:GW], SLOPE, None, ALU.mult))

                        def take(dve, b, ps):
                            g = b // BG
                            if b % BG == 0 and g >= 2:
                                dve.wait_ge(xl_stored, 16 * (g - 1))
                                dve.wait_ge(low_made, g - 1)
                            nc.vector.tensor_tensor(XRg[:, g % 2, b % BG, 0:GW], ps[:, 1, 0:GW], BA[:, 1, :], ALU.add).then_inc(dve_step, 1)
                            steps[0] += 1
                            return nc.vector.tensor_tensor(XLg[:, g % 2, b % BG, :], ps[:, 0, 0:GW], BA[:, 0, :], ALU.add)

                        def take_off(dve, made, g, k, off):
                            dve.wait_ge(made, g + 1)
                            nc.vector.tensor_tensor(XRg[:, g % 2, :, :], XRg[:, g % 2, :, :], parts(k, g), ALU.subtract).then_inc(off, 1)

                        def between(dve, b):
                            if b % BG != BG - 1:
                                return
                            v = nc.vector
                            g = b // BG
                            xl, xr = XLg[:, g % 2, :, :], XRg[:, g % 2, :, :]
                            if g >= 1:
                                take_off(dve, high_made, g - 1, 0, high_off)
                            dve.wait_ge(dve_step, steps[0])
                            dve.wait_ge(taken_b.sem, taken_b.at(b + 1))
                            link(v.tensor_tensor(TMP[:, :, :], xl[:, :, 0:FA], xr[:, :, 0:FA], ALU.add))
                            link(v.scalar_tensor_tensor(TMP[:, :, :], TMP[:, :, :], SLOPE, TMP[:, :, :], ALU.mult, ALU.max))
                            link(v.tensor_tensor(TMP[:, :, :], TMP[:, :, :], att_bc[0:BN, l, :].unsqueeze(1).to_broadcast([BN, BG, FA]), ALU.mult))
                            link(v.tensor_reduce(xr[:, :, GW:PW], TMP[:, :, :].rearrange("p b (h f) -> p b h f", f=D), AX, ALU.add))
                            dve.sem_inc(own_made, 1)
                            if g >= 1:
                                take_off(dve, mid_made, g - 1, 1, mid_off)

                        def after(dve):
                            take_off(dve, high_made, NB // BG - 1, 0, high_off)
                            take_off(dve, mid_made, NB // BG - 1, 1, mid_off)

                        def split(act, b):
                            def part(k, g, ready, made):
                                act.wait_ge(ready, g + 1)
                                nc.scalar.activation(parts(k, g), XRg[:, g % 2, :, :], ACT.Copy).then_inc(made, 1)

                            if (b - BG) % BG == 1 and b > BG:
                                g = b // BG - 1
                                if g >= 1:
                                    part(1, g - 1, high_off, mid_made)
                                part(0, g, own_made, high_made)
                                if g >= 1:
                                    part(2, g - 1, mid_off, low_made)
                            if b == NB - 1:
                                g = NB // BG - 1
                                part(1, g - 1, high_off, mid_made)
                                part(0, g, own_made, high_made)
                                part(2, g - 1, mid_off, low_made)
                                part(1, g, high_off, mid_made)
                                part(2, g, mid_off, low_made)

                        def store(sp):
                            for g in range(NB // BG):
                                if g >= 1:
                                    sp.wait_ge(xl_stored, 16 * g)
                                sp.wait_ge(taken_b.sem, taken_b.at((g + 1) * BG))
                                sp.dma_start(xl_table.rearrange("(b p) f -> p b f", p=BN)[:, g * BG:(g + 1) * BG, :], XLg[:, g % 2, :, :]).then_inc(xl_stored, 16)
                            sp.wait_ge(xl_stored, 16 * (NB // BG))

                        dense(H[:, :, :], D, [WA[:, 0, :], WA[:, 1, :]], take, before, after, store, between, split)
                    pair_scores(SCORE, XR, l)
                softmax_phase(SCORE, HA, False, True)
                SUM = sb("sums", [BN, NB, D + HA], F32, ls)
                shared_sums(SUM, SCORE, HA, GW, stash_a, True)
                phase[0] += 1
                xt = ExitStack()
                with xt:
                    XL = sb("xl_again", [BN, NB, GW], F32, xt)
                    lone = sb("lone", [BN, NB], F32, xt)
                    own = sb("own", [BN, NB, D], F32, xt)
                    xl_back = once("xl_back")
                    with nc.Block() as block:
                        @block.sync
                        def _(sp):
                            sp.dma_start(XL[:, :, :], xl_table.rearrange("(b p) f -> p b f", p=BN)).then_inc(xl_back, 16)

                        @block.vector
                        def _(dve):
                            v = nc.vector
                            link(v.tensor_scalar(lone[:, :], deg_in[:, :], 0.0, None, ALU.is_equal))
                            link(v.tensor_tensor(SUM[:, :, D:], SUM[:, :, D:], lone[:, :].unsqueeze(2).to_broadcast([BN, NB, HA]), ALU.add))
                            dve.wait_ge(xl_back, 16)
                            link(v.tensor_tensor(XL[:, :, 0:FA].rearrange("p b (h f) -> p b h f", f=D), XL[:, :, 0:FA].rearrange("p b (h f) -> p b h f", f=D),
                                                 SUM[:, :, D:].unsqueeze(3).to_broadcast([BN, NB, HA, D]), ALU.mult))
                            link(v.tensor_reduce(own[:, :, :], XL[:, :, 0:FA].rearrange("p b (h f) -> p b f h", f=D), AX, ALU.add))
                            link(v.tensor_tensor(own[:, :, :], own[:, :, :], SUM[:, :, 0:D], ALU.add))
                            link(v.scalar_tensor_tensor(own[:, :, :], own[:, :, :], 1.0 / HA, bcn(bc_n[:, 4 + l, :]), ALU.mult, ALU.add))
                            link(v.tensor_scalar(H[:, :, :], own[:, :, :], 0.0, None, ALU.max))

        AGG_s = ExitStack()
        with AGG_s:
            def take(dve, b, ps):
                v = nc.vector
                return v.tensor_tensor(H[:, b, :], ps[:, 0, 0:D], bc_n[:, 6, :], ALU.add)

            def after(dve):
                link(nc.vector.tensor_tensor(X[:, :, :], X[:, :, :], H[:, :, :], ALU.add))

            dense(H[:, :, :], D, [wfc[:, :]], take, None, after)

        norm_phase()
        for l in range(2):
            FR = D + HR
            ls = ExitStack()
            with ls:
                phase[0] += 1
                SCORE = sb("score", [P, NS, HR], F32, ls)
                xs = ExitStack()
                with xs:
                    XQ = sb("query_parts", [BN, 3, NB * R * HR], BF16, xs)
                    xt = ExitStack()
                    with xt:
                        T3 = sb("rel_rows", [BN, NB, R, FR], F32, xt)
                        Q3 = sb("queries", [BN, NB * R * HR], F32, xt)
                        Q3v = Q3[:, :].rearrange("p (b f) -> p b f", b=NB)
                        rel_made = once("rel_made")
                        rel_stored = once("rel_stored")

                        def take(dve, b, ps, T3=T3, Q3v=Q3v):
                            v = nc.vector
                            v.tensor_copy(T3[:, b, :, 0:D], ps[:, 0, :].rearrange("p (r f) -> p r f", f=D))
                            v.tensor_copy(T3[:, b, :, D:FR], ps[:, 1, 0:R * HR].rearrange("p (r h) -> p r h", h=HR))
                            return v.tensor_copy(Q3v[:, b, :], ps[:, 1, R * HR:2 * R * HR])

                        def after(dve, rel_made=rel_made, XQ=XQ, Q3=Q3):
                            dve.sem_inc(rel_made, 1)
                            v = nc.vector
                            for k in range(3):
                                link(v.tensor_copy(XQ[:, k, :], Q3[:, :]))
                                if k < 2:
                                    link(v.tensor_tensor(Q3[:, :], Q3[:, :], XQ[:, k, :], ALU.subtract))

                        def store(sp, T3=T3, rel_made=rel_made, rel_stored=rel_stored):
                            sp.wait_ge(rel_made, 1)
                            sp.dma_start(rel_table.rearrange("(b p r) w -> p b (r w)", p=BN, r=R),
                                         T3[:, :, :, :].rearrange("p b r w -> p b (r w)")).then_inc(rel_stored, 16)
                            sp.wait_ge(rel_stored, 16)

                        dense(H[:, :, :], D, [w3[:, l, :, :].rearrange("p r f -> p (r f)"), wkq[:, l, :, :, :].rearrange("p k r h -> p (k r h)")],
                              take, None, after, store)
                    relation_scores(SCORE, XQ)
                softmax_phase(SCORE, HR, True, False)
                SUM = sb("sums", [BN, NB, D + HR], F32, ls)
                shared_sums(SUM, SCORE, HR, FR, stash_r, False)
                with nc.Block() as block:
                    @block.vector
                    def _(dve):
                        v = nc.vector
                        link(v.tensor_scalar(SUM[:, :, D:], SUM[:, :, D:], TINY, None, ALU.add))
                        link(v.reciprocal(SUM[:, :, D:], SUM[:, :, D:]))
                        link(v.tensor_tensor(H[:, :, :].rearrange("p b (h f) -> p b h f", h=HR), SUM[:, :, 0:D].rearrange("p b (h f) -> p b h f", h=HR),
                                             SUM[:, :, D:].unsqueeze(3).to_broadcast([BN, NB, HR, DR]), ALU.mult))
                        link(v.tensor_tensor(H[:, :, :], H[:, :, :], bcn(bc_n[:, 7 + l, :]), ALU.add))
                        if l == 0:
                            link(v.tensor_scalar(H[:, :, :], H[:, :, :], 0.0, None, ALU.max))
                        else:
                            link(v.tensor_tensor(X[:, :, :], X[:, :, :], H[:, :, :], ALU.add))

        s_out = sem("out_stored")
        with nc.Block() as block:
            @block.sync
            def _(sp):
                sp.dma_start(out.rearrange("(b p) f -> p b f", p=BN), X[:, :, :]).then_inc(s_out, 16)
                sp.wait_ge(s_out, 16)


_INS = ['x', 'src', 'dst', 'edge_attr_64', 'edge_attr_64_n2', 'edge_type_8', 'edge_weight', 'L0_gnn_W_self', 'L0_gnn_W_neigh', 'L0_gnn_b_neigh', 'L1_gnn_a_mu0', 'L1_gnn_a_ls0', 'L1_gnn_a_mu1', 'L1_gnn_a_ls1', 'L1_gnn_W0', 'L1_gnn_b0', 'L1_gnn_W1', 'L1_gnn_b1', 'L2_gnn_W1l', 'L2_gnn_b1l', 'L2_gnn_W1r', 'L2_gnn_b1r', 'L2_gnn_att1', 'L2_gnn_bias1', 'L2_gnn_W2l', 'L2_gnn_b2l', 'L2_gnn_W2r', 'L2_gnn_b2r', 'L2_gnn_att2', 'L2_gnn_bias2', 'L2_gnn_Wfc', 'L2_gnn_bfc', 'L3_gnn_W1', 'L3_gnn_Q1', 'L3_gnn_K1', 'L3_gnn_b1', 'L3_gnn_W2', 'L3_gnn_Q2', 'L3_gnn_K2', 'L3_gnn_b2']
_TURNED = ('L0_gnn_W_self', 'L0_gnn_W_neigh', 'L3_gnn_W1', 'L3_gnn_W2')


def kernel(**inputs):
    import numpy as _np
    import concourse.bacc as _bacc
    from concourse import mybir as _mybir
    from concourse.bass_utils import run_bass_kernel_spmd as _run

    nc = _bacc.Bacc("TRN2", target_bir_lowering=False, num_devices=1)
    arrays, io = {}, {}

    def give(name, a):
        a = _np.ascontiguousarray(a)
        arrays[f"in_{name}_dram"] = a
        io[name] = nc.dram_tensor(f"in_{name}_dram", a.shape, _mybir.dt.from_np(a.dtype), kind="ExternalInput").ap()

    for name in _INS:
        a = _np.asarray(inputs[name])
        if name.startswith("edge_attr"):
            a = _np.concatenate([a, _np.zeros((C, D), a.dtype)])
        give(name, a)
        if name in _TURNED:
            give(name + "_T", _np.swapaxes(_np.asarray(inputs[name]), -1, -2))
    out = nc.dram_tensor("out_0_dram", (N, D), F32, kind="ExternalOutput").ap()
    build(nc, io, out)
    r = _run(nc, [arrays], core_ids=[0])
    return r.results[0]["out_0_dram"]
```
